# Optimizing a Trainium2 kernel written in Bass

```python
import numpy as np
import jax
import jax.numpy as jnp

def _softmax(x, axis=-1):
    return jax.nn.softmax(x, axis=axis)

def _gelu(x):
    return jax.nn.gelu(x, approximate=True)

def _silu(x):
    return jax.nn.silu(x)

def _sigmoid(x):
    return jax.nn.sigmoid(x)

def _layernorm(x, axis=-1, eps=1e-05):
    m = jnp.mean(x, axis=axis, keepdims=True)
    v = jnp.var(x, axis=axis, keepdims=True)
    return (x - m) / jnp.sqrt(v + eps)

def _scatter_add(tgt, idx, src, axis=0):
    return tgt.at[idx].add(src)

def _segment_sum(src, seg, n):
    return jax.ops.segment_sum(src, seg, n)
kernel_name = 'mk_xattn_ffn_d2_seqx_r8_a1cca8'

def setup_inputs(seed: int=0):
    np.random.seed(seed)
    _w = jnp.asarray

    def _rec_inputs():
        import jax
        import jax.numpy as jnp
        _rk = jax.random.key(seed)
        x = -0.0002928 + 1 * jax.random.normal(jax.random.fold_in(_rk, 1), (16, 128, 128), jnp.float32)
        _lenS = 128 - jax.random.randint(jax.random.fold_in(_rk, 7), (16,), 0, max(1, 128 // 4) + 1, jnp.int32)
        _lenS2 = 128 - jax.random.randint(jax.random.fold_in(_rk, 8), (16,), 0, max(1, 128 // 4) + 1, jnp.int32)
        _ctx_1024P = jax.random.normal(jax.random.fold_in(_rk, 11), (16, 16, 128), jnp.float32)
        _ctx_1024c = jax.random.dirichlet(jax.random.fold_in(_rk, 511), 0.3 * jnp.ones((16,), jnp.float32), (16, 128))
        _ctx_1024t = jnp.einsum('bsk,bkd->bsd', _ctx_1024c, _ctx_1024P)
        _ctx_1024t = _ctx_1024t * jax.lax.rsqrt(jnp.mean(jnp.square(_ctx_1024t)) + 1e-12) * 0.953939
        ctx_1024 = -1.39393e-06 + 0.999914 * (_ctx_1024t + 0.3 * jax.random.normal(jax.random.fold_in(_rk, 611), (16, 128, 128), jnp.float32))
        _validS = jnp.arange(128)[None, :] < _lenS[:, None]
        _validS2 = jnp.arange(128)[None, :] < _lenS2[:, None]
        _causal = jnp.tril(jnp.ones((128, 128), dtype=bool))
        mask_BxS2_if1 = jnp.where(jnp.ones((16, 128), dtype=bool), 1, 0).astype(jnp.int32)
        return (x, ctx_1024, mask_BxS2_if1)
    x, ctx_1024, mask_BxS2_if1 = _rec_inputs()

    def _L0_xattn_setup():
        import jax, jax.numpy as jnp
        import numpy as np
        D_MODEL = 128
        NUM_HEADS = 16
        D_K = D_MODEL // NUM_HEADS

        def _split_heads(x):
            B, S, _ = x.shape
            return x.reshape(B, S, NUM_HEADS, D_K).transpose(0, 2, 1, 3)
        key = jax.random.key(seed)
        ks = jax.random.split(key, 11)
        B, S = (2, 256)
        scale = 1.0 / np.sqrt(D_MODEL)
        inp = {'Q': jax.random.normal(ks[0], (B, S, D_MODEL), dtype=jnp.float32), 'K': jax.random.normal(ks[1], (B, S, D_MODEL), dtype=jnp.float32), 'V': jax.random.normal(ks[2], (B, S, D_MODEL), dtype=jnp.float32), 'Wq': jax.random.normal(ks[3], (D_MODEL, D_MODEL), dtype=jnp.float32) * scale, 'bq': jax.random.normal(ks[4], (D_MODEL,), dtype=jnp.float32) * scale, 'Wk': jax.random.normal(ks[5], (D_MODEL, D_MODEL), dtype=jnp.float32) * scale, 'bk': jax.random.normal(ks[6], (D_MODEL,), dtype=jnp.float32) * scale, 'Wv': jax.random.normal(ks[7], (D_MODEL, D_MODEL), dtype=jnp.float32) * scale, 'bv': jax.random.normal(ks[8], (D_MODEL,), dtype=jnp.float32) * scale, 'Wo': jax.random.normal(ks[9], (D_MODEL, D_MODEL), dtype=jnp.float32) * scale, 'bo': jax.random.normal(ks[10], (D_MODEL,), dtype=jnp.float32) * scale}
        return inp
    _L0_xattn_all = _L0_xattn_setup()
    _L0_xattn_in = {k: v for k, v in _L0_xattn_all.items() if k in ('Wq', 'bq', 'Wk', 'bk', 'Wv', 'bv', 'Wo', 'bo')}
    del _L0_xattn_all

    def _L0_ffn_setup():
        import jax, jax.numpy as jnp
        import numpy as np
        D_MODEL, HIDDEN, N_EXPERTS, TOP_K = (128, 256, 8, 2)
        RMS_EPS = 1e-06
        key = jax.random.key(seed)
        ks = jax.random.split(key, 6)
        B, S = (4, 256)
        return {'x': jax.random.normal(ks[0], (B, S, D_MODEL), jnp.float32), 'norm_weight': jnp.ones((D_MODEL,), jnp.float32), 'gate_w': jax.random.normal(ks[1], (N_EXPERTS, D_MODEL), jnp.float32) * 0.02, 'w1': jax.random.normal(ks[2], (N_EXPERTS, HIDDEN, D_MODEL), jnp.float32) * 0.02, 'b1': jnp.zeros((N_EXPERTS, HIDDEN), jnp.float32), 'w2': jax.random.normal(ks[3], (N_EXPERTS, D_MODEL, HIDDEN), jnp.float32) * 0.02, 'b2': jnp.zeros((N_EXPERTS, D_MODEL), jnp.float32)}
    _L0_ffn_all = _L0_ffn_setup()
    _L0_ffn_in = {k: v for k, v in _L0_ffn_all.items() if k in ('norm_weight', 'gate_w', 'w1', 'b1', 'w2', 'b2')}
    del _L0_ffn_all

    def _L1_xattn_setup():
        import jax, jax.numpy as jnp
        import numpy as np
        D_MODEL = 128
        NUM_HEADS = 16
        D_KEY = D_MODEL // NUM_HEADS
        MASK_FUTURE = True
        NEG_INF = -jnp.inf
        key = jax.random.key(seed)
        ks = jax.random.split(key, 7)
        B, N = (4, 256)
        return {'query': jax.random.normal(ks[0], (B, N, D_MODEL), dtype=jnp.float32), 'key': jax.random.normal(ks[1], (B, N, D_MODEL), dtype=jnp.float32), 'value': jax.random.normal(ks[2], (B, N, D_MODEL), dtype=jnp.float32), 'mask': jnp.ones((B, N), dtype=jnp.int32), 'Wq': jax.random.normal(ks[3], (D_MODEL, D_MODEL), dtype=jnp.float32) * 0.02, 'Wk': jax.random.normal(ks[4], (D_MODEL, D_MODEL), dtype=jnp.float32) * 0.02, 'Wv': jax.random.normal(ks[5], (D_MODEL, D_MODEL), dtype=jnp.float32) * 0.02, 'Wo': jax.random.normal(ks[6], (D_MODEL, D_MODEL), dtype=jnp.float32) * 0.02}
    _L1_xattn_all = _L1_xattn_setup()
    _L1_xattn_in = {k: v for k, v in _L1_xattn_all.items() if k in ('Wq', 'Wk', 'Wv', 'Wo')}
    del _L1_xattn_all

    def _L1_ffn_setup():
        import jax, jax.numpy as jnp
        import numpy as np
        HIDDEN = 128
        INNER = 512

        def _weight_quant(w):
            scale = 1.0 / jnp.clip(jnp.mean(jnp.abs(w)), 1e-05)
            wq = jnp.clip(jnp.round(w * scale), -1.0, 1.0) / scale
            return w + jax.lax.stop_gradient(wq - w)

        def _act_quant(x):
            scale = 127.0 / jnp.clip(jnp.max(jnp.abs(x), axis=-1, keepdims=True), 1e-05)
            xq = jnp.clip(jnp.round(x * scale), -128.0, 127.0) / scale
            return x + jax.lax.stop_gradient(xq - x)

        def _bitlinear(x, w):
            return jnp.einsum('bsi,oi->bso', _act_quant(x), _weight_quant(w))
        key = jax.random.key(seed)
        k0, k1, k2, k3 = jax.random.split(key, 4)
        x = jax.random.normal(k0, (4, 256, HIDDEN), dtype=jnp.float32)
        w_gate = jax.random.normal(k1, (INNER, HIDDEN), dtype=jnp.float32) / np.sqrt(HIDDEN)
        w_up = jax.random.normal(k2, (INNER, HIDDEN), dtype=jnp.float32) / np.sqrt(HIDDEN)
        w_down = jax.random.normal(k3, (HIDDEN, INNER), dtype=jnp.float32) / np.sqrt(INNER)
        return {'x': x, 'w_gate': w_gate, 'w_up': w_up, 'w_down': w_down}
    _L1_ffn_all = _L1_ffn_setup()
    _L1_ffn_in = {k: v for k, v in _L1_ffn_all.items() if k in ('w_gate', 'w_up', 'w_down')}
    del _L1_ffn_all
    return {'x': x, 'ctx_1024': ctx_1024, 'mask_BxS2_if1': mask_BxS2_if1, 'L0_xattn_Wq': _L0_xattn_in['Wq'], 'L0_xattn_bq': _L0_xattn_in['bq'], 'L0_xattn_Wk': _L0_xattn_in['Wk'], 'L0_xattn_bk': _L0_xattn_in['bk'], 'L0_xattn_Wv': _L0_xattn_in['Wv'], 'L0_xattn_bv': _L0_xattn_in['bv'], 'L0_xattn_Wo': _L0_xattn_in['Wo'], 'L0_xattn_bo': _L0_xattn_in['bo'], 'L0_ffn_norm_weight': _L0_ffn_in['norm_weight'], 'L0_ffn_gate_w': _L0_ffn_in['gate_w'], 'L0_ffn_w1': _L0_ffn_in['w1'], 'L0_ffn_b1': _L0_ffn_in['b1'], 'L0_ffn_w2': _L0_ffn_in['w2'], 'L0_ffn_b2': _L0_ffn_in['b2'], 'L1_xattn_Wq': _L1_xattn_in['Wq'], 'L1_xattn_Wk': _L1_xattn_in['Wk'], 'L1_xattn_Wv': _L1_xattn_in['Wv'], 'L1_xattn_Wo': _L1_xattn_in['Wo'], 'L1_ffn_w_gate': _L1_ffn_in['w_gate'], 'L1_ffn_w_up': _L1_ffn_in['w_up'], 'L1_ffn_w_down': _L1_ffn_in['w_down']}

def reference(x, ctx_1024, mask_BxS2_if1, L0_xattn_Wq, L0_xattn_bq, L0_xattn_Wk, L0_xattn_bk, L0_xattn_Wv, L0_xattn_bv, L0_xattn_Wo, L0_xattn_bo, L0_ffn_norm_weight, L0_ffn_gate_w, L0_ffn_w1, L0_ffn_b1, L0_ffn_w2, L0_ffn_b2, L1_xattn_Wq, L1_xattn_Wk, L1_xattn_Wv, L1_xattn_Wo, L1_ffn_w_gate, L1_ffn_w_up, L1_ffn_w_down):
    import jax
    import jax.numpy as jnp

    def _L0_xattn_ref(Q, K, V, Wq, bq, Wk, bk, Wv, bv, Wo, bo):
        import jax, jax.numpy as jnp
        import numpy as np
        D_MODEL = 128
        NUM_HEADS = 16
        D_K = D_MODEL // NUM_HEADS

        def _split_heads(x):
            B, S, _ = x.shape
            return x.reshape(B, S, NUM_HEADS, D_K).transpose(0, 2, 1, 3)
        q = _split_heads(Q @ Wq.T + bq)
        k = _split_heads(K @ Wk.T + bk)
        v = _split_heads(V @ Wv.T + bv)
        scores = jnp.einsum('bhqd,bhkd->bhqk', q, k) / jnp.sqrt(jnp.float32(D_K))
        probs = jax.nn.softmax(scores, axis=-1)
        out = jnp.einsum('bhqk,bhkd->bhqd', probs, v)
        B, H, S, dk = out.shape
        out = out.transpose(0, 2, 1, 3).reshape(B, S, D_MODEL)
        return out @ Wo.T + bo

    def _L0_ffn_ref(x, norm_weight, gate_w, w1, b1, w2, b2):
        import jax, jax.numpy as jnp
        import numpy as np
        D_MODEL, HIDDEN, N_EXPERTS, TOP_K = (128, 256, 8, 2)
        RMS_EPS = 1e-06
        B, S, D = x.shape
        E = gate_w.shape[0]
        t = x * jax.lax.rsqrt(jnp.mean(x * x, axis=-1, keepdims=True) + RMS_EPS) * norm_weight
        tokens = t.reshape(-1, D)
        T = tokens.shape[0]
        gate_logits = tokens @ gate_w.T
        gate_scores, expert_idx = jax.lax.top_k(gate_logits, TOP_K)
        routing_weights = jax.nn.softmax(gate_scores, axis=-1)
        combine = jnp.zeros((T, E), tokens.dtype).at[jnp.arange(T)[:, None], expert_idx].add(routing_weights)

        def body(acc, params):
            W1, B1, W2, B2, c = params
            h = jax.nn.gelu(tokens @ W1.T + B1, approximate=False)
            o = h @ W2.T + B2
            return (acc + c[:, None] * o, None)
        out, _ = jax.lax.scan(body, jnp.zeros_like(tokens), (w1, b1, w2, b2, combine.T))
        return x + out.reshape(B, S, D)

    def _L1_xattn_ref(query, key, value, mask, Wq, Wk, Wv, Wo):
        import jax, jax.numpy as jnp
        import numpy as np
        D_MODEL = 128
        NUM_HEADS = 16
        D_KEY = D_MODEL // NUM_HEADS
        MASK_FUTURE = True
        NEG_INF = -jnp.inf
        B, Nq, _ = query.shape
        Nk = key.shape[1]

        def proj(x, W, N):
            return (x @ W).reshape(B, N, NUM_HEADS, D_KEY).transpose(0, 2, 1, 3)
        Q = proj(query, Wq, Nq)
        K = proj(key, Wk, Nk)
        V = proj(value, Wv, Nk)
        scores = jnp.einsum('bhqd,bhkd->bhqk', Q, K) / np.sqrt(D_KEY).astype(np.float32)
        scores = jnp.where(mask[:, None, None, :] == 0, NEG_INF, scores)
        if MASK_FUTURE:
            causal = jnp.triu(jnp.ones((Nq, Nk), dtype=jnp.bool_), k=1)
            scores = jnp.where(causal[None, None, :, :], NEG_INF, scores)
        attn = jax.nn.softmax(scores, axis=-1)
        out = jnp.einsum('bhqk,bhkd->bhqd', attn, V)
        out = out.transpose(0, 2, 1, 3).reshape(B, Nq, D_MODEL)
        return out @ Wo

    def _L1_ffn_ref(x, w_gate, w_up, w_down):
        import jax, jax.numpy as jnp
        import numpy as np
        HIDDEN = 128
        INNER = 512

        def _weight_quant(w):
            scale = 1.0 / jnp.clip(jnp.mean(jnp.abs(w)), 1e-05)
            wq = jnp.clip(jnp.round(w * scale), -1.0, 1.0) / scale
            return w + jax.lax.stop_gradient(wq - w)

        def _act_quant(x):
            scale = 127.0 / jnp.clip(jnp.max(jnp.abs(x), axis=-1, keepdims=True), 1e-05)
            xq = jnp.clip(jnp.round(x * scale), -128.0, 127.0) / scale
            return x + jax.lax.stop_gradient(xq - x)

        def _bitlinear(x, w):
            return jnp.einsum('bsi,oi->bso', _act_quant(x), _weight_quant(w))
        gate = jax.nn.silu(_bitlinear(x, w_gate))
        up = _bitlinear(x, w_up)
        return _bitlinear(gate * up, w_down)
    x = x + _L0_xattn_ref(_layernorm(x, axis=-1), ctx_1024, ctx_1024, L0_xattn_Wq, L0_xattn_bq, L0_xattn_Wk, L0_xattn_bk, L0_xattn_Wv, L0_xattn_bv, L0_xattn_Wo, L0_xattn_bo)
    x = x + _L0_ffn_ref(_layernorm(x, axis=-1), L0_ffn_norm_weight, L0_ffn_gate_w, L0_ffn_w1, L0_ffn_b1, L0_ffn_w2, L0_ffn_b2)
    x = x + _L1_xattn_ref(_layernorm(x, axis=-1), ctx_1024, ctx_1024, mask_BxS2_if1, L1_xattn_Wq, L1_xattn_Wk, L1_xattn_Wv, L1_xattn_Wo)
    x = x + _L1_ffn_ref(_layernorm(x, axis=-1), L1_ffn_w_gate, L1_ffn_w_up, L1_ffn_w_down)
    return x

_drawn_inputs = setup_inputs


def setup_inputs(seed=0):
    import zlib

    import numpy as np

    out = dict(_drawn_inputs(seed))
    spreads = {'L0_ffn_norm_weight': (1.0, 0.6), 'L0_ffn_b1': (0.0, 0.8), 'L0_ffn_b2': (0.0, 0.269)}
    factors = {'L0_xattn_bq': 2.917,
     'L0_xattn_bk': 64.0,
     'L0_ffn_w1': 4.438,
     'L0_ffn_w2': 4.006,
     'L1_xattn_Wq': 8.0,
     'L1_xattn_Wk': 8.0,
     'L1_xattn_Wv': 4.497,
     'L1_xattn_Wo': 4.313}
    for name, (base, spread) in spreads.items():
        noise = np.random.default_rng([zlib.crc32(name.encode()), seed]).standard_normal(out[name].shape)
        drawn = base * np.exp(spread * noise) if base else spread * noise
        out[name] = jnp.asarray(drawn.astype(out[name].dtype))
    for name, factor in factors.items():
        out[name] = (out[name] * factor).astype(out[name].dtype)
    return out
```

```python
from contextlib import ExitStack

import concourse.bass as bass
from concourse import mybir

ALU = mybir.AluOpType
ACT = mybir.ActivationFunctionType
AX_X = mybir.AxisListType.X
F32 = mybir.dt.float32
BF16 = mybir.dt.bfloat16
I32 = mybir.dt.int32
U32 = mybir.dt.uint32

P = 128
B = 16
T = B * P
D = 128
H = 16
DK = D // H
HQ = 4
NQ = H // HQ
G = 4
NG = B // G
GT = G * P
E = 8
HID = 256
M = HID // P
F = 512
FK = F // P
EPS_LN = 1e-5
EPS_RMS = 1e-6
SCALE = 1.0 / DK ** 0.5
MASKED = -1e30
MAGIC = 1.5 * 2.0 ** 23

Q_PART = (0, 0, 0, 1, 1, 2)
K_PART = (0, 1, 2, 0, 1, 0)
ROW_MAX = 64
ROW_MASK = 67
PARTS = 3


def wait(eng, sem, value):
    if isinstance(value, int) and value <= 0:
        return
    eng.wait_ge(sem, value)


def exists(b):
    return not isinstance(b, int) or 0 <= b < B


def bcast(ap, shape):
    return ap.to_broadcast(shape)


def mean_and_variance(dve, sem, st_all, mean, vareps, tmp):
    c = Chain(dve, sem, 0)
    c.step(dve.tensor_tensor(mean[:], st_all[:, :, 1], st_all[:, :, 4], ALU.add))
    c.step(dve.tensor_tensor(tmp[:], st_all[:, :, 1], st_all[:, :, 4], ALU.subtract))
    c.step(dve.tensor_tensor(vareps[:], st_all[:, :, 2], st_all[:, :, 5], ALU.add))
    c.settle()
    c.step(dve.tensor_scalar(mean[:], mean[:], 0.5, None, ALU.mult))
    c.step(dve.tensor_tensor(tmp[:], tmp[:], tmp[:], ALU.mult))
    c.step(dve.tensor_scalar(vareps[:], vareps[:], 1.0 / D, EPS_LN, ALU.mult, ALU.add))
    c.settle()
    c.step(dve.scalar_tensor_tensor(out=vareps[:], in0=tmp[:], scalar=0.25, in1=vareps[:],
                                    op0=ALU.mult, op1=ALU.add))
    assert c.n == STAT_STEPS


STAT_STEPS = 7


def of_slot(b, s, each):
    return (b - s) * (each // 2) + each


class Chain:

    def __init__(self, eng, sem, base):
        self.eng, self.sem, self.base, self.n = eng, sem, base, 0

    def step(self, ins):
        self.n += 1
        ins.then_inc(self.sem, 1)

    def settle(self):
        wait(self.eng, self.sem, self.base + self.n)


def main_kernel(nc, t):
    with ExitStack() as ctx:
        def sb(name, shape, dt, stack=ctx):
            return stack.enter_context(nc.sbuf_tensor(name, shape, dt))

        x_all = sb("x_all", [P, B, D], F32)
        st_all = sb("st_all", [P, B, 6], F32)
        mean = sb("mean", [P, B], F32)
        vareps = sb("vareps", [P, B], F32)
        rstd = sb("rstd", [P, B], F32)
        half = sb("half", [P, B], F32)
        ident = sb("ident", [P, P], F32)
        identb = sb("identb", [P, P], BF16)
        ones = sb("ones", [P, P], F32)
        oneb = sb("oneb", [P, T], BF16)
        zerob = sb("zerob", [P, T], BF16)
        upper = sb("upper", [P, P], BF16)
        lower = sb("lower", [P, P], BF16)
        attn_w = sb("attn_w", [P, 2, 4, D], F32)
        attn_bias = sb("attn_bias", [P, 2], F32)
        row_bias = sb("row_bias", [P, 2, D], F32)
        gate_w = sb("gate_w", [P, E], F32)
        norm_w = sb("norm_w", [P, 1], F32)
        b1 = sb("b1", [P, E * M], F32)
        b2 = sb("b2", [E, D], F32)
        iota_e = sb("iota_e", [P, E], F32)
        ffn_wq = sb("ffn_wq", [P, 3, F], BF16)
        w_scale = sb("w_scale", [P, 4], F32)

        with ExitStack() as ph:
            ffn_w = sb("ffn_w", [P, 3, F], F32, ph)
            wtmp = sb("wtmp", [P, 3, F], F32, ph)
            iota_i = sb("iota_i", [P, E], I32, ph)
            wsum = sb("wsum", [P, 4], F32, ph)
            winv = sb("winv", [P, 4], F32, ph)
            ps = ph.enter_context(nc.psum_tensor("ps_setup", [P, 512], F32))
            x_in, small_in, ffn_in = (ph.enter_context(nc.semaphore(n)) for n in ("x_in", "small_in", "ffn_in"))
            consts, dve_step, pool_step, sums_done, wsum_ready = (
                ph.enter_context(nc.semaphore(n)) for n in ("consts", "dve_step0", "pool_step0", "sums_done", "wsum_ready"))
            stats_ready = ph.enter_context(nc.semaphore("stats_ready0"))
            block = ph.enter_context(nc.Block())

            @block.sync
            def _(sp):
                sp.dma_start(x_all[:], t["x"].rearrange("b s d -> s b d")).then_inc(x_in, 16)
                for n, key in enumerate(("w_gate", "w_up")):
                    sp.dma_start(ffn_w[:, n, :], t[key]).then_inc(ffn_in, 16)
                sp.dma_start(ffn_w[:, 2, :].rearrange("p (k o) -> p k o", k=FK),
                             t["w_down"]).then_inc(ffn_in, 16)
                n = 0
                for layer in range(2):
                    for m, key in enumerate(("Wq", "Wk", "Wv", "Wo")):
                        sp.dma_start(attn_w[:, layer, m, :], t[f"L{layer}_{key}"]).then_inc(small_in, 16)
                        n += 1
                for dst, src in ((attn_bias[:, 0:1], t["bq"]), (attn_bias[:, 1:2], t["bk"]),
                                 (row_bias[:, 0, :], t["bv"].to_broadcast([P, D])),
                                 (row_bias[:, 1, :], t["bo"].to_broadcast([P, D])),
                                 (gate_w[:], t["gate_w"]), (norm_w[:], t["norm_w"]),
                                 (b1[:], t["b1"]), (b2[:], t["b2"])):
                    sp.dma_start(dst, src).then_inc(small_in, 16)
                    n += 1
                sp.wait_ge(small_in, 16 * n)

            @block.gpsimd
            def _(pool):
                pool.memset(ident[:], 0.0).then_inc(pool_step, 1)
                pool.memset(identb[:], 0.0).then_inc(pool_step, 1)
                pool.memset(upper[:], 0.0).then_inc(pool_step, 1)
                pool.memset(lower[:], 0.0).then_inc(pool_step, 1)
                pool.memset(half[:], -0.5).then_inc(pool_step, 1)
                pool.memset(ones[:], 1.0).then_inc(consts, 1)
                pool.iota(iota_i[:], pattern=[[1, E]], base=0, channel_multiplier=0).then_inc(pool_step, 1)
                pool.wait_ge(pool_step, 6)
                for tile, on in ((ident, 1.0), (identb, 1.0)):
                    pool.affine_select(out=tile[:], in_=tile[:], compare_op=ALU.not_equal, fill=on, base=0,
                                       pattern=[[-1, P]], channel_multiplier=1).then_inc(consts, 1)
                pool.affine_select(out=upper[:], in_=upper[:], compare_op=ALU.is_ge, fill=MASKED, base=0,
                                   pattern=[[-1, P]], channel_multiplier=1).then_inc(consts, 1)
                pool.affine_select(out=lower[:], in_=lower[:], compare_op=ALU.is_ge, fill=MASKED, base=0,
                                   pattern=[[1, P]], channel_multiplier=-1).then_inc(consts, 1)
                pool.tensor_copy(iota_e[:], iota_i[:]).then_inc(consts, 1)
                pool.memset(oneb[:], 1.0).then_inc(consts, 1)
                pool.memset(zerob[:], 0.0).then_inc(consts, 1)

            @block.vector
            def _(dve):
                c = Chain(dve, dve_step, 0)
                dve.wait_ge(x_in, 16)
                for b in range(B):
                    dve.bn_stats(st_all[:, b, :], x_all[:, b, :]).then_inc(stats_ready, 1)
                dve.wait_ge(ffn_in, 48)
                for n in range(3):
                    dve.tensor_reduce(wsum[:, n:n + 1], ffn_w[:, n, :], AX_X, ALU.add,
                                      apply_absolute_value=True).then_inc(wsum_ready, 1)
                dve.wait_ge(sums_done, 1)
                c.step(dve.tensor_scalar(w_scale[:, 0:3], ps[:, 0:3], 1.0 / (D * F), EPS_LN, ALU.mult, ALU.max))
                c.settle()
                c.step(dve.reciprocal(winv[:, 0:3], w_scale[:, 0:3]))
                c.settle()
                for n in range(3):
                    c.step(dve.tensor_scalar(wtmp[:, n, :], ffn_w[:, n, :], winv[:, n:n + 1], 1.0, ALU.mult, ALU.min))
                c.settle()
                c.step(dve.tensor_scalar(wtmp[:], wtmp[:], -1.0, MAGIC, ALU.max, ALU.add))
                c.settle()
                c.step(dve.tensor_scalar(ffn_wq[:], wtmp[:], -MAGIC, None, ALU.add))

            @block.tensor
            def _(pe):
                pe.wait_ge(consts, 1)
                pe.wait_ge(wsum_ready, 3)
                pe.matmul(ps[:, 0:3], ones[:], wsum[:, 0:3], start=True, stop=True).then_inc(sums_done, 1)

        with ExitStack() as ph:
            q_rows = sb("q_rows", [P, H, T], BF16, ph)
            k_rows = sb("k_rows", [P, H, T], BF16, ph)
            v_all = sb("v_all", [P, B, D], F32, ph)
            fill_rows(nc, t, q_rows, k_rows, oneb, zerob)
            for layer in range(2):
                if layer == 1:
                    moe(nc, t, x_all, st_all, mean, vareps, rstd, half, ident, gate_w, norm_w, b1, b2, iota_e)
                prepare(nc, t, layer, x_all, st_all, mean, vareps, rstd, half, ident, attn_w, attn_bias, row_bias, v_all,
                        q_rows, k_rows, oneb, zerob)
                attention(nc, layer, x_all, st_all, ident, identb, upper, lower, attn_w, row_bias, v_all,
                          q_rows, k_rows)
        ternary_ffn(nc, t, x_all, st_all, mean, vareps, rstd, half, identb, ffn_wq, w_scale)


def fill_rows(nc, t, q_rows, k_rows, oneb, zerob):
    with ExitStack() as ph:
        cleared, filled = (ph.enter_context(nc.semaphore(n)) for n in ("cleared", "filled"))
        block = ph.enter_context(nc.Block())

        @block.vector
        def _(dve):
            dve.memset(q_rows[:].rearrange("p h t -> p (h t)").bitcast(U32), 0).then_inc(cleared, 1)

        @block.gpsimd
        def _(pool):
            pool.memset(k_rows[:].rearrange("p h t -> p (h t)").bitcast(U32), 0).then_inc(cleared, 1)

        @block.sync
        def _(sp):
            sp.wait_ge(cleared, 2)
            for r in range(PARTS):
                sp.dma_start(k_rows[ROW_MAX + r:ROW_MAX + r + 1, :, :], oneb[0:H, :]).then_inc(filled, 16)
            sp.wait_ge(filled, 16 * PARTS)


def prepare(nc, t, layer, x_all, st_all, mean, vareps, rstd, half, ident, attn_w, attn_bias, row_bias, v_all,
            q_rows, k_rows, oneb, zerob):
    with ExitStack() as ph:
        def sb(name, shape, dt):
            return ph.enter_context(nc.sbuf_tensor(f"{name}{layer}", shape, dt))

        def sem(name):
            return ph.enter_context(nc.semaphore(f"{name}{layer}"))

        SL = 2
        ctx_t = sb("ctx_t", [P, SL, GT], F32)
        xn = sb("xn", [P, SL, G, D], F32)
        xn_t = sb("xn_t", [P, SL, GT], F32)
        full = sb("full", [P, SL, 2, GT], F32)
        rest = sb("rest", [P, SL, 2, GT], F32)
        parts = sb("parts", [P, SL, 2, PARTS, GT], BF16)
        mask_i = sb("mask_i", [B, P], I32)
        mask_b = sb("mask_b", [B, P], BF16)
        tmp = sb("tmp", [P, B], F32)
        ps_t = ph.enter_context(nc.psum_tensor(f"ps_t{layer}", [P, SL, GT], F32))
        ps_qk = ph.enter_context(nc.psum_tensor(f"ps_qk{layer}", [P, 2, 2, GT], F32))
        ps_v = ph.enter_context(nc.psum_tensor(f"ps_v{layer}", [P, SL, GT], F32))
        parts_dram = nc.dram_tensor(f"parts_dram{layer}", (NG, 2, P, PARTS, GT), BF16).ap()

        ctx_in = [sem(f"ctx_in_{s}_") for s in range(SL)]
        mask_in, var_ready, rstd_ready = sem("mask_in"), sem("var_ready"), sem("rstd_ready")
        xn_ready, t_done, xt_ready = sem("xn_ready"), sem("t_done"), sem("xt_ready")
        qk_done, v_done, full_ready, v_ready = sem("qk_done"), sem("v_done"), sem("full_ready"), sem("v_ready")
        first_ready, parts_ready, split_step = sem("first_ready"), sem("parts_ready"), sem("split_step")
        stored, laid, mask_ready = sem("stored"), sem("laid"), sem("mask_ready")
        bias_added = sem("bias_added")
        block = ph.enter_context(nc.Block())

        @block.sync
        def _(sp):
            n_extra = 0
            if layer == 1:
                sp.dma_start(mask_i[:], t["mask"]).then_inc(mask_in, 16)
                for r in range(PARTS):
                    sp.dma_start(q_rows[ROW_MAX + r:ROW_MAX + r + 1, :, :], zerob[0:H, :]).then_inc(laid, 16)
                sp.dma_start(q_rows[ROW_MASK:ROW_MASK + 1, :, :], oneb[0:H, :]).then_inc(laid, 16)
                sp.wait_ge(mask_ready, 1)
                for h in range(H):
                    sp.dma_start(k_rows[ROW_MASK:ROW_MASK + 1, h, :], mask_b[:]).then_inc(laid, 16)
                n_extra = PARTS + 1 + H

            def load(g, s):
                wait(sp, v_done, g - SL + 1)
                sp.dma_start(ctx_t[:, s, :], t["ctx_t"][:, bass.ds(g * GT, GT)]).then_inc(ctx_in[s], 16)

            def lay_out(g, s):
                sp.wait_ge(parts_ready, 2 * g + 2)
                for side in range(2):
                    sp.dma_start(parts_dram[bass.ds(g, 1), side].rearrange("g p r s -> (g p) r s"),
                                 parts[:, s, side]).then_inc(stored, 16)
                sp.wait_ge(stored, 32 * g + 32)
                for side, rows, which in ((0, q_rows, Q_PART), (1, k_rows, K_PART)):
                    for r, part in enumerate(which):
                        src = parts_dram[bass.ds(g, 1), side, :, part].rearrange("g (h d) s -> (g d) h s", d=DK)
                        sp.dma_start(rows[r * DK:(r + 1) * DK, :, bass.ds(g * GT, GT)], src).then_inc(laid, 16)

            for g in range(SL):
                load(g, g)
            for g in range(NG):
                lay_out(g, g % SL)
                if g + SL < NG:
                    load(g + SL, g % SL)
            sp.wait_ge(laid, 16 * (n_extra + 2 * len(Q_PART) * NG))

        @block.gpsimd
        def _(pool):
            pool.wait_ge(var_ready, STAT_STEPS)
            pool.tensor_tensor(rstd[:], vareps[:], half[:], ALU.pow).then_inc(rstd_ready, 1)
            if layer == 0:
                pool.wait_ge(xn_ready, B)
                pool.tensor_tensor(x_all[:], x_all[:], row_bias[:, 1, :].unsqueeze(1).to_broadcast([P, B, D]),
                                   ALU.add).then_inc(bias_added, 1)

        @block.vector
        def _(dve):
            mean_and_variance(dve, var_ready, st_all, mean, vareps, tmp)
            if layer == 1:
                dve.wait_ge(mask_in, 16)
                dve.tensor_scalar(mask_b[:], mask_i[:], 0, MASKED, ALU.is_equal, ALU.mult).then_inc(mask_ready, 1)
            dve.wait_ge(rstd_ready, 1)

            def normalise(g, s):
                wait(dve, t_done, g - SL + 1)
                for j in range(G):
                    b = g * G + j
                    dve.tensor_scalar(xn[:, s, j, :], x_all[:, bass.ds(b, 1), :].rearrange("p b d -> p (b d)"),
                                      mean[:, bass.ds(b, 1)], rstd[:, bass.ds(b, 1)],
                                      ALU.subtract, ALU.mult).then_inc(xn_ready, 1)

            def split(g, s):
                c = Chain(dve, split_step, g * 4)
                dve.wait_ge(v_done, g + 1)
                v_out = v_all[:, bass.ds(g * G, G), :]
                v_in = ps_v[:, s, :].rearrange("p (j d) -> p j d", j=G)
                if layer == 0:
                    dve.tensor_tensor(v_out, v_in, row_bias[:, 0, :].unsqueeze(1).to_broadcast([P, G, D]),
                                      ALU.add).then_inc(v_ready, 1)
                else:
                    dve.tensor_copy(v_out, v_in).then_inc(v_ready, 1)
                wait(dve, stored, 32 * (g - SL + 1))
                for side in range(2):
                    dve.wait_ge(first_ready, 2 * g + side + 1)
                    dve.wait_ge(full_ready, 2 * g + side + 1)
                    c.step(dve.tensor_tensor(rest[:, s, side], full[:, s, side], parts[:, s, side, 0], ALU.subtract))
                    c.settle()
                    c.step(dve.tensor_copy(parts[:, s, side, 1], rest[:, s, side]))
                    c.settle()
                    dve.tensor_tensor(parts[:, s, side, 2], rest[:, s, side], parts[:, s, side, 1],
                                      ALU.subtract).then_inc(parts_ready, 1)

            normalise(0, 0)
            for g in range(NG):
                if g + 1 < NG:
                    normalise(g + 1, (g + 1) % SL)
                split(g, g % SL)

        @block.tensor
        def _(pe):
            def group(g, s):
                pe.wait_ge(xn_ready, g * G + G)
                wait(pe, xt_ready, g - SL + 1)
                for j in range(G):
                    last = pe.transpose(ps_t[:, s, j * P:(j + 1) * P], xn[:, s, j, :], ident[:])
                last.then_inc(t_done, 1)
                pe.wait_ge(ctx_in[s], of_slot(g, s, 16))
                wait(pe, v_ready, g - SL + 1)
                for j in range(G):
                    last = pe.matmul(ps_v[:, s, j * D:(j + 1) * D], ctx_t[:, s, j * P:(j + 1) * P],
                                     attn_w[:, layer, 2, :], start=True, stop=True)
                wait(pe, full_ready, 2 * (g - SL + 1))
                pe.matmul(ps_qk[:, 1, s, :], attn_w[:, layer, 1, :], ctx_t[:, s, :],
                          start=True, stop=True).then_inc(v_done, 1)
                pe.wait_ge(xt_ready, g + 1)
                pe.matmul(ps_qk[:, 0, s, :], attn_w[:, layer, 0, :], xn_t[:, s, :],
                          start=True, stop=True).then_inc(qk_done, 1)

            for g in range(NG):
                group(g, g % SL)

        @block.scalar
        def _(act):
            def group(g, s):
                act.wait_ge(t_done, g + 1)
                wait(act, qk_done, g - SL + 1)
                act.activation(xn_t[:, s, :], ps_t[:, s, :], ACT.Copy).then_inc(xt_ready, 1)
                act.wait_ge(qk_done, g + 1)
                wait(act, parts_ready, 2 * (g - SL + 1))
                wait(act, stored, 32 * (g - SL + 1))
                for side in range(2):
                    bias = attn_bias[:, side:side + 1] if layer == 0 else 0.0
                    act.activation(parts[:, s, side, 0], ps_qk[:, side, s, :], ACT.Identity, bias=bias)\
                       .then_inc(first_ready, 1)
                    act.activation(full[:, s, side], ps_qk[:, side, s, :], ACT.Identity, bias=bias)\
                       .then_inc(full_ready, 1)

            for g in range(NG):
                group(g, g % SL)


def attention(nc, layer, x_all, st_all, ident, identb, upper, lower, attn_w, row_bias, v_all, q_rows, k_rows):
    with ExitStack() as ph:
        def sb(name, shape, dt):
            return ph.enter_context(nc.sbuf_tensor(f"{name}{layer}", shape, dt))

        def psum(name, shape, dt):
            return ph.enter_context(nc.psum_tensor(f"{name}{layer}", shape, dt))

        def sem(name):
            return ph.enter_context(nc.semaphore(f"{name}{layer}"))

        W = HQ * P
        VW = 32
        neg = sb("neg", [P, 2, H], F32)
        neg_rest = sb("neg_rest", [P, 2, H], F32)
        neg_parts = sb("neg_parts", [P, 2, P], BF16)
        neg_t = sb("neg_t", [PARTS * H, 2, P], BF16)
        probs = sb("probs", [P, NQ, W], F32)
        v_aug = sb("v_aug", [P, 2, H, VW], F32)
        o_t = sb("o_t", [P, 2, W], F32)
        inv = sb("inv", [P, 2, H], F32)
        o = sb("o", [P, 2, D], F32)
        oo_t = sb("oo_t", [P, 2, P], F32)
        ps_s = psum("ps_s", [P, 2, W], F32)
        ps_e = psum("ps_e", [P, 2, W], F32)
        ps_v = psum("ps_pv", [P, W], F32)
        ps_o = psum("ps_o", [P, W], F32)
        ps_n = psum("ps_n", [P, 2 * W], BF16)
        ps_y = psum("ps_y", [P, W], F32)

        scored, max_done, neg_step, neg_ready = sem("scored"), sem("max_done"), sem("neg_step"), sem("neg_ready")
        negt_done, negt_ready = sem("negt_done"), sem("negt_ready")
        neg_laid = [sem(f"neg_laid_{s}_") for s in range(2)]
        shifted, exp_done, pv_done, vaug_ready = sem("shifted"), sem("exp_done"), sem("pv_done"), sem("vaug_ready")
        ot_ready, ot_back, inv_ready, o_ready = sem("ot_ready"), sem("ot_back"), sem("inv_ready"), sem("o_ready")
        oot_done, oot_ready, y_done, x_ready = sem("oot_done"), sem("oot_ready"), sem("y_done"), sem("x_ready")
        st_ready, padded, cleared = sem("st_ready"), sem("padded"), sem("cleared")
        block = ph.enter_context(nc.Block())

        def run(eng, step):
            for b in range(-2, 2):
                step(b, b % 2)
            with eng.Fori(1, B // 2 - 1) as i:
                for j in range(2):
                    step(i * 2 + j, j)
            for b in range(B - 2, B + 2):
                step(b, b % 2)

        @block.tensor
        def _(pe):
            def cols(b):
                return bass.ds(b * P, P)

            def scores(b, q):
                n = b * NQ + q
                wait(pe, max_done, n - 1)
                bank = ps_s[:, q % 2, :]
                if layer == 1:
                    pe.matmul(bank, identb[:], upper[:].unsqueeze(1).to_broadcast([P, HQ, P]),
                              start=True, stop=False, skip_group_check=True)
                for j in range(HQ):
                    h = q * HQ + j
                    last = pe.matmul(ps_s[:, q % 2, j * P:(j + 1) * P], q_rows[:, h, cols(b)], k_rows[:, h, cols(b)],
                                     start=(layer == 0), stop=True, skip_group_check=True)
                last.then_inc(scored, 1)

            def shifted_scores(b, q, s):
                n = b * NQ + q
                if q == 0:
                    wait(pe, neg_laid[s], of_slot(b, s, 16 * PARTS))
                wait(pe, exp_done, n - 1)
                if layer == 1:
                    pe.matmul(ps_e[:, q % 2, :], identb[:], lower[:].unsqueeze(1).to_broadcast([P, HQ, P]),
                              start=True, stop=False, skip_group_check=True)
                for j in range(HQ):
                    h = q * HQ + j
                    last = pe.matmul(ps_e[:, q % 2, j * P:(j + 1) * P], k_rows[:, h, cols(b)], q_rows[:, h, cols(b)],
                                     start=(layer == 0), stop=True, skip_group_check=True)
                last.then_inc(shifted, 1)

            def values(b, q, s):
                n = b * NQ + q
                if q == 0:
                    wait(pe, vaug_ready, b + 1)
                    wait(pe, ot_ready, b)
                wait(pe, exp_done, n + 1)
                for j in range(HQ):
                    last = pe.matmul(ps_v[VW * j:VW * (j + 1), q * P:(q + 1) * P], v_aug[:, s, q * HQ + j, :],
                                     probs[:, q, j * P:(j + 1) * P], start=True, stop=True)
                last.then_inc(pv_done, 1)

            def turn_maxima(b, s):
                wait(pe, neg_ready, b + 1)
                wait(pe, negt_ready, b)
                pe.transpose(ps_n[:, 0:P], neg_parts[:, s, :], identb[:])\
                  .then_inc(negt_done, 1)

            def turn_back(b, s):
                wait(pe, ot_ready, b + 1)
                wait(pe, o_ready, b)
                for q in range(NQ):
                    last = pe.transpose(ps_o[:, q * P:(q + 1) * P], o_t[:, s, q * P:(q + 1) * P], ident[:])
                last.then_inc(ot_back, 1)

            def turn_output(b, s):
                wait(pe, o_ready, b + 1)
                wait(pe, x_ready, b)
                pe.transpose(ps_y[:, 0:P], o[:, s, :], ident[:]).then_inc(oot_done, 1)

            def project(b, s):
                wait(pe, oot_ready, b + 1)
                pe.matmul(ps_y[:, P:2 * P], oo_t[:, s, :], attn_w[:, layer, 3, :], start=True, stop=True)\
                  .then_inc(y_done, 1)

            def step(b, s):
                for q in range(NQ):
                    if exists(b + 2):
                        scores(b + 2, q)
                    if exists(b):
                        shifted_scores(b, q, s)
                    if q == 0 and exists(b - 1):
                        values(b - 1, NQ - 1, 1 - s)
                    if q > 0 and exists(b):
                        values(b, q - 1, s)
                    if q == 0 and exists(b - 2):
                        project(b - 2, s)
                    if q == 1 and exists(b + 1):
                        turn_maxima(b + 1, 1 - s)
                    if q == 2 and exists(b - 1):
                        turn_back(b - 1, 1 - s)
                    if q == 3 and exists(b - 1):
                        turn_output(b - 1, 1 - s)

            run(pe, step)

        @block.vector
        def _(dve):
            def maxima(b, q, s):
                n = b * NQ + q
                wait(dve, scored, n + 1)
                dve.tensor_reduce(neg[:, s, q * HQ:(q + 1) * HQ], ps_s[:, q % 2, :].rearrange("p (h k) -> p h k", h=HQ),
                                  AX_X, ALU.max, negate=True).then_inc(max_done, 1)

            def split(b, s):
                c = Chain(dve, neg_step, b * 3)
                wait(dve, max_done, (b + 1) * NQ)
                c.step(dve.tensor_copy(neg_parts[:, s, 0 * H:1 * H], neg[:, s, :]))
                c.settle()
                c.step(dve.tensor_tensor(neg_rest[:, s, :], neg[:, s, :], neg_parts[:, s, 0 * H:1 * H], ALU.subtract))
                c.settle()
                c.step(dve.tensor_copy(neg_parts[:, s, 1 * H:2 * H], neg_rest[:, s, :]))
                c.settle()
                dve.tensor_tensor(neg_parts[:, s, 2 * H:3 * H], neg_rest[:, s, :], neg_parts[:, s, 1 * H:2 * H],
                                  ALU.subtract).then_inc(neg_ready, 1)

            def normalise(b, s):
                wait(dve, ot_back, b + 1)
                heads = ps_o[:].rearrange("p (h c) -> p h c", h=H)
                dve.reciprocal(inv[:, s, :], heads[:, :, DK]).then_inc(inv_ready, 1)
                wait(dve, inv_ready, b + 1)
                dve.tensor_tensor(o[:, s, :].rearrange("p (h d) -> p h d", h=H), heads[:, :, 0:DK],
                                  inv[:, s, :].unsqueeze(2).to_broadcast([P, H, DK]), ALU.mult).then_inc(o_ready, 1)

            def residual(b, s):
                wait(dve, y_done, b + 1)
                x_b = x_all[:, bass.ds(b, 1), :].rearrange("p b d -> p (b d)")
                dve.tensor_tensor(x_b, ps_y[:, P:2 * P], x_b, ALU.add).then_inc(x_ready, 1)

            def stats(b):
                dve.bn_stats(st_all[:, bass.ds(b, 1), :].rearrange("p b n -> p (b n)"),
                             x_all[:, bass.ds(b, 1), :].rearrange("p b d -> p (b d)")).then_inc(st_ready, 1)

            dve.wait_ge(padded, 1)

            def step(b, s):
                for q in range(NQ):
                    if q == 1 and exists(b - 2):
                        wait(dve, x_ready, b - 1)
                    if exists(b + 2):
                        maxima(b + 2, q, s)
                    if q == 0 and exists(b - 2):
                        residual(b - 2, s)
                    if q == 1 and exists(b - 2):
                        stats(b - 2)
                    if q == 2 and exists(b - 1):
                        normalise(b - 1, 1 - s)
                if exists(b + 2):
                    split(b + 2, s)

            run(dve, step)

        @block.scalar
        def _(act):
            def exponentials(b, q):
                n = b * NQ + q
                wait(act, shifted, n + 1)
                wait(act, pv_done, n - NQ + 1)
                act.activation(probs[:, q, :], ps_e[:, q % 2, :], ACT.Exp, scale=SCALE).then_inc(exp_done, 1)

            def copy_sums(b, s):
                wait(act, pv_done, (b + 1) * NQ)
                wait(act, ot_back, b - 1)
                act.activation(o_t[:, s, :], ps_v[:], ACT.Copy).then_inc(ot_ready, 1)

            def copy_maxima(b, s):
                wait(act, negt_done, b + 1)
                wait(act, neg_laid[s], of_slot(b - 2, s, 16 * PARTS))
                act.activation(neg_t[:, s, :], ps_n[0:PARTS * H, 0:P], ACT.Copy).then_inc(negt_ready, 1)

            def copy_output(b, s):
                wait(act, oot_done, b + 1)
                wait(act, y_done, b - 1)
                act.activation(oo_t[:, s, :], ps_y[:, 0:P], ACT.Copy).then_inc(oot_ready, 1)

            def step(b, s):
                for q in range(NQ):
                    if exists(b):
                        exponentials(b, q)
                    if q == 0 and exists(b - 1):
                        copy_sums(b - 1, 1 - s)
                    if q == 1 and exists(b + 1):
                        copy_maxima(b + 1, 1 - s)
                    if q == 3 and exists(b - 1):
                        copy_output(b - 1, 1 - s)

            run(act, step)

        @block.sync
        def _(sp):
            def lay_maxima(b, s):
                sp.wait_ge(negt_ready, b + 1)
                for r in range(PARTS):
                    sp.dma_start(q_rows[ROW_MAX + r:ROW_MAX + r + 1, :, bass.ds(b * P, P)],
                                 neg_t[r * H:(r + 1) * H, s, :]).then_inc(neg_laid[s], 16)

            with sp.Fori(0, B // 2) as i:
                for j in range(2):
                    lay_maxima(i * 2 + j, j)

        @block.gpsimd
        def _(pool):
            pool.memset(neg_parts[:], 0.0).then_inc(padded, 1)
            pool.memset(v_aug[:], 0.0).then_inc(cleared, 1)
            pool.wait_ge(cleared, 1)
            pool.memset(v_aug[:, :, :, DK:DK + 1], 1.0).then_inc(cleared, 1)

            def fill(b, s):
                wait(pool, pv_done, (b - 1) * NQ)
                pool.tensor_copy(v_aug[:, s, :, 0:DK],
                                 v_all[:, bass.ds(b, 1), :].rearrange("p b (h d) -> p (b h) d", h=H))\
                    .then_inc(vaug_ready, 1)

            pool.wait_ge(cleared, 2)
            for b in range(2):
                fill(b, b)
            with pool.Fori(1, B // 2) as i:
                for j in range(2):
                    fill(i * 2 + j, j)


def moe(nc, t, x_all, st_all, mean, vareps, rstd, half, ident, gate_w, norm_w, b1, b2, iota_e):
    with ExitStack() as outer:
        tok_t = outer.enter_context(nc.sbuf_tensor("tok_t", [P, T], F32))
        comb = outer.enter_context(nc.sbuf_tensor("comb", [P, B, E], F32))
        w1 = outer.enter_context(nc.sbuf_tensor("w1", [P, E, HID], F32))
        w2 = outer.enter_context(nc.sbuf_tensor("w2", [P, E, M, D], F32))
        with ExitStack() as ph:
            def sb(name, shape, dt):
                return ph.enter_context(nc.sbuf_tensor(name, shape, dt))

            def sem(name):
                return ph.enter_context(nc.semaphore(name))

            tmp, ms, rms = sb("tmp_m", [P, B], F32), sb("ms", [P, B], F32), sb("rms", [P, B], F32)
            xh, tk, tks = sb("xh", [P, 2, D], F32), sb("tk", [P, 2, D], F32), sb("tks", [P, 2, P], F32)
            logits = sb("logits", [P, B, E], F32)
            top, idx = sb("top", [P, B, E], F32), sb("idx", [P, B, E], U32)
            idx_f, eq = sb("idx_f", [P, B, 2], F32), sb("eq", [P, 2, B, E], F32)
            diff, ex, den, wt = sb("diff", [P, B], F32), sb("ex", [P, B], F32), sb("den", [P, B], F32), sb("wt", [P, 2, B], F32)
            ps_t = ph.enter_context(nc.psum_tensor("ps_tm", [P, 2, 512], F32))
            ps_g = ph.enter_context(nc.psum_tensor("ps_g", [P, 2, 512], F32))
            w_in, pool_chain, rstd_ready, ms_ready, rms_ready = (
                sem("w_in"), sem("pool_chain"), sem("rstd_ready_m"), sem("ms_ready"), sem("rms_ready"))
            xh_ready, tk_ready, x_added = sem("xh_ready"), sem("tk_ready"), sem("x_added")
            t_done, tks_ready, kept, g_done, top_step = (
                sem("t_done_m"), sem("tks_ready"), sem("kept"), sem("g_done"), sem("top_step"))
            tail, diff_ready, ex_ready = sem("tail"), sem("diff_ready"), sem("ex_ready")
            lg_ready, var_ready, ms_sq = sem("lg_ready"), sem("var_ready_m"), sem("ms_sq")
            block = ph.enter_context(nc.Block())

            @block.sync
            def _(sp):
                sp.dma_start(w1[:], t["w1"]).then_inc(w_in, 16)
                sp.dma_start(w2[:], t["w2"]).then_inc(w_in, 16)
                sp.wait_ge(w_in, 32)

            @block.gpsimd
            def _(pool):
                pool.wait_ge(var_ready, STAT_STEPS)
                pool.tensor_tensor(rstd[:], vareps[:], half[:], ALU.pow).then_inc(rstd_ready, 1)
                pool.wait_ge(ms_ready, 3)
                pool.tensor_tensor(rms[:], ms[:], half[:], ALU.pow).then_inc(rms_ready, 1)

                def batch(b, s):
                    pool.wait_ge(xh_ready, b + 1)
                    pool.wait_ge(tk_ready, b + 1)
                    x_b = x_all[:, bass.ds(b, 1), :].rearrange("p b d -> p (b d)")
                    pool.tensor_tensor(x_b, x_b, xh[:, s, :], ALU.add).then_inc(x_added, 1)
                    pool.wait_ge(tks_ready, b + 1)
                    pool.tensor_copy(tok_t[:, bass.ds(b * P, P)], tks[:, s, :]).then_inc(kept, 1)

                with pool.Fori(0, B // 2) as i:
                    for j in range(2):
                        batch(i * 2 + j, j)

            @block.vector
            def _(dve):
                mean_and_variance(dve, var_ready, st_all, mean, vareps, tmp)
                dve.wait_ge(var_ready, STAT_STEPS)
                dve.tensor_scalar(tmp[:], vareps[:], -EPS_LN, None, ALU.add).then_inc(ms_ready, 1)
                dve.wait_ge(ms_ready, 1)
                dve.wait_ge(rstd_ready, 1)
                dve.tensor_tensor(ms[:], tmp[:], rstd[:], ALU.mult).then_inc(ms_ready, 1)
                dve.wait_ge(ms_ready, 2)
                dve.tensor_tensor(ms[:], ms[:], rstd[:], ALU.mult).then_inc(ms_sq, 1)
                dve.wait_ge(ms_sq, 1)
                dve.tensor_scalar(ms[:], ms[:], EPS_RMS, None, ALU.add).then_inc(ms_ready, 1)
                dve.wait_ge(rms_ready, 1)

                def normalise(b, s):
                    wait(dve, x_added, b - 1)
                    dve.tensor_scalar(xh[:, s, :], x_all[:, bass.ds(b, 1), :].rearrange("p b d -> p (b d)"),
                                      mean[:, bass.ds(b, 1)], rstd[:, bass.ds(b, 1)],
                                      ALU.subtract, ALU.mult).then_inc(xh_ready, 1)
                    dve.wait_ge(xh_ready, b + 1)
                    wait(dve, t_done, b - 1)
                    dve.tensor_scalar(tk[:, s, :], xh[:, s, :], rms[:, bass.ds(b, 1)], None, ALU.mult)\
                       .then_inc(tk_ready, 1)

                def rank(b, s):
                    dve.wait_ge(g_done, b + 1)
                    lg = logits[:, bass.ds(b, 1), :].rearrange("p b e -> p (b e)")
                    dve.tensor_copy(lg, ps_g[:, s, 0:E]).then_inc(lg_ready, 1)

                normalise(0, 0)
                normalise(1, 1)
                with dve.Fori(0, B // 2 - 1) as i:
                    for j in range(2):
                        rank(i * 2 + j, j)
                        normalise(i * 2 + j + 2, j)
                rank(B - 2, 0)
                rank(B - 1, 1)
                dve.wait_ge(lg_ready, B)
                for b in range(B):
                    dve.max(top[:, b, :], logits[:, b, :]).then_inc(top_step, 1)
                dve.wait_ge(top_step, B)
                for b in range(B):
                    dve.max_index(idx[:, b, :], top[:, b, :], logits[:, b, :]).then_inc(top_step, 1)
                c = Chain(dve, tail, 0)
                dve.wait_ge(top_step, 2 * B)
                c.step(dve.tensor_copy(idx_f[:], idx[:, :, 0:2]))
                dve.tensor_tensor(diff[:], top[:, :, 1], top[:, :, 0], ALU.subtract).then_inc(diff_ready, 1)
                c.settle()
                for n in range(2):
                    c.step(dve.tensor_tensor(eq[:, n], iota_e[:].unsqueeze(1).to_broadcast([P, B, E]),
                                             idx_f[:, :, n:n + 1].to_broadcast([P, B, E]), ALU.is_equal))
                dve.wait_ge(ex_ready, 1)
                c.step(dve.tensor_scalar(den[:], ex[:], 1.0, None, ALU.add))
                c.settle()
                c.step(dve.reciprocal(wt[:, 0, :], den[:]))
                c.settle()
                c.step(dve.tensor_tensor(wt[:, 1, :], ex[:], wt[:, 0, :], ALU.mult))
                c.settle()
                for n in range(2):
                    c.step(dve.tensor_tensor(eq[:, n], eq[:, n], wt[:, n, :].unsqueeze(2).to_broadcast([P, B, E]),
                                             ALU.mult))
                c.settle()
                c.step(dve.tensor_tensor(comb[:], eq[:, 0], eq[:, 1], ALU.add))

            @block.tensor
            def _(pe):
                def turn(b, s):
                    pe.wait_ge(tk_ready, b + 1)
                    wait(pe, tks_ready, b - 1)
                    pe.transpose(ps_t[:, s, 0:P], tk[:, s, :], ident[:]).then_inc(t_done, 1)

                def gate(b, s):
                    pe.wait_ge(tks_ready, b + 1)
                    wait(pe, lg_ready, b - 1)
                    pe.matmul(ps_g[:, s, 0:E], tks[:, s, :], gate_w[:], start=True, stop=True).then_inc(g_done, 1)

                turn(0, 0)
                turn(1, 1)
                for b in range(2):
                    gate(b, b)
                    turn(b + 2, b)
                with pe.Fori(1, B // 2 - 1) as i:
                    for j in range(2):
                        gate(i * 2 + j, j)
                        turn(i * 2 + j + 2, j)
                gate(B - 2, 0)
                gate(B - 1, 1)

            @block.scalar
            def _(act):
                def batch(b, s):
                    act.wait_ge(t_done, b + 1)
                    wait(act, g_done, b - 1)
                    wait(act, kept, b - 1)
                    act.activation(tks[:, s, :], ps_t[:, s, 0:P], ACT.Copy, scale=norm_w[:, 0:1]).then_inc(tks_ready, 1)

                for b in range(2):
                    batch(b, b)
                with act.Fori(1, B // 2) as i:
                    for j in range(2):
                        batch(i * 2 + j, j)
                act.wait_ge(diff_ready, 1)
                act.activation(ex[:], diff[:], ACT.Exp).then_inc(ex_ready, 1)

        with ExitStack() as ph:
            def sb(name, shape, dt):
                return ph.enter_context(nc.sbuf_tensor(name, shape, dt))

            def sem(name):
                return ph.enter_context(nc.semaphore(name))

            hid = sb("hid", [P, 2 * M, GT], F32)
            c_g = sb("c_g", [P, G, E], F32)
            c_t = sb("c_t", [E, GT], F32)
            ps_h = ph.enter_context(nc.psum_tensor("ps_h", [P, 2, GT], F32))
            ps_y = ph.enter_context(nc.psum_tensor("ps_ym", [P, 2, GT], F32))
            ps_c = ph.enter_context(nc.psum_tensor("ps_c", [P, GT], F32))
            ps_b = ph.enter_context(nc.psum_tensor("ps_b", [P, GT], F32))
            h_done, h_ready, y_done, y_read = sem("h_done"), sem("h_ready"), sem("y_done_m"), sem("y_read")
            cg_ready, ct_done, ct_ready, b_done, b_read = (
                sem("cg_ready"), sem("ct_done"), sem("ct_ready"), sem("b_done"), sem("b_read"))
            st_ready = sem("st_ready_m")
            block = ph.enter_context(nc.Block())

            @block.tensor
            def _(pe):
                def hidden(g, e):
                    for m in range(M):
                        n = g * (E * M) + e * M + m
                        wait(pe, h_ready, n - 1)
                        pe.matmul(ps_h[:, m, :], w1[:, e, m * P:(m + 1) * P], tok_t[:, bass.ds(g * GT, GT)],
                                  start=True, stop=True).then_inc(h_done, 1)

                def out(g, e):
                    n = g * E + e
                    pe.wait_ge(h_ready, (n + 1) * M)
                    wait(pe, y_read, (n - 1) * G)
                    for j in range(G):
                        for m in range(M):
                            last = pe.matmul(ps_y[:, e % 2, j * D:(j + 1) * D],
                                             hid[:, (e % 2) * M + m, j * P:(j + 1) * P], w2[:, e, m, :],
                                             start=(m == 0), stop=(m == M - 1))
                    last.then_inc(y_done, 1)

                def bias(g):
                    pe.wait_ge(cg_ready, g + 1)
                    wait(pe, ct_ready, g)
                    for j in range(G):
                        last = pe.transpose(ps_c[0:E, j * P:(j + 1) * P], c_g[:, j, :], ident[:])
                    last.then_inc(ct_done, 1)
                    pe.wait_ge(ct_ready, g + 1)
                    wait(pe, b_read, g)
                    for j in range(G):
                        last = pe.matmul(ps_b[:, j * D:(j + 1) * D], c_t[:, j * P:(j + 1) * P], b2[:],
                                         start=True, stop=True)
                    last.then_inc(b_done, 1)

                def group(g):
                    hidden(g, 0)
                    for e in range(E):
                        if e + 1 < E:
                            hidden(g, e + 1)
                        if e == 0:
                            bias(g)
                        out(g, e)

                group(0)
                with pe.Fori(1, NG) as g:
                    group(g)

            @block.scalar
            def _(act):
                def group(g):
                    for e in range(E):
                        for m in range(M):
                            n = g * (E * M) + e * M + m
                            act.wait_ge(h_done, n + 1)
                            wait(act, y_done, g * E + e - 1)
                            act.activation(hid[:, (e % 2) * M + m, :], ps_h[:, m, :], ACT.Gelu,
                                           bias=b1[:, e * M + m:e * M + m + 1]).then_inc(h_ready, 1)
                        if e == 1:
                            act.wait_ge(ct_done, g + 1)
                            wait(act, b_done, g)
                            act.activation(c_t[:], ps_c[0:E, :], ACT.Copy).then_inc(ct_ready, 1)

                group(0)
                with act.Fori(1, NG) as g:
                    group(g)

            @block.vector
            def _(dve):
                def x_of(g, j):
                    return x_all[:, bass.ds(g * G + j, 1), :].rearrange("p b d -> p (b d)")

                def stats(g):
                    for j in range(G):
                        dve.bn_stats(st_all[:, bass.ds(g * G + j, 1), :].rearrange("p b n -> p (b n)"), x_of(g, j))\
                           .then_inc(st_ready, 1)

                def group(g, first=False):
                    wait(dve, y_read, g * E * G)
                    wait(dve, ct_done, g)
                    dve.tensor_copy(c_g[:], comb[:, bass.ds(g * G, G), :]).then_inc(cg_ready, 1)
                    if not first:
                        stats(g - 1)
                    dve.wait_ge(b_done, g + 1)
                    x_g = x_all[:, bass.ds(g * G, G), :]
                    dve.tensor_tensor(x_g, ps_b[:].rearrange("p (j d) -> p j d", j=G), x_g, ALU.add).then_inc(b_read, 1)
                    dve.wait_ge(b_read, g + 1)
                    for e in range(E):
                        n = g * E + e
                        dve.wait_ge(y_done, n + 1)
                        for j in range(G):
                            wait(dve, y_read, (n - 1) * G + j + 1)
                            dve.scalar_tensor_tensor(out=x_of(g, j), in0=ps_y[:, e % 2, j * D:(j + 1) * D],
                                                     scalar=c_g[:, j, e:e + 1], in1=x_of(g, j),
                                                     op0=ALU.mult, op1=ALU.add).then_inc(y_read, 1)

                group(0, first=True)
                with dve.Fori(1, NG) as g:
                    group(g)
                dve.wait_ge(y_read, NG * E * G)
                stats(NG - 1)


def ternary_ffn(nc, t, x_all, st_all, mean, vareps, rstd, half, identb, ffn_wq, w_scale):
    with ExitStack() as ph:
        def sb(name, shape, dt):
            return ph.enter_context(nc.sbuf_tensor(name, shape, dt))

        def sem(name):
            return ph.enter_context(nc.semaphore(name))

        tmp = sb("tmp_f", [P, B], F32)
        xh, amax, scl = sb("xh_f", [P, 2, D], F32), sb("amax", [P, 2, 2], F32), sb("scl", [P, 2, 8], F32)
        xr, xq, xq_t = sb("xr", [P, 2, D], F32), sb("xq", [P, 2, D], BF16), sb("xq_t", [P, 2, P], BF16)
        gate, gu = sb("gate", [P, 2, F], F32), sb("gu", [P, 2, F], F32)
        gr, gq, gq_t = sb("gr", [P, 2, F], F32), sb("gq", [P, 2, F], BF16), sb("gq_t", [P, 2, F], BF16)
        out = sb("x_out", [P, 2, D], F32)
        ps_t = ph.enter_context(nc.psum_tensor("ps_tf", [P, 2 * F], BF16))
        ps_x = ph.enter_context(nc.psum_tensor("ps_xf", [P, 2 * F], BF16))
        ps_g = ph.enter_context(nc.psum_tensor("ps_gf", [P, 2, F], F32))
        ps_u = ph.enter_context(nc.psum_tensor("ps_uf", [P, 2, F], F32))
        ps_d = ph.enter_context(nc.psum_tensor("ps_df", [P, 2, F], F32))
        var_ready, rstd_ready = sem("var_ready_f"), sem("rstd_ready_f")
        in_step, xr_ready, xq_ready, xt_done, xt_ready = (
            sem("in_step"), sem("xr_ready"), sem("xq_ready"), sem("xt_done_f"), sem("xt_ready_f"))
        gu_done, gate_ready, mid_step, gr_ready, gq_ready = (
            sem("gu_done"), sem("gate_ready"), sem("mid_step"), sem("gr_ready"), sem("gq_ready"))
        gt_done, gt_ready, d_done, out_ready = sem("gt_done"), sem("gt_ready"), sem("d_done"), sem("out_ready")
        stored = [sem(f"stored_f{s}") for s in range(2)]
        block = ph.enter_context(nc.Block())

        @block.gpsimd
        def _(pool):
            pool.wait_ge(var_ready, STAT_STEPS)
            pool.tensor_tensor(rstd[:], vareps[:], half[:], ALU.pow).then_inc(rstd_ready, 1)

        def pipeline(eng, head, mid, tail):
            def step(b, s):
                if exists(b):
                    head(b, s)
                if exists(b - 1):
                    mid(b - 1, 1 - s)
                if exists(b - 2):
                    tail(b - 2, s)

            for b in range(4):
                step(b, b % 2)
            with eng.Fori(2, B // 2) as i:
                for j in range(2):
                    step(i * 2 + j, j)
            for b in range(B, B + 2):
                step(b, b % 2)

        IN, MID = 5, 6

        @block.vector
        def _(dve):
            mean_and_variance(dve, var_ready, st_all, mean, vareps, tmp)
            dve.wait_ge(rstd_ready, 1)

            def head(b, s):
                c = Chain(dve, in_step, b * IN)
                c.step(dve.tensor_scalar(xh[:, s, :], x_all[:, bass.ds(b, 1), :].rearrange("p b d -> p (b d)"),
                                         mean[:, bass.ds(b, 1)], rstd[:, bass.ds(b, 1)], ALU.subtract, ALU.mult))
                c.settle()
                c.step(dve.tensor_reduce(amax[:, s, 0:1], xh[:, s, :], AX_X, ALU.max, apply_absolute_value=True))
                c.settle()
                wait(dve, gate_ready, b - 1)
                c.step(dve.tensor_scalar(scl[:, s, 0:1], amax[:, s, 0:1], 1e-5, 1.0 / 127.0, ALU.max, ALU.mult))
                c.settle()
                c.step(dve.reciprocal(scl[:, s, 1:2], scl[:, s, 0:1]))
                c.step(dve.tensor_scalar(scl[:, s, 2:4], w_scale[:, 0:2], scl[:, s, 0:1], None, ALU.mult))
                c.settle()
                assert c.n == IN
                wait(dve, xq_ready, b - 1)
                dve.tensor_scalar(xr[:, s, :], xh[:, s, :], scl[:, s, 1:2], 127.0, ALU.mult, ALU.min)\
                   .then_inc(xr_ready, 1)
                dve.wait_ge(xr_ready, 2 * b + 1)
                dve.tensor_scalar(xr[:, s, :], xr[:, s, :], -128.0, MAGIC, ALU.max, ALU.add).then_inc(xr_ready, 1)

            def mid(b, s):
                c = Chain(dve, mid_step, b * MID)
                dve.wait_ge(gate_ready, b + 1)
                c.step(dve.scalar_tensor_tensor(out=gu[:, s, :], in0=ps_u[:, s, :], scalar=scl[:, s, 3:4],
                                                in1=gate[:, s, :], op0=ALU.mult, op1=ALU.mult))
                c.settle()
                c.step(dve.tensor_reduce(amax[:, s, 1:2], gu[:, s, :], AX_X, ALU.max, apply_absolute_value=True))
                c.settle()
                c.step(dve.tensor_scalar(scl[:, s, 4:5], amax[:, s, 1:2], 1e-5, 1.0 / 127.0, ALU.max, ALU.mult))
                c.settle()
                c.step(dve.reciprocal(scl[:, s, 5:6], scl[:, s, 4:5]))
                c.step(dve.tensor_scalar(scl[:, s, 6:7], w_scale[:, 2:3], scl[:, s, 4:5], None, ALU.mult))
                c.settle()
                wait(dve, gq_ready, b - 1)
                c.step(dve.tensor_scalar(gr[:, s, :], gu[:, s, :], scl[:, s, 5:6], 127.0, ALU.mult, ALU.min))
                c.settle()
                assert c.n == MID
                dve.tensor_scalar(gr[:, s, :], gr[:, s, :], -128.0, MAGIC, ALU.max, ALU.add).then_inc(gr_ready, 1)

            def tail(b, s):
                dve.wait_ge(d_done, b + 1)
                wait(dve, stored[s], of_slot(b - 2, s, 16))
                dve.scalar_tensor_tensor(out=out[:, s, :], in0=ps_d[:, s, 0:D], scalar=scl[:, s, 6:7],
                                         in1=x_all[:, bass.ds(b, 1), :].rearrange("p b d -> p (b d)"),
                                         op0=ALU.mult, op1=ALU.add).then_inc(out_ready, 1)

            pipeline(dve, head, mid, tail)

        @block.scalar
        def _(act):
            def head(b, s):
                act.wait_ge(xr_ready, 2 * b + 2)
                wait(act, xt_done, b - 1)
                act.activation(xq[:, s, :], xr[:, s, :], ACT.Copy, bias=-MAGIC).then_inc(xq_ready, 1)
                act.wait_ge(xt_done, b + 1)
                wait(act, gu_done, b - 1)
                act.activation(xq_t[:, s, :], ps_x[:, 0:P], ACT.Copy).then_inc(xt_ready, 1)

            def mid(b, s):
                act.wait_ge(gu_done, b + 1)
                wait(act, mid_step, (b - 2) * MID + 1)
                act.activation(gate[:, s, :], ps_g[:, s, :], ACT.Silu, scale=scl[:, s, 2:3]).then_inc(gate_ready, 1)
                act.wait_ge(gr_ready, b + 1)
                wait(act, gt_done, b - 1)
                act.activation(gq[:, s, :], gr[:, s, :], ACT.Copy, bias=-MAGIC).then_inc(gq_ready, 1)

            def tail(b, s):
                act.wait_ge(gt_done, b + 1)
                wait(act, d_done, b - 1)
                act.activation(gq_t[:, s, :], ps_t[:, 0:F], ACT.Copy).then_inc(gt_ready, 1)

            pipeline(act, head, mid, tail)

        @block.tensor
        def _(pe):
            def head(b, s):
                pe.wait_ge(xq_ready, b + 1)
                wait(pe, xt_ready, b)
                pe.transpose(ps_x[:, 0:P], xq[:, s, :], identb[:]).then_inc(xt_done, 1)
                pe.wait_ge(xt_ready, b + 1)
                wait(pe, mid_step, (b - 2) * MID + 1)
                pe.matmul(ps_g[:, s, :], xq_t[:, s, :], ffn_wq[:, 0, :], start=True, stop=True)
                pe.matmul(ps_u[:, s, :], xq_t[:, s, :], ffn_wq[:, 1, :], start=True, stop=True).then_inc(gu_done, 1)

            def mid(b, s):
                pe.wait_ge(gq_ready, b + 1)
                wait(pe, gt_ready, b)
                for k in range(FK):
                    last = pe.transpose(ps_t[:, k * P:(k + 1) * P], gq[:, s, k * P:(k + 1) * P], identb[:])
                last.then_inc(gt_done, 1)

            def tail(b, s):
                pe.wait_ge(gt_ready, b + 1)
                wait(pe, out_ready, b - 1)
                for k in range(FK):
                    last = pe.matmul(ps_d[:, s, 0:D], gq_t[:, s, k * P:(k + 1) * P], ffn_wq[:, 2, k * D:(k + 1) * D],
                                     start=(k == 0), stop=(k == FK - 1))
                last.then_inc(d_done, 1)

            pipeline(pe, head, mid, tail)

        @block.sync
        def _(sp):
            def store(b, s):
                sp.wait_ge(out_ready, b + 1)
                sp.dma_start(t["out"][bass.ds(b, 1)].rearrange("b s d -> (b s) d"), out[:, s, :]).then_inc(stored[s], 16)

            with sp.Fori(0, B // 2) as i:
                for j in range(2):
                    store(i * 2 + j, j)
            for s in range(2):
                sp.wait_ge(stored[s], of_slot(B - 2 + s, s, 16))


def kernel(x, ctx_1024, mask_BxS2_if1, L0_xattn_Wq, L0_xattn_bq, L0_xattn_Wk, L0_xattn_bk, L0_xattn_Wv,
           L0_xattn_bv, L0_xattn_Wo, L0_xattn_bo, L0_ffn_norm_weight, L0_ffn_gate_w, L0_ffn_w1, L0_ffn_b1,
           L0_ffn_w2, L0_ffn_b2, L1_xattn_Wq, L1_xattn_Wk, L1_xattn_Wv, L1_xattn_Wo, L1_ffn_w_gate,
           L1_ffn_w_up, L1_ffn_w_down):
    import numpy as np
    import concourse.bacc as bacc
    from concourse import mybir as mb
    from concourse.bass_utils import run_bass_kernel_spmd

    a = {
        "x": x,
        "ctx_t": np.transpose(ctx_1024, (2, 0, 1)).reshape(D, T),
        "mask": mask_BxS2_if1,
        "L0_Wq": np.transpose(L0_xattn_Wq), "L0_Wk": np.transpose(L0_xattn_Wk),
        "L0_Wv": np.transpose(L0_xattn_Wv), "L0_Wo": np.transpose(L0_xattn_Wo),
        "L1_Wq": L1_xattn_Wq, "L1_Wk": L1_xattn_Wk, "L1_Wv": L1_xattn_Wv, "L1_Wo": L1_xattn_Wo,
        "bq": np.reshape(L0_xattn_bq, (D, 1)), "bk": np.reshape(L0_xattn_bk, (D, 1)),
        "bv": np.reshape(L0_xattn_bv, (1, D)), "bo": np.reshape(L0_xattn_bo, (1, D)),
        "norm_w": np.reshape(L0_ffn_norm_weight, (D, 1)),
        "gate_w": np.transpose(L0_ffn_gate_w),
        "w1": np.transpose(L0_ffn_w1, (2, 0, 1)),
        "b1": np.transpose(np.reshape(L0_ffn_b1, (E * M, P))),
        "w2": np.transpose(np.reshape(L0_ffn_w2, (E, D, M, P)), (3, 0, 2, 1)),
        "b2": L0_ffn_b2,
        "w_gate": np.transpose(L1_ffn_w_gate), "w_up": np.transpose(L1_ffn_w_up),
        "w_down": np.transpose(np.reshape(L1_ffn_w_down, (D, FK, P)), (2, 1, 0)),
    }
    nc = bacc.Bacc("TRN2", target_bir_lowering=False, num_devices=1)
    arrays, t = {}, {}
    for name, value in a.items():
        value = np.ascontiguousarray(value)
        arrays[f"in_{name}"] = value
        t[name] = nc.dram_tensor(f"in_{name}", value.shape, mb.dt.from_np(value.dtype), kind="ExternalInput").ap()
    t["out"] = nc.dram_tensor("out", (B, P, D), mb.dt.float32, kind="ExternalOutput").ap()
    main_kernel(nc, t)
    return run_bass_kernel_spmd(nc, [arrays], core_ids=[0]).results[0]["out"]
```

```python
from contextlib import ExitStack

import concourse.bass as bass
from concourse import mybir

ALU = mybir.AluOpType
ACT = mybir.ActivationFunctionType
AX_X = mybir.AxisListType.X
F32 = mybir.dt.float32
BF16 = mybir.dt.bfloat16
I32 = mybir.dt.int32
U32 = mybir.dt.uint32

P = 128
B = 16
T = B * P
D = 128
H = 16
DK = D // H
HQ = 4
NQ = H // HQ
G = 4
NG = B // G
GT = G * P
E = 8
HID = 256
M = HID // P
F = 512
FK = F // P
EPS_LN = 1e-5
EPS_RMS = 1e-6
SCALE = 1.0 / DK ** 0.5
MASKED = -1e30
MAGIC = 1.5 * 2.0 ** 23

PARTS = 3
PRODUCTS = PARTS * PARTS * DK
ROW_MAX = 96
ROW_MASK = ROW_MAX + PARTS
K_PARTS = 5
SLOTS = 4
STAT_STEPS = 7


def wait(eng, sem, value):
    if isinstance(value, int) and value <= 0:
        return
    eng.wait_ge(sem, value)


def exists(b):
    return not isinstance(b, int) or 0 <= b < B


def of_slot(b, r, slots, each):
    return (b - r) * (each // slots) + each


def batch_of(x_all, b):
    return x_all[:, bass.ds(b, 1), :].rearrange("p b d -> p (b d)")


class Chain:

    def __init__(self, eng, sem, base):
        self.eng, self.sem, self.base, self.n = eng, sem, base, 0

    def step(self, ins):
        self.n += 1
        ins.then_inc(self.sem, 1)

    def settle(self):
        wait(self.eng, self.sem, self.base + self.n)


def mean_and_variance(dve, sem, base, st, mean, vareps, tmp):
    c = Chain(dve, sem, base)
    c.step(dve.tensor_tensor(mean, st[:, :, 1], st[:, :, 4], ALU.add))
    c.step(dve.tensor_tensor(tmp, st[:, :, 1], st[:, :, 4], ALU.subtract))
    c.step(dve.tensor_tensor(vareps, st[:, :, 2], st[:, :, 5], ALU.add))
    c.settle()
    c.step(dve.tensor_scalar(mean, mean, 0.5, None, ALU.mult))
    c.step(dve.tensor_tensor(tmp, tmp, tmp, ALU.mult))
    c.step(dve.tensor_scalar(vareps, vareps, 1.0 / D, EPS_LN, ALU.mult, ALU.add))
    c.settle()
    c.step(dve.scalar_tensor_tensor(out=vareps, in0=tmp, scalar=0.25, in1=vareps, op0=ALU.mult, op1=ALU.add))
    assert c.n == STAT_STEPS


def load_rows(sp, c, layer, b, r):
    k_rows, q_rows, rows_in = c["k_rows"], c["q_rows"], c["rows_in"][layer]
    rows = c["k_dram"][layer, bass.ds(b, 1)]
    windows = bass.AP(tensor=rows.tensor, offset=rows.offset,
                      ap=[[DK * H * P, PARTS], [H * P, PARTS * DK], [1, H * P]])
    sp.dma_start(k_rows[0:PRODUCTS, r].rearrange("p h t -> p (h t)"), windows).then_inc(rows_in[r], 16)
    sp.dma_start(q_rows[0:PRODUCTS, r].rearrange("p h t -> p (h t)"),
                 c["q_dram"][layer, bass.ds(b, 1)].rearrange("b r (d h) s -> b (r d) (h s)", h=H)
                 .to_broadcast([PARTS, PARTS * DK, H * P])).then_inc(rows_in[r], 16)
    if layer == 1:
        sp.dma_start(k_rows[ROW_MASK:ROW_MASK + 1, r],
                     c["mask_dram"][bass.ds(b, 1)].unsqueeze(1).to_broadcast([1, H, P])).then_inc(rows_in[r], 16)


def store_parts(sp, dram, b, parts, n_stored, sem):
    for r in range(n_stored):
        sp.dma_start(dram[bass.ds(b, G), r].rearrange("b p s -> p b s"), parts[:, r % PARTS, :]).then_inc(sem, 16)


def main_kernel(nc, t):
    with ExitStack() as ctx:
        def sb(name, shape, dt):
            return ctx.enter_context(nc.sbuf_tensor(name, shape, dt))

        c = {
            "x": sb("x_all", [P, B, D], F32), "st": sb("st_all", [P, B, 6], F32),
            "mean": sb("mean", [P, B], F32), "vareps": sb("vareps", [P, 2 * B], F32),
            "rstd": sb("rstd", [P, 2 * B], F32), "half": sb("half", [P, 2 * B], F32),
            "ident": sb("ident", [P, P], F32), "identb": sb("identb", [P, P], BF16),
            "ones": sb("ones", [P, P], F32),
            "upper": sb("upper", [P, P], BF16),
            "lower": sb("lower", [P, P], BF16),
            "attn_w": sb("attn_w", [P, 2, 4, D], F32),
            "attn_bias": sb("attn_bias", [P, 2], F32),
            "row_bias": sb("row_bias", [P, 2, D], F32),
            "v": sb("v_all", [P, 2, B, D], F32),
            "k_rows": sb("k_rows", [P, SLOTS, H, P], BF16), "q_rows": sb("q_rows", [P, SLOTS, H, P], BF16),
            "ffn_wq": sb("ffn_wq", [P, 3, F], BF16),
            "w_scale": sb("w_scale", [P, 3], F32),
            "zero": sb("zero", [P, 1], I32),
            "ctx_t": sb("ctx_t", [P, T], F32),
            "w1": sb("w1", [P, E, HID], F32), "w2": sb("w2", [P, E, M, D], F32), "ffn_w": sb("ffn_w", [P, 3, F], F32),
            "gate_w": sb("gate_w", [P, E], F32), "norm_w": sb("norm_w", [P, 1], F32),
            "b1": sb("b1", [P, E * M], F32), "b2": sb("b2", [E, D], F32),
            "parts_stored": ctx.enter_context(nc.semaphore("parts_stored")),
            "rows_in": [[ctx.enter_context(nc.semaphore(f"rows_in{layer}_{r}")) for r in range(SLOTS)]
                        for layer in range(2)],
            "k_dram": nc.dram_tensor("k_dram", (2, B, K_PARTS, P, P), BF16).ap(),
            "q_dram": nc.dram_tensor("q_dram", (2, B, PARTS, P, P), BF16).ap(),
            "mask_dram": nc.dram_tensor("mask_dram", (B, P), BF16).ap(),
        }
        context(nc, t, c)
        attention(nc, t, c, 0)
        experts(nc, t, c)
        attention(nc, t, c, 1)
        ternary_ffn(nc, t, c)


def context(nc, t, c):
    x_all, ident, identb, upper = c["x"], c["ident"], c["identb"], c["upper"]
    attn_w, k_rows, q_rows, ctx_t, mean, rstd = (c["attn_w"], c["k_rows"], c["q_rows"], c["ctx_t"], c["mean"], c["rstd"])
    units = [("k", 0), ("k", 1), ("q", 0), ("k", 2), ("q", 1), ("k", 3), ("q", 2), ("q", 3)]
    with ExitStack() as ph:
        def sb(name, shape, dt):
            return ph.enter_context(nc.sbuf_tensor(name, shape, dt))

        def sem(name):
            return ph.enter_context(nc.semaphore(name))

        N = len(units)
        xn, xn_t = sb("xn", [P, B, D], F32), sb("xn_t", [P, NG, GT], F32)
        full = sb("full", [P, N, GT], F32)
        rest = sb("rest", [P, N, GT], F32)
        parts = sb("parts", [P, N, PARTS, GT], BF16)
        mask_i, mask_b = sb("mask_i", [B, P], I32), sb("mask_b", [B, P], BF16)
        one_rows = sb("one_rows", [H, SLOTS * P], BF16)
        tmp = sb("tmp", [P, B], F32)
        ps_p = ph.enter_context(nc.psum_tensor("ps_p", [P, 2, GT], F32))
        ps_x = ph.enter_context(nc.psum_tensor("ps_x", [P, 2, GT], F32))
        ps_v = ph.enter_context(nc.psum_tensor("ps_v", [P, 2, GT], F32))
        w_in = {m: sem(f"w{m}_in") for m in (0, 1, 2)}
        x_in, late_in, mask_in, bias_in, row_in = sem("x_in"), sem("late_in"), sem("mask_in"), sem("bias_in"), sem("row_in")
        ctx_in = [sem(f"ctx_in{g}") for g in range(NG)]
        made, consts, ones_ready, rows_clear, rows_set = (
            sem("made"), sem("consts"), sem("ones_ready"), sem("rows_clear"), sem("rows_set"))
        stats_ready, stats_step, mask_ready, mask_out = (
            sem("stats_ready"), sem("stats_step"), sem("mask_ready"), sem("mask_out"))
        xn_ready, t_done, xt_ready = sem("xn_ready"), sem("t_done"), sem("xt_ready")
        p_done, v_done, copied, rest_ready, split_step, v_ready = (
            sem("p_done"), sem("v_done"), sem("copied"), sem("rest_ready"), sem("split_step"), sem("v_ready"))
        first_stored, stored = sem("first_stored"), c["parts_stored"]
        block = ph.enter_context(nc.Block())

        @block.sync
        def _(sp):
            def load_ctx(g):
                sp.dma_start(ctx_t[:, g * GT:(g + 1) * GT], t["ctx_t"][:, g * GT:(g + 1) * GT]).then_inc(ctx_in[g], 16)

            def load_w(layer, m, signal):
                sp.dma_start(attn_w[:, layer, m, :], t[f"L{layer}_" + ("Wq", "Wk", "Wv", "Wo")[m]]).then_inc(signal, 16)

            load_w(0, 1, w_in[1])
            load_ctx(0)
            sp.dma_start(x_all[:], t["x"].rearrange("b s d -> s b d")).then_inc(x_in, 16)
            sp.dma_start(c["attn_bias"][:, 0:1], t["bq"]).then_inc(bias_in, 16)
            sp.dma_start(c["attn_bias"][:, 1:2], t["bk"]).then_inc(bias_in, 16)
            load_w(0, 2, w_in[2])
            load_ctx(1)
            for n, row in enumerate(("bv", "bo")):
                sp.dma_start(c["row_bias"][:, n, :], t[row].to_broadcast([P, D])).then_inc(row_in, 16)
            load_w(0, 0, w_in[0])
            load_ctx(2)
            load_ctx(3)
            sp.dma_start(mask_i[:], t["mask"]).then_inc(mask_in, 16)
            for layer, m in ((0, 3), (1, 0), (1, 1), (1, 2), (1, 3)):
                load_w(layer, m, late_in)
            for n, (kind, g) in enumerate(units):
                sp.wait_ge(split_step, 2 * (n + 1))
                store_parts(sp, c[kind + "_dram"][0], g * G, parts[:, n], K_PARTS if kind == "k" else PARTS,
                            first_stored if g == 0 else stored)
                if n == units.index(("q", 0)):
                    sp.wait_ge(ones_ready, 1)
                    sp.wait_ge(rows_clear, 3)
                    for r in range(PARTS):
                        sp.dma_start(k_rows[ROW_MAX + r:ROW_MAX + r + 1], one_rows[:]).then_inc(rows_set, 16)
                    sp.dma_start(q_rows[ROW_MASK:ROW_MASK + 1], one_rows[:]).then_inc(rows_set, 16)
                    sp.wait_ge(first_stored, 16 * (K_PARTS + PARTS))
                    for b in range(SLOTS):
                        load_rows(sp, c, 0, b, b)
            sp.wait_ge(mask_ready, 1)
            sp.dma_start(c["mask_dram"], mask_b[:]).then_inc(mask_out, 16)
            sp.wait_ge(rows_set, 16 * (PARTS + 1))
            sp.wait_ge(mask_out, 16)
            sp.wait_ge(late_in, 16 * 5)

        @block.gpsimd
        def _(pool):
            pool.memset(ident[:], 0.0).then_inc(made, 1)
            pool.memset(identb[:], 0.0).then_inc(made, 1)
            pool.memset(upper[:], 0.0).then_inc(made, 1)
            pool.memset(c["lower"][:], 0.0).then_inc(made, 1)
            pool.memset(c["half"][:], -0.5).then_inc(consts, 1)
            pool.memset(c["ones"][:], 1.0).then_inc(consts, 1)
            pool.memset(c["zero"][:], 0).then_inc(consts, 1)
            pool.wait_ge(made, 4)
            for tile in (ident, identb):
                pool.affine_select(out=tile[:], in_=tile[:], compare_op=ALU.not_equal, fill=1.0, base=0,
                                   pattern=[[-1, P]], channel_multiplier=1).then_inc(consts, 1)
            pool.affine_select(out=upper[:], in_=upper[:], compare_op=ALU.is_ge, fill=MASKED, base=0,
                               pattern=[[-1, P]], channel_multiplier=1).then_inc(consts, 1)
            pool.affine_select(out=c["lower"][:], in_=c["lower"][:], compare_op=ALU.is_ge, fill=MASKED, base=0,
                               pattern=[[1, P]], channel_multiplier=-1).then_inc(consts, 1)
            pool.memset(one_rows[:], 1.0).then_inc(ones_ready, 1)
            pool.memset(q_rows[:, 0:2].rearrange("p s h t -> p (s h t)").bitcast(U32), 0).then_inc(rows_clear, 1)
            pool.wait_ge(consts, 7)
            for n in range(N):
                for g in {1: (0, 1), 2: (2, 3)}.get(n, ()):
                    pool.wait_ge(stats_step, STAT_STEPS)
                    cols = slice(g * G, (g + 1) * G)
                    pool.tensor_tensor(rstd[:, cols], c["vareps"][:, cols], c["half"][:, cols], ALU.pow)\
                        .then_inc(stats_step, 1)
                pool.wait_ge(copied, 2 * (n + 1))
                pool.tensor_tensor(rest[:, n], full[:, n], parts[:, n, 0], ALU.subtract).then_inc(rest_ready, 1)

        @block.vector
        def _(dve):
            dve.memset(k_rows[:].rearrange("p s h t -> p (s h t)").bitcast(U32), 0).then_inc(rows_clear, 1)
            dve.memset(q_rows[:, 2:SLOTS].rearrange("p s h t -> p (s h t)").bitcast(U32), 0).then_inc(rows_clear, 1)
            dve.wait_ge(x_in, 16)
            for b in range(B):
                dve.bn_stats(c["st"][:, b, :], x_all[:, b, :]).then_inc(stats_ready, 1)
            dve.wait_ge(stats_ready, B)
            mean_and_variance(dve, stats_step, 0, c["st"], mean[:], c["vareps"][:, 0:B], tmp[:])

            def values(g):
                dve.wait_ge(v_done, g + 1)
                dve.wait_ge(row_in, 32)
                dve.tensor_tensor(c["v"][:, 0, g * G:(g + 1) * G, :], ps_v[:, g % 2, :].rearrange("p (b d) -> p b d", b=G),
                                  c["row_bias"][:, 0, :].unsqueeze(1).to_broadcast([P, G, D]), ALU.add)\
                   .then_inc(v_ready, 1)

            def normalise(g):
                dve.wait_ge(stats_step, STAT_STEPS + g + 1)
                for b in range(g * G, (g + 1) * G):
                    dve.tensor_scalar(xn[:, b, :], x_all[:, b, :], mean[:, b:b + 1], rstd[:, b:b + 1],
                                      ALU.subtract, ALU.mult).then_inc(xn_ready, 1)

            def split(n):
                dve.wait_ge(rest_ready, n + 1)
                dve.tensor_copy(parts[:, n, 1], rest[:, n]).then_inc(split_step, 1)
                dve.wait_ge(split_step, 2 * n + 1)
                dve.tensor_tensor(parts[:, n, 2], rest[:, n], parts[:, n, 1], ALU.subtract).then_inc(split_step, 1)

            values(0)
            split(0)
            normalise(0)
            normalise(1)
            values(1)
            split(1)
            normalise(2)
            split(2)
            values(2)
            normalise(3)
            split(3)
            split(4)
            values(3)
            split(5)
            split(6)
            dve.wait_ge(mask_in, 16)
            dve.tensor_scalar(mask_b[:], mask_i[:], 0, MASKED, ALU.is_equal, ALU.mult).then_inc(mask_ready, 1)
            split(7)

        @block.tensor
        def _(pe):
            def turn(g):
                pe.wait_ge(xn_ready, (g + 1) * G)
                wait(pe, xt_ready, g - 1)
                for j in range(G):
                    last = pe.transpose(ps_x[:, g % 2, j * P:(j + 1) * P], xn[:, g * G + j, :], ident[:])
                last.then_inc(t_done, 1)

            def values(g):
                wait(pe, v_ready, g - 1)
                for j in range(G):
                    last = pe.matmul(ps_v[:, g % 2, j * D:(j + 1) * D], ctx_t[:, (g * G + j) * P:(g * G + j + 1) * P],
                                     attn_w[:, 0, 2, :], start=True, stop=True)
                last.then_inc(v_done, 1)

            for n, (kind, g) in enumerate(units):
                wait(pe, copied, 2 * (n - 1))
                if kind == "k":
                    if g == 0:
                        pe.wait_ge(w_in[1], 16)
                    pe.wait_ge(ctx_in[g], 16)
                    pe.matmul(ps_p[:, n % 2, :], attn_w[:, 0, 1, :], ctx_t[:, g * GT:(g + 1) * GT],
                              start=True, stop=True).then_inc(p_done, 1)
                    if g == 0:
                        pe.wait_ge(w_in[2], 16)
                    values(g)
                else:
                    if g == 0:
                        pe.wait_ge(consts, 7)
                        turn(0)
                        pe.wait_ge(w_in[0], 16)
                    if g + 1 < NG:
                        turn(g + 1)
                    pe.wait_ge(xt_ready, g + 1)
                    pe.matmul(ps_p[:, n % 2, :], attn_w[:, 0, 0, :], xn_t[:, g, :],
                              start=True, stop=True).then_inc(p_done, 1)

        @block.scalar
        def _(act):
            act.wait_ge(bias_in, 32)

            def copy_turned(g):
                act.wait_ge(t_done, g + 1)
                act.activation(xn_t[:, g, :], ps_x[:, g % 2, :], ACT.Copy).then_inc(xt_ready, 1)

            for n, (kind, g) in enumerate(units):
                if kind == "q":
                    if g == 0:
                        copy_turned(0)
                    if g + 1 < NG:
                        copy_turned(g + 1)
                act.wait_ge(p_done, n + 1)
                bias = c["attn_bias"][:, 1:2] if kind == "k" else c["attn_bias"][:, 0:1]
                act.activation(parts[:, n, 0], ps_p[:, n % 2, :], ACT.Identity, bias=bias).then_inc(copied, 1)
                act.activation(full[:, n], ps_p[:, n % 2, :], ACT.Identity, bias=bias).then_inc(copied, 1)


def attention(nc, t, c, layer):
    x_all, ident, identb, attn_w = c["x"], c["ident"], c["identb"], c["attn_w"]
    k_rows, q_rows, rows_in = c["k_rows"], c["q_rows"], c["rows_in"][layer]
    with ExitStack() as ph:
        def sb(name, shape, dt):
            return ph.enter_context(nc.sbuf_tensor(f"{name}{layer}", shape, dt))

        def psum(name, shape, dt):
            return ph.enter_context(nc.psum_tensor(f"{name}{layer}", shape, dt))

        def sem(name):
            return ph.enter_context(nc.semaphore(f"{name}{layer}"))

        W = HQ * P
        VW = 32
        neg = sb("neg", [P, 2, H], F32)
        neg_rest = sb("neg_rest", [P, 2, H], F32)
        neg_parts = sb("neg_parts", [P, 2, P], BF16)
        neg_t = sb("neg_t", [PARTS * H, 2, P], BF16)
        probs = sb("probs", [P, NQ, W], F32)
        v_aug = sb("v_aug", [P, 2, H, VW], F32)
        o_t = sb("o_t", [P, 2, W], F32)
        inv = sb("inv", [P, 2, H], F32)
        o = sb("o", [P, 2, D], F32)
        oo_t = sb("oo_t", [P, 2, P], F32)
        ps_s = psum("ps_s", [P, 2, W], F32)
        ps_e = psum("ps_e", [P, 2, W], F32)
        ps_v = psum("ps_pv", [P, W], F32)
        ps_o = psum("ps_o", [P, W], F32)
        ps_n = psum("ps_n", [P, 2 * W], BF16)
        ps_y = psum("ps_y", [P, W], F32)

        bias_added, weights_in = sem("bias_added"), sem("weights_in")
        scored, max_done, neg_step, neg_ready = sem("scored"), sem("max_done"), sem("neg_step"), sem("neg_ready")
        negt_done, negt_ready = sem("negt_done"), sem("negt_ready")
        neg_laid = [sem(f"neg_laid{r}_") for r in range(SLOTS)]
        shifted, exp_done, pv_done, vaug_ready = (
            sem("shifted"), sem("exp_done"), sem("pv_done"), sem("vaug_ready"))
        ot_ready, ot_back, o_step = sem("ot_ready"), sem("ot_back"), sem("o_step")
        oot_done, oot_ready, y_done, x_ready = sem("oot_done"), sem("oot_ready"), sem("y_done"), sem("x_ready")
        st_ready, cleared, row_clear = sem("st_ready"), sem("cleared"), sem("row_clear")
        n_loads = 2 if layer == 0 else 3
        block = ph.enter_context(nc.Block())

        def run(eng, step, before_loop=None):
            for b in range(-2, 2):
                step(b, b % SLOTS)
            if before_loop:
                before_loop()
            with eng.Fori(0, (B - 4) // SLOTS) as i:
                for j in range(SLOTS):
                    step(i * SLOTS + (2 + j), (2 + j) % SLOTS)
            for b in range(B - 2, B + 2):
                step(b, b % SLOTS)

        @block.sync
        def _(sp):
            def lay_maxima(b, r):
                wait(sp, negt_ready, b + 1)
                sp.dma_start(q_rows[ROW_MAX:ROW_MASK, r], neg_t[:, r % 2, :]).then_inc(neg_laid[r], 16)

            if layer == 0:
                for key in ("gate_w", "norm_w", "b1", "b2", "w1", "w2"):
                    sp.dma_start(c[key][:], t[key]).then_inc(weights_in, 16)
                for n, key in enumerate(("w_gate", "w_up")):
                    sp.dma_start(c["ffn_w"][:, n, :], t[key]).then_inc(weights_in, 16)
                sp.dma_start(c["ffn_w"][:, 2, :].rearrange("p (k o) -> p k o", k=FK), t["w_down"]).then_inc(weights_in, 16)
            for b in range(2):
                lay_maxima(b, b)
            if layer == 0:
                sp.wait_ge(c["parts_stored"], 16 * (K_PARTS + PARTS) * (NG - 1))
            with sp.Fori(1, B // SLOTS) as i:
                for r in range(SLOTS):
                    b = i * SLOTS + r
                    sp.wait_ge(shifted, (b - SLOTS + 1) * NQ)
                    load_rows(sp, c, layer, b, r)
                    lay_maxima(b - 2, (r - 2) % SLOTS)
            for b in range(B - 2, B):
                lay_maxima(b, b % SLOTS)
            if layer == 0:
                sp.wait_ge(weights_in, 16 * 9)

        @block.tensor
        def _(pe):
            def scores(b, q, r):
                n = b * NQ + q
                if q == 0:
                    wait(pe, rows_in[r], of_slot(b, r, SLOTS, 16 * n_loads))
                    wait(pe, row_clear, b - SLOTS + 1)
                wait(pe, max_done, n - 1)
                if layer == 1:
                    pe.matmul(ps_s[:, q % 2, :], identb[:], c["upper"][:].unsqueeze(1).to_broadcast([P, HQ, P]),
                              start=True, stop=False, skip_group_check=True)
                for j in range(HQ):
                    h = q * HQ + j
                    last = pe.matmul(ps_s[:, q % 2, j * P:(j + 1) * P], q_rows[:, r, h, :], k_rows[:, r, h, :],
                                     start=(layer == 0), stop=True, skip_group_check=True)
                last.then_inc(scored, 1)

            def shifted_scores(b, q, r):
                n = b * NQ + q
                if q == 0:
                    wait(pe, neg_laid[r], of_slot(b, r, SLOTS, 16))
                wait(pe, exp_done, n - 1)
                if layer == 1:
                    pe.matmul(ps_e[:, q % 2, :], identb[:], c["lower"][:].unsqueeze(1).to_broadcast([P, HQ, P]),
                              start=True, stop=False, skip_group_check=True)
                for j in range(HQ):
                    h = q * HQ + j
                    last = pe.matmul(ps_e[:, q % 2, j * P:(j + 1) * P], k_rows[:, r, h, :], q_rows[:, r, h, :],
                                     start=(layer == 0), stop=True, skip_group_check=True)
                last.then_inc(shifted, 1)

            def values(b, q, s):
                n = b * NQ + q
                if q == 0:
                    wait(pe, vaug_ready, b + 1)
                    wait(pe, ot_ready, b)
                wait(pe, exp_done, n + 1)
                for j in range(HQ):
                    last = pe.matmul(ps_v[VW * j:VW * (j + 1), q * P:(q + 1) * P], v_aug[:, s, q * HQ + j, :],
                                     probs[:, q, j * P:(j + 1) * P], start=True, stop=True)
                last.then_inc(pv_done, 1)

            def turn_maxima(b, s):
                wait(pe, neg_ready, b + 1)
                wait(pe, negt_ready, b)
                pe.transpose(ps_n[:, 0:P], neg_parts[:, s, :], identb[:]).then_inc(negt_done, 1)

            def turn_back(b, s):
                wait(pe, ot_ready, b + 1)
                wait(pe, o_step, 2 * b)
                for q in range(NQ):
                    last = pe.transpose(ps_o[:, q * P:(q + 1) * P], o_t[:, s, q * P:(q + 1) * P], ident[:])
                last.then_inc(ot_back, 1)

            def turn_output(b, s):
                wait(pe, o_step, 2 * b + 2)
                wait(pe, x_ready, b)
                pe.transpose(ps_y[:, 0:P], o[:, s, :], ident[:]).then_inc(oot_done, 1)

            def project(b, s):
                wait(pe, oot_ready, b + 1)
                pe.matmul(ps_y[:, P:2 * P], oo_t[:, s, :], attn_w[:, layer, 3, :], start=True, stop=True)\
                  .then_inc(y_done, 1)

            def step(b, r):
                s = r % 2
                for q in range(NQ):
                    if exists(b + 2):
                        scores(b + 2, q, (r + 2) % SLOTS)
                    if exists(b):
                        shifted_scores(b, q, r)
                    if q == 1 and exists(b - 2):
                        turn_output(b - 2, s)
                    if q == 0 and exists(b - 1):
                        values(b - 1, NQ - 1, 1 - s)
                    if q > 0 and exists(b):
                        values(b, q - 1, s)
                    if q == 1 and exists(b + 1):
                        turn_maxima(b + 1, 1 - s)
                    if q == 2 and exists(b - 2):
                        project(b - 2, s)
                    if q == 2 and exists(b - 1):
                        turn_back(b - 1, 1 - s)

            run(pe, step)

        @block.vector
        def _(dve):
            dve.wait_ge(cleared, 1)

            def maxima(b, q, s):
                n = b * NQ + q
                wait(dve, scored, n + 1)
                dve.tensor_reduce(neg[:, s, q * HQ:(q + 1) * HQ], ps_s[:, q % 2, :].rearrange("p (h k) -> p h k", h=HQ),
                                  AX_X, ALU.max, negate=True).then_inc(max_done, 1)

            def split(b, s):
                ch = Chain(dve, neg_step, b * 3)
                wait(dve, max_done, (b + 1) * NQ)
                ch.step(dve.tensor_copy(neg_parts[:, s, 0:H], neg[:, s, :]))
                ch.settle()
                ch.step(dve.tensor_tensor(neg_rest[:, s, :], neg[:, s, :], neg_parts[:, s, 0:H], ALU.subtract))
                ch.settle()
                ch.step(dve.tensor_copy(neg_parts[:, s, H:2 * H], neg_rest[:, s, :]))
                ch.settle()
                dve.tensor_tensor(neg_parts[:, s, 2 * H:3 * H], neg_rest[:, s, :], neg_parts[:, s, H:2 * H],
                                  ALU.subtract).then_inc(neg_ready, 1)

            def normalise_output(b, s):
                wait(dve, ot_back, b + 1)
                heads = ps_o[:].rearrange("p (h c) -> p h c", h=H)
                dve.reciprocal(inv[:, s, :], heads[:, :, DK]).then_inc(o_step, 1)
                wait(dve, o_step, 2 * b + 1)
                dve.tensor_tensor(o[:, s, :].rearrange("p (h d) -> p h d", h=H), heads[:, :, 0:DK],
                                  inv[:, s, :].unsqueeze(2).to_broadcast([P, H, DK]), ALU.mult).then_inc(o_step, 1)

            def residual(b):
                wait(dve, y_done, b + 1)
                dve.tensor_tensor(batch_of(x_all, b), ps_y[:, P:2 * P], batch_of(x_all, b), ALU.add).then_inc(x_ready, 1)

            def stats(b):
                dve.bn_stats(batch_of(c["st"], b), batch_of(x_all, b)).then_inc(st_ready, 1)

            def step(b, r):
                s = r % 2
                for q in range(NQ):
                    if q == 3 and exists(b - 2):
                        residual(b - 2)
                        wait(dve, x_ready, b - 1)
                    if exists(b + 2):
                        maxima(b + 2, q, s)
                    if q == 3 and exists(b - 2):
                        stats(b - 2)
                    if q == 3 and exists(b - 1):
                        normalise_output(b - 1, 1 - s)
                if exists(b + 2):
                    split(b + 2, s)

            run(dve, step, (lambda: dve.wait_ge(bias_added, 1)) if layer == 0 else None)

        @block.scalar
        def _(act):
            def exponentials(b, q):
                n = b * NQ + q
                wait(act, shifted, n + 1)
                wait(act, pv_done, n - NQ + 1)
                act.activation(probs[:, q, :], ps_e[:, q % 2, :], ACT.Exp, scale=SCALE).then_inc(exp_done, 1)

            def copy_sums(b, s):
                wait(act, pv_done, (b + 1) * NQ)
                act.activation(o_t[:, s, :], ps_v[:], ACT.Copy).then_inc(ot_ready, 1)

            def copy_maxima(b, r):
                s = r % 2
                wait(act, negt_done, b + 1)
                wait(act, neg_laid[(r - 2) % SLOTS], of_slot(b - 2, (r - 2) % SLOTS, SLOTS, 16))
                act.activation(neg_t[:, s, :], ps_n[0:PARTS * H, 0:P], ACT.Copy).then_inc(negt_ready, 1)

            def copy_output(b, s):
                wait(act, oot_done, b + 1)
                act.activation(oo_t[:, s, :], ps_y[:, 0:P], ACT.Copy).then_inc(oot_ready, 1)

            def step(b, r):
                s = r % 2
                for q in range(NQ):
                    if exists(b):
                        exponentials(b, q)
                    if q == 0 and exists(b - 1):
                        copy_sums(b - 1, 1 - s)
                    if q == 1 and exists(b - 2):
                        copy_output(b - 2, s)
                    if q == 1 and exists(b + 1):
                        copy_maxima(b + 1, (r + 1) % SLOTS)

            run(act, step)

        @block.gpsimd
        def _(pool):
            pool.memset(neg_parts[:], 0.0).then_inc(cleared, 1)
            pool.memset(v_aug[:], 0.0).then_inc(cleared, 1)
            pool.wait_ge(cleared, 2)
            pool.memset(v_aug[:, :, :, DK:DK + 1], 1.0).then_inc(cleared, 1)
            pool.wait_ge(cleared, 3)

            def fill(b, s):
                wait(pool, pv_done, (b - 1) * NQ)
                wait(pool, row_clear, b - 2)
                pool.tensor_copy(v_aug[:, s, :, 0:DK],
                                 c["v"][:, layer, bass.ds(b, 1), :].rearrange("p b (h d) -> p (b h) d", h=H))\
                    .then_inc(vaug_ready, 1)

            def clear_maxima(b, r):
                wait(pool, vaug_ready, b + 3 if exists(b + 2) else B)
                zeros = c["zero"][ROW_MAX:ROW_MASK, 0:1].to_broadcast([PARTS, H * P // 2])
                pool.tensor_tensor(q_rows[ROW_MAX:ROW_MASK, r].rearrange("p h t -> p (h t)").bitcast(I32), zeros, zeros,
                                   ALU.add).then_inc(row_clear, 1)

            def step(b, r):
                if exists(b + 1):
                    fill(b + 1, 1 - r % 2)
                if exists(b - 1) and exists(b + 1):
                    clear_maxima(b - 1, (r - 1) % SLOTS)

            def add_bias():
                pool.wait_ge(row_clear, 1)
                pool.tensor_tensor(x_all[:], x_all[:], c["row_bias"][:, 1, :].unsqueeze(1).to_broadcast([P, B, D]),
                                   ALU.add).then_inc(bias_added, 1)
                pool.wait_ge(bias_added, 1)

            run(pool, step, add_bias if layer == 0 else None)


def experts(nc, t, c):
    x_all, ident, mean, rstd, vareps = c["x"], c["ident"], c["mean"], c["rstd"], c["vareps"]
    attn_w, ctx_t, w1, w2, ffn_w = c["attn_w"], c["ctx_t"], c["w1"], c["w2"], c["ffn_w"]
    gate_w, norm_w, b1, b2 = c["gate_w"], c["norm_w"], c["b1"], c["b2"]
    with ExitStack() as ph:
        def sb(name, shape, dt):
            return ph.enter_context(nc.sbuf_tensor(name, shape, dt))

        def sem(name):
            return ph.enter_context(nc.semaphore(name))

        wtmp = sb("wtmp", [P, 3, F], F32)
        wsum, winv = sb("wsum", [P, 3], F32), sb("winv", [P, 3], F32)
        tok_t = sb("tok_t", [P, T], F32)
        tmp = sb("tmp_m", [P, B], F32)
        rank_i, rank = sb("rank_i", [P, E], I32), sb("rank", [P, E], F32)
        tk = sb("tk", [P, B, D], F32)
        x_scl, x_off = sb("x_scl_m", [P, B], F32), sb("x_off", [P, B], F32)
        k_full, k_rest, k_parts = sb("k1_full", [P, NG, GT], F32), sb("k1_rest", [P, NG, GT], F32), sb("k1_parts", [P, NG, PARTS, GT], BF16)
        q_full, q_rest, q_parts = sb("q1_full", [P, GT], F32), sb("q1_rest", [P, GT], F32), sb("q1_parts", [P, NG, PARTS, GT], BF16)
        xn, xn_t = sb("xn1", [P, G, D], F32), sb("xn1_t", [P, GT], F32)
        st_g = sb("st_g", [P, G, 6], F32)
        mean_g, vareps_g, rstd_g, tmp_g = (sb(f"{n}_g", [P, G], F32) for n in ("mean", "vareps", "rstd", "tmp"))
        logits, second = sb("logits", [P, B, E], F32), sb("second", [P, B, E], F32)
        best, eq, score = sb("best", [P, 2, B], F32), sb("eq", [P, 2, B, E], F32), sb("score", [P, 2, B, E], F32)
        mark, sel = sb("mark", [P, 2, B], F32), sb("sel", [P, 2, B, E], F32)
        diff, ex, den, wt = sb("diff", [P, B], F32), sb("ex", [P, B], F32), sb("den", [P, B], F32), sb("wt", [P, 2, B], F32)
        comb = sb("comb", [P, B, E], F32)
        hid = sb("hid", [P, 2 * M, GT], F32)
        c_g, c_t = sb("c_g", [P, G, E], F32), sb("c_t", [E, GT], F32)
        ps_h = ph.enter_context(nc.psum_tensor("ps_h", [P, 2, GT], F32))
        ps_y = ph.enter_context(nc.psum_tensor("ps_ym", [P, 2, GT], F32))
        ps_c = ph.enter_context(nc.psum_tensor("ps_c", [P, GT], F32))
        ps_b = ph.enter_context(nc.psum_tensor("ps_b", [P, GT], F32))
        ps_g = ph.enter_context(nc.psum_tensor("ps_g", [P, GT], F32))
        ps_q = ph.enter_context(nc.psum_tensor("ps_q", [P, GT], F32))
        stats_step = sem("stats_step_m")
        tk_ready, x_added, rank_ready = sem("tk_ready"), sem("x_added"), sem("rank_ready")
        k_done, k_copied, k_rest_ready, k_split, k_stored, v_done, v_ready = (
            sem("k1_done"), sem("k1_copied"), sem("k1_rest"), sem("k1_split"), sem("k1_stored"), sem("v1_done"), sem("v1_ready"))
        q_stats, xn_ready, xn_turned, xnt_ready, q_done, q_copied, q_rest_ready, q_split, q_stored = (
            sem("q1_stats"), sem("xn1_ready"), sem("xn1_turned"), sem("xn1_t_ready"), sem("q1_done"),
            sem("q1_copied"), sem("q1_rest_ready"), sem("q1_split"), sem("q1_stored"))
        t_done, tok_ready, g_done, top_step, diff_ready, ex_ready = (
            sem("t_done_m"), sem("tok_ready"), sem("g_done"), sem("top_step"), sem("diff_ready"), sem("ex_ready"))
        wsum_ready, sums_done, quant_step = sem("wsum_ready"), sem("sums_done"), sem("quant_step")
        h_done, h_ready, y_done, y_read = sem("h_done"), sem("h_ready"), sem("y_done_m"), sem("y_read")
        cg_ready, ct_done, ct_ready, b_done, b_read = (
            sem("cg_ready"), sem("ct_done"), sem("ct_ready"), sem("b_done"), sem("b_read"))
        st_ready, scale_ready = sem("st_ready_m"), sem("scale_ready")
        block = ph.enter_context(nc.Block())

        def group_parts(g):
            return q_parts[:, bass.ds(g, 1)].rearrange("p g r s -> p (g r) s")

        @block.sync
        def _(sp):
            for g in range(NG):
                sp.wait_ge(k_split, 2 * (g + 1))
                store_parts(sp, c["k_dram"][1], g * G, k_parts[:, g], K_PARTS, k_stored)

            def store_queries(g):
                sp.wait_ge(q_split, 2 * (g + 1))
                store_parts(sp, c["q_dram"][1], g * G, group_parts(g), PARTS, q_stored)

            store_queries(0)
            sp.wait_ge(k_stored, 16 * K_PARTS * NG)
            sp.wait_ge(q_stored, 16 * PARTS)
            for b in range(SLOTS):
                load_rows(sp, c, 1, b, b)
            with sp.Fori(1, NG) as g:
                store_queries(g)
            sp.wait_ge(q_stored, 16 * PARTS * NG)

        @block.gpsimd
        def _(pool):
            pool.iota(rank_i[:], pattern=[[-1, E]], base=E, channel_multiplier=0).then_inc(rank_ready, 1)
            pool.wait_ge(rank_ready, 1)
            pool.tensor_copy(rank[:], rank_i[:]).then_inc(rank_ready, 1)
            pool.wait_ge(stats_step, STAT_STEPS + 2)
            for cols in [slice(B + g * G, B + (g + 1) * G) for g in range(NG)] + [slice(0, B)]:
                pool.tensor_tensor(rstd[:, cols], vareps[:, cols], c["half"][:, cols], ALU.pow).then_inc(stats_step, 1)
            for g in range(NG):
                pool.wait_ge(k_copied, 2 * (g + 1))
                pool.tensor_tensor(k_rest[:, g], k_full[:, g], k_parts[:, g, 0], ALU.subtract).then_inc(k_rest_ready, 1)

            def queries(g):
                wait(pool, q_stats, g * (STAT_STEPS + 1) + STAT_STEPS)
                pool.tensor_tensor(rstd_g[:], vareps_g[:], c["half"][:, 0:G], ALU.pow).then_inc(q_stats, 1)
                wait(pool, q_copied, 2 * (g + 1))
                pool.tensor_tensor(q_rest[:], q_full[:], group_parts(g)[:, 0, :], ALU.subtract).then_inc(q_rest_ready, 1)

            with pool.Fori(0, NG) as g:
                queries(g)

        @block.vector
        def _(dve):
            mean_and_variance(dve, stats_step, 0, c["st"], mean[:], vareps[:, 0:B], tmp[:])
            dve.wait_ge(stats_step, STAT_STEPS)
            dve.tensor_scalar(tmp[:], vareps[:, 0:B], -EPS_LN, None, ALU.add).then_inc(stats_step, 1)
            dve.wait_ge(stats_step, STAT_STEPS + 1)
            dve.scalar_tensor_tensor(out=vareps[:, B:2 * B], in0=vareps[:, 0:B], scalar=EPS_RMS, in1=tmp[:],
                                     op0=ALU.mult, op1=ALU.add).then_inc(stats_step, 1)
            for b in range(B):
                if b % G == 0:
                    dve.wait_ge(stats_step, STAT_STEPS + 3 + b // G)
                dve.tensor_scalar(tk[:, b, :], x_all[:, b, :], mean[:, b:b + 1], rstd[:, B + b:B + b + 1],
                                  ALU.subtract, ALU.mult).then_inc(tk_ready, 1)
            for n in range(3):
                dve.tensor_reduce(wsum[:, n:n + 1], ffn_w[:, n, :], AX_X, ALU.add,
                                  apply_absolute_value=True).then_inc(wsum_ready, 1)
            dve.wait_ge(stats_step, STAT_STEPS + 3 + NG)
            dve.tensor_scalar(x_scl[:], rstd[:, 0:B], 1.0, None, ALU.add).then_inc(scale_ready, 1)
            dve.scalar_tensor_tensor(out=x_off[:], in0=mean[:], scalar=-1.0, in1=rstd[:, 0:B], op0=ALU.mult,
                                     op1=ALU.mult).then_inc(scale_ready, 1)

            ch = Chain(dve, top_step, 0)
            dve.wait_ge(g_done, 1)
            dve.wait_ge(rank_ready, 2)
            ch.step(dve.tensor_copy(logits[:].rearrange("p b e -> p (b e)"), ps_g[:, 0:B * E]))
            ch.settle()
            rank_b = rank[:].unsqueeze(1).to_broadcast([P, B, E])
            for n, lg in enumerate((logits, second)):
                ch.step(dve.tensor_reduce(best[:, n, :], lg[:], AX_X, ALU.max))
                ch.settle()
                ch.step(dve.tensor_tensor(eq[:, n], lg[:], best[:, n, :].unsqueeze(2).to_broadcast([P, B, E]), ALU.is_equal))
                ch.settle()
                ch.step(dve.tensor_tensor(score[:, n], eq[:, n], rank_b, ALU.mult))
                ch.settle()
                ch.step(dve.tensor_reduce(mark[:, n, :], score[:, n], AX_X, ALU.max))
                ch.settle()
                ch.step(dve.tensor_tensor(sel[:, n], rank_b, mark[:, n, :].unsqueeze(2).to_broadcast([P, B, E]), ALU.is_equal))
                ch.settle()
                if n == 0:
                    ch.step(dve.scalar_tensor_tensor(out=second[:], in0=sel[:, 0], scalar=-3e38, in1=logits[:],
                                                     op0=ALU.mult, op1=ALU.add))
                    ch.settle()
            dve.tensor_tensor(diff[:], best[:, 1, :], best[:, 0, :], ALU.subtract).then_inc(diff_ready, 1)
            dve.wait_ge(ex_ready, 1)
            ch.step(dve.tensor_scalar(den[:], ex[:], 1.0, None, ALU.add))
            ch.settle()
            ch.step(dve.reciprocal(wt[:, 0, :], den[:]))
            ch.settle()
            ch.step(dve.tensor_tensor(wt[:, 1, :], ex[:], wt[:, 0, :], ALU.mult))
            ch.settle()
            for n in range(2):
                ch.step(dve.tensor_tensor(sel[:, n], sel[:, n], wt[:, n, :].unsqueeze(2).to_broadcast([P, B, E]), ALU.mult))
            ch.settle()
            ch.step(dve.tensor_tensor(comb[:], sel[:, 0], sel[:, 1], ALU.add))
            ch.settle()
            dve.wait_ge(x_added, B)

            def stats(g):
                for j in range(G):
                    dve.bn_stats(st_g[:, j, :], batch_of(x_all, g * G + j)).then_inc(st_ready, 1)

            def split_keys(g):
                dve.wait_ge(k_rest_ready, g + 1)
                dve.tensor_copy(k_parts[:, g, 1], k_rest[:, g]).then_inc(k_split, 1)
                dve.wait_ge(k_split, 2 * g + 1)
                dve.tensor_tensor(k_parts[:, g, 2], k_rest[:, g], k_parts[:, g, 1], ALU.subtract).then_inc(k_split, 1)

            def query_stats(g):
                wait(dve, st_ready, (g + 1) * G)
                mean_and_variance(dve, q_stats, g * (STAT_STEPS + 1), st_g, mean_g[:], vareps_g[:], tmp_g[:])

            def normalise(g):
                wait(dve, q_stats, (g + 1) * (STAT_STEPS + 1))
                for j in range(G):
                    dve.tensor_scalar(xn[:, j, :], batch_of(x_all, g * G + j), mean_g[:, j:j + 1], rstd_g[:, j:j + 1],
                                      ALU.subtract, ALU.mult).then_inc(xn_ready, 1)

            def split_queries(g):
                wait(dve, q_rest_ready, g + 1)
                dve.tensor_copy(group_parts(g)[:, 1, :], q_rest[:]).then_inc(q_split, 1)
                wait(dve, q_split, 2 * g + 1)
                dve.tensor_tensor(group_parts(g)[:, 2, :], q_rest[:], group_parts(g)[:, 1, :], ALU.subtract)\
                   .then_inc(q_split, 1)

            def group(g, first=False):
                wait(dve, y_read, g * E * G)
                wait(dve, ct_done, g)
                dve.tensor_copy(c_g[:], comb[:, bass.ds(g * G, G), :]).then_inc(cg_ready, 1)
                if not first:
                    stats(g - 1)
                dve.wait_ge(cg_ready, g + 1)
                for e in range(E):
                    n = g * E + e
                    dve.wait_ge(y_done, n + 1)
                    for j in range(G):
                        wait(dve, y_read, (n - 1) * G + j + 1)
                        dve.scalar_tensor_tensor(out=batch_of(x_all, g * G + j), in0=ps_y[:, e % 2, j * D:(j + 1) * D],
                                                 scalar=c_g[:, j, e:e + 1], in1=batch_of(x_all, g * G + j),
                                                 op0=ALU.mult, op1=ALU.add).then_inc(y_read, 1)
                    if e == 2:
                        dve.wait_ge(b_done, g + 1)
                        dve.wait_ge(y_read, (n + 1) * G)
                        x_g = x_all[:, bass.ds(g * G, G), :]
                        dve.tensor_tensor(x_g, ps_b[:].rearrange("p (j d) -> p j d", j=G), x_g, ALU.add).then_inc(b_read, 1)
                        dve.wait_ge(b_read, g + 1)
                    if first and e >= E - NG:
                        split_keys(e - (E - NG))
                    if not first:
                        if e == 0:
                            query_stats(g - 1)
                        if e == 2:
                            normalise(g - 1)
                        if e == E - 1:
                            split_queries(g - 1)

            group(0, first=True)
            qs = Chain(dve, quant_step, 0)
            dve.wait_ge(sums_done, 1)
            qs.step(dve.tensor_scalar(c["w_scale"][:], ps_q[:, 0:3], 1.0 / (D * F), 1e-5, ALU.mult, ALU.max))
            qs.settle()
            qs.step(dve.reciprocal(winv[:], c["w_scale"][:]))
            qs.settle()
            for n in range(3):
                qs.step(dve.tensor_scalar(wtmp[:, n, :], ffn_w[:, n, :], winv[:, n:n + 1], 1.0, ALU.mult, ALU.min))
            qs.settle()
            qs.step(dve.tensor_scalar(wtmp[:], wtmp[:], -1.0, MAGIC, ALU.max, ALU.add))
            qs.settle()
            qs.step(dve.tensor_scalar(c["ffn_wq"][:], wtmp[:], -MAGIC, None, ALU.add))
            with dve.Fori(1, NG) as g:
                group(g)
            dve.wait_ge(y_read, NG * E * G)
            stats(NG - 1)
            query_stats(NG - 1)
            normalise(NG - 1)
            split_queries(NG - 1)

        @block.tensor
        def _(pe):

            def context_group(g):
                wait(pe, k_copied, 2 * (g - 1))
                pe.matmul(ps_y[:, g % 2, :], attn_w[:, 1, 1, :], ctx_t[:, g * GT:(g + 1) * GT],
                          start=True, stop=True).then_inc(k_done, 1)
                wait(pe, v_ready, g - 1)
                for j in range(G):
                    last = pe.matmul((ps_c, ps_b)[g % 2][:, j * D:(j + 1) * D], ctx_t[:, (g * G + j) * P:(g * G + j + 1) * P],
                                     attn_w[:, 1, 2, :], start=True, stop=True)
                last.then_inc(v_done, 1)

            def turn_tokens(g):
                pe.wait_ge(tk_ready, (g + 1) * G)
                wait(pe, tok_ready, g - 1)
                for j in range(G):
                    last = pe.transpose(ps_h[:, g % 2, j * P:(j + 1) * P], tk[:, g * G + j, :], ident[:])
                last.then_inc(t_done, 1)

            def gate(g):
                pe.wait_ge(tok_ready, g + 1)
                for j in range(G):
                    b = g * G + j
                    last = pe.matmul(ps_g[:, b * E:(b + 1) * E], tok_t[:, b * P:(b + 1) * P], gate_w[:],
                                     start=True, stop=True)
                return last

            for g in range(NG):
                context_group(g)
            turn_tokens(0)
            for g in range(NG):
                if g + 1 < NG:
                    turn_tokens(g + 1)
                last = gate(g)
            last.then_inc(g_done, 1)
            pe.wait_ge(k_copied, 2 * NG)
            pe.wait_ge(v_ready, NG)
            pe.wait_ge(wsum_ready, 3)
            pe.matmul(ps_q[:, 0:3], c["ones"][:], wsum[:], start=True, stop=True).then_inc(sums_done, 1)

            def hidden(g, e):
                for m in range(M):
                    n = g * (E * M) + e * M + m
                    wait(pe, h_ready, n - 1)
                    pe.matmul(ps_h[:, m, :], w1[:, e, m * P:(m + 1) * P], tok_t[:, bass.ds(g * GT, GT)],
                              start=True, stop=True).then_inc(h_done, 1)

            def out(g, e):
                n = g * E + e
                pe.wait_ge(h_ready, (n + 1) * M)
                wait(pe, y_read, (n - 1) * G)
                for j in range(G):
                    for m in range(M):
                        last = pe.matmul(ps_y[:, e % 2, j * D:(j + 1) * D],
                                         hid[:, (e % 2) * M + m, j * P:(j + 1) * P], w2[:, e, m, :],
                                         start=(m == 0), stop=(m == M - 1))
                last.then_inc(y_done, 1)

            def turn_weights(g):
                pe.wait_ge(cg_ready, g + 1)
                wait(pe, ct_ready, g)
                for j in range(G):
                    last = pe.transpose(ps_c[0:E, j * P:(j + 1) * P], c_g[:, j, :], ident[:])
                last.then_inc(ct_done, 1)

            def bias(g):
                pe.wait_ge(ct_ready, g + 1)
                wait(pe, b_read, g)
                for j in range(G):
                    last = pe.matmul(ps_b[:, j * D:(j + 1) * D], c_t[:, j * P:(j + 1) * P], b2[:],
                                     start=True, stop=True)
                last.then_inc(b_done, 1)

            def turn_queries(g):
                wait(pe, xn_ready, (g + 1) * G)
                for j in range(G):
                    last = pe.transpose(ps_c[:, j * P:(j + 1) * P], xn[:, j, :], ident[:])
                last.then_inc(xn_turned, 1)

            def project_queries(g):
                wait(pe, xnt_ready, g + 1)
                pe.matmul(ps_q[:], attn_w[:, 1, 0, :], xn_t[:], start=True, stop=True).then_inc(q_done, 1)

            def group(g, first=False):
                hidden(g, 0)
                for e in range(E):
                    if e + 1 < E:
                        hidden(g, e + 1)
                    if e == 1:
                        turn_weights(g)
                    if e == 2:
                        bias(g)
                    out(g, e)
                    if not first:
                        if e == 3:
                            turn_queries(g - 1)
                        if e == 4:
                            project_queries(g - 1)

            group(0, first=True)
            with pe.Fori(1, NG) as g:
                group(g)
            turn_queries(NG - 1)
            project_queries(NG - 1)

        @block.scalar
        def _(act):

            def copy_context(g):
                act.wait_ge(k_done, g + 1)
                act.activation(k_parts[:, g, 0], ps_y[:, g % 2, :], ACT.Copy).then_inc(k_copied, 1)
                act.activation(k_full[:, g], ps_y[:, g % 2, :], ACT.Copy).then_inc(k_copied, 1)
                act.wait_ge(v_done, g + 1)
                act.activation(c["v"][:, 1, g * G:(g + 1) * G, :].rearrange("p b d -> p (b d)"), (ps_c, ps_b)[g % 2][:],
                               ACT.Copy).then_inc(v_ready, 1)

            for g in range(NG):
                copy_context(g)
            for g in range(NG):
                act.wait_ge(t_done, g + 1)
                act.activation(tok_t[:, g * GT:(g + 1) * GT], ps_h[:, g % 2, :], ACT.Copy, scale=norm_w[:, 0:1])\
                   .then_inc(tok_ready, 1)
            act.wait_ge(scale_ready, 2)
            act.wait_ge(tk_ready, B)
            for b in range(B):
                act.activation(x_all[:, b, :], x_all[:, b, :], ACT.Identity, bias=x_off[:, b:b + 1],
                               scale=x_scl[:, b:b + 1]).then_inc(x_added, 1)
            act.wait_ge(diff_ready, 1)
            act.activation(ex[:], diff[:], ACT.Exp).then_inc(ex_ready, 1)

            def copy_turned(g):
                wait(act, xn_turned, g + 1)
                act.activation(xn_t[:], ps_c[:], ACT.Copy).then_inc(xnt_ready, 1)

            def copy_queries(g):
                wait(act, q_done, g + 1)
                act.activation(group_parts(g)[:, 0, :], ps_q[:], ACT.Copy).then_inc(q_copied, 1)
                act.activation(q_full[:], ps_q[:], ACT.Copy).then_inc(q_copied, 1)

            def group(g, first=False):
                for e in range(E):
                    for m in range(M):
                        n = g * (E * M) + e * M + m
                        act.wait_ge(h_done, n + 1)
                        wait(act, y_done, g * E + e - 1)
                        act.activation(hid[:, (e % 2) * M + m, :], ps_h[:, m, :], ACT.Gelu,
                                       bias=b1[:, e * M + m:e * M + m + 1]).then_inc(h_ready, 1)
                    if e == 2:
                        act.wait_ge(ct_done, g + 1)
                        wait(act, b_done, g)
                        act.activation(c_t[:], ps_c[0:E, :], ACT.Copy).then_inc(ct_ready, 1)
                    if not first:
                        if e == 4:
                            copy_turned(g - 1)
                        if e == 5:
                            copy_queries(g - 1)

            group(0, first=True)
            with act.Fori(1, NG) as g:
                group(g)
            copy_turned(NG - 1)
            copy_queries(NG - 1)


def ternary_ffn(nc, t, c):
    x_all, ident, mean, rstd = c["x"], c["ident"], c["mean"], c["rstd"]
    with ExitStack() as ph:
        def sb(name, shape, dt):
            return ph.enter_context(nc.sbuf_tensor(name, shape, dt))

        def sem(name):
            return ph.enter_context(nc.semaphore(name))

        tmp = sb("tmp_f", [P, B], F32)
        xh, xr = sb("xh_f", [P, B, D], F32), sb("xr", [P, B, D], F32)
        x_max, x_scl, x_inv = sb("x_max", [P, B], F32), sb("x_scl", [P, B], F32), sb("x_inv", [P, B], F32)
        gate_scl, up_scl = sb("gate_scl", [P, B], F32), sb("up_scl", [P, B], F32)
        magic = sb("magic", [P, 2], F32)
        xq_t = sb("xq_t", [P, B, P], BF16)
        gate, gu, gr = sb("gate", [P, 2, F], F32), sb("gu", [P, 2, F], F32), sb("gr", [P, 2, F], F32)
        g_max, g_scl = sb("g_max", [P, 4], F32), sb("g_scl", [P, 4, 4], F32)
        gq_t = sb("gq_t", [P, 2, F], BF16)
        ps_t = ph.enter_context(nc.psum_tensor("ps_tf", [P, 2, F], F32))
        ps_g = ph.enter_context(nc.psum_tensor("ps_gf", [P, 2, F], F32))
        ps_u = ph.enter_context(nc.psum_tensor("ps_uf", [P, 2, F], F32))
        ps_d = ph.enter_context(nc.psum_tensor("ps_df", [P, 2, F], F32))
        stats_step, magic_ready = sem("stats_step_f"), sem("magic_ready")
        xh_ready, head_step, fma_ready, clamp_ready, xt_done, xt_ready = (
            sem("xh_ready_f"), sem("head_step"), sem("fma_ready"), sem("clamp_ready"), sem("xt_done_f"), sem("xt_ready_f"))
        gu_done, gate_ready, gu_ready, gmax_ready, gscl_step, gr_ready, gc_ready = (
            sem("gu_done"), sem("gate_ready"), sem("gu_ready"), sem("gmax_ready"), sem("gscl_step"), sem("gr_ready"), sem("gc_ready"))
        gt_done, gt_ready, d_done, out_ready = sem("gt_done"), sem("gt_ready"), sem("d_done"), sem("out_ready")
        stored = sem("stored_f")
        block = ph.enter_context(nc.Block())
        HEAD = 5

        def run(eng, step, head):
            for h in range(NG):
                head(h)
                step(h, h % 4)
            head(NG)
            with eng.Fori(1, B // 4) as i:
                for j in range(4):
                    step(i * 4 + j, j)
            for h in range(B, B + 4):
                step(h, h % 4)

        @block.gpsimd
        def _(pool):
            pool.memset(magic[:, 0:1], MAGIC).then_inc(magic_ready, 1)
            pool.memset(magic[:, 1:2], -MAGIC).then_inc(magic_ready, 1)
            pool.wait_ge(stats_step, STAT_STEPS)
            for g in range(NG):
                cols = slice(g * G, (g + 1) * G)
                pool.tensor_tensor(rstd[:, cols], c["vareps"][:, cols], c["half"][:, cols], ALU.pow).then_inc(stats_step, 1)


        @block.vector
        def _(dve):
            mean_and_variance(dve, stats_step, 0, c["st"], mean[:], c["vareps"][:, 0:B], tmp[:])

            def scale_x(g):
                dve.wait_ge(stats_step, STAT_STEPS + 1 + g)
                a, b = g * G, (g + 1) * G
                for n in range(a, b):
                    dve.tensor_scalar(xh[:, n, :], x_all[:, n, :], mean[:, n:n + 1], rstd[:, n:n + 1],
                                      ALU.subtract, ALU.mult).then_inc(xh_ready, 1)
                dve.wait_ge(xh_ready, b)
                ch = Chain(dve, head_step, g * HEAD)
                ch.step(dve.tensor_reduce(x_max[:, a:b], xh[:, a:b, :], AX_X, ALU.max, apply_absolute_value=True))
                ch.settle()
                ch.step(dve.tensor_scalar(x_scl[:, a:b], x_max[:, a:b], 1e-5, 1.0 / 127.0, ALU.max, ALU.mult))
                ch.settle()
                ch.step(dve.reciprocal(x_inv[:, a:b], x_scl[:, a:b]))
                ch.step(dve.tensor_scalar(gate_scl[:, a:b], x_scl[:, a:b], c["w_scale"][:, 0:1], None, ALU.mult))
                ch.step(dve.tensor_scalar(up_scl[:, a:b], x_scl[:, a:b], c["w_scale"][:, 1:2], None, ALU.mult))
                assert ch.n == HEAD

            def clamp_x(g):
                a, b = g * G, (g + 1) * G
                dve.wait_ge(fma_ready, b)
                dve.tensor_scalar(xr[:, a:b, :], xr[:, a:b, :], MAGIC + 127.0, MAGIC - 128.0, ALU.min, ALU.max)\
                   .then_inc(clamp_ready, 1)

            scale_x(0)

            def head(g):
                if g + 1 < NG:
                    scale_x(g + 1)
                if g < NG:
                    clamp_x(g)
                else:
                    dve.wait_ge(head_step, NG * HEAD)

            def product(b, s):
                wait(dve, gate_ready, b + 1)
                wait(dve, gr_ready, b - 1)
                dve.scalar_tensor_tensor(out=gu[:, s, :], in0=ps_u[:, s, :], scalar=up_scl[:, bass.ds(b, 1)],
                                         in1=gate[:, s, :], op0=ALU.mult, op1=ALU.mult).then_inc(gu_ready, 1)

            def maximum(b, r):
                wait(dve, gu_ready, b + 1)
                dve.tensor_reduce(g_max[:, r:r + 1], gu[:, r % 2, :], AX_X, ALU.max, apply_absolute_value=True)\
                   .then_inc(gmax_ready, 1)

            def scales(b, r):
                wait(dve, gmax_ready, b + 1)
                dve.tensor_scalar(g_scl[:, r, 0:1], g_max[:, r:r + 1], 1e-5, 1.0 / 127.0, ALU.max, ALU.mult)\
                   .then_inc(gscl_step, 1)
                wait(dve, gscl_step, b * 3 + 1)
                dve.reciprocal(g_scl[:, r, 1:2], g_scl[:, r, 0:1]).then_inc(gscl_step, 1)
                dve.tensor_scalar(g_scl[:, r, 2:3], c["w_scale"][:, 2:3], g_scl[:, r, 0:1], None, ALU.mult)\
                   .then_inc(gscl_step, 1)

            def clamp_gu(b, s):
                wait(dve, gt_ready, b + 1)
                dve.tensor_scalar(gq_t[:, s, :], gq_t[:, s, :], 127.0, -128.0, ALU.min, ALU.max).then_inc(gc_ready, 1)

            def tail(b, r):
                wait(dve, d_done, b + 1)
                dve.scalar_tensor_tensor(out=batch_of(x_all, b), in0=ps_d[:, r % 2, 0:D], scalar=g_scl[:, r, 2:3],
                                         in1=batch_of(x_all, b), op0=ALU.mult, op1=ALU.add).then_inc(out_ready, 1)

            def step(h, r):
                if exists(h - 1):
                    product(h - 1, (r - 1) % 2)
                if exists(h - 1):
                    maximum(h - 1, (r - 1) % 4)
                if exists(h - 3):
                    clamp_gu(h - 3, (r - 3) % 2)
                if exists(h - 4):
                    tail(h - 4, r)
                if exists(h - 1):
                    scales(h - 1, (r - 1) % 4)

            run(dve, step, head)

        @block.scalar
        def _(act):
            act.wait_ge(magic_ready, 2)

            def round_x(g):
                act.wait_ge(head_step, (g + 1) * HEAD)
                for n in range(g * G, (g + 1) * G):
                    act.activation(xr[:, n, :], xh[:, n, :], ACT.Identity, bias=magic[:, 0:1], scale=x_inv[:, n:n + 1])\
                       .then_inc(fma_ready, 1)

            def copy_x(g):
                act.wait_ge(xt_done, g + 1)
                act.activation(xq_t[:, g * G:(g + 1) * G, :].rearrange("p b s -> p (b s)"), ps_d[:, g % 2, :],
                               ACT.Identity, bias=magic[:, 1:2]).then_inc(xt_ready, 1)

            round_x(0)

            def head(g):
                if g + 1 < NG:
                    round_x(g + 1)
                if g < NG:
                    copy_x(g)

            def silu(b, s):
                wait(act, gu_done, b + 1)
                wait(act, gu_ready, b - 1)
                act.activation(gate[:, s, :], ps_g[:, s, :], ACT.Silu, scale=gate_scl[:, bass.ds(b, 1)])\
                   .then_inc(gate_ready, 1)

            def round_gu(b, r):
                wait(act, gscl_step, b * 3 + 3)
                wait(act, gt_done, b - 1)
                act.activation(gr[:, r % 2, :], gu[:, r % 2, :], ACT.Identity, bias=magic[:, 0:1], scale=g_scl[:, r, 1:2])\
                   .then_inc(gr_ready, 1)

            def copy_gu(b, s):
                wait(act, gt_done, b + 1)
                act.activation(gq_t[:, s, :], ps_t[:, s, :], ACT.Identity, bias=magic[:, 1:2]).then_inc(gt_ready, 1)

            def step(h, r):
                if exists(h - 3):
                    copy_gu(h - 3, (r - 3) % 2)
                if exists(h - 2):
                    round_gu(h - 2, (r - 2) % 4)
                if exists(h):
                    silu(h, r % 2)

            run(act, step, head)

        @block.tensor
        def _(pe):
            def head(g):
                if g == NG:
                    pe.wait_ge(xt_ready, NG)
                    return
                pe.wait_ge(clamp_ready, g + 1)
                wait(pe, xt_ready, g - 1)
                for j in range(G):
                    last = pe.transpose(ps_d[:, g % 2, j * P:(j + 1) * P], xr[:, g * G + j, :], ident[:])
                last.then_inc(xt_done, 1)
                if g == 0:
                    pe.wait_ge(xt_ready, 1)

            def gate_and_up(b, s):
                wait(pe, gu_ready, b - 1)
                x_b = xq_t[:, bass.ds(b, 1), :].rearrange("p b s -> p (b s)")
                pe.matmul(ps_g[:, s, :], x_b, c["ffn_wq"][:, 0, :], start=True, stop=True)
                pe.matmul(ps_u[:, s, :], x_b, c["ffn_wq"][:, 1, :], start=True, stop=True).then_inc(gu_done, 1)

            def turn(b, s):
                wait(pe, gr_ready, b + 1)
                wait(pe, gt_ready, b - 1)
                for k in range(FK):
                    last = pe.transpose(ps_t[:, s, k * P:(k + 1) * P], gr[:, s, k * P:(k + 1) * P], ident[:])
                last.then_inc(gt_done, 1)

            def down(b, s):
                wait(pe, gc_ready, b + 1)
                for k in range(FK):
                    last = pe.matmul(ps_d[:, s, 0:D], gq_t[:, s, k * P:(k + 1) * P], c["ffn_wq"][:, 2, k * D:(k + 1) * D],
                                     start=(k == 0), stop=(k == FK - 1))
                last.then_inc(d_done, 1)

            def step(h, r):
                if exists(h):
                    gate_and_up(h, r % 2)
                if exists(h - 4):
                    down(h - 4, r % 2)
                if exists(h - 2):
                    turn(h - 2, r % 2)

            run(pe, step, head)

        @block.sync
        def _(sp):
            with sp.Fori(0, B) as b:
                sp.wait_ge(out_ready, b + 1)
                sp.dma_start(t["out"][bass.ds(b, 1)].rearrange("b s d -> (b s) d"), batch_of(x_all, b))\
                  .then_inc(stored, 16)
            sp.wait_ge(stored, 16 * B)


def kernel(x, ctx_1024, mask_BxS2_if1, L0_xattn_Wq, L0_xattn_bq, L0_xattn_Wk, L0_xattn_bk, L0_xattn_Wv,
           L0_xattn_bv, L0_xattn_Wo, L0_xattn_bo, L0_ffn_norm_weight, L0_ffn_gate_w, L0_ffn_w1, L0_ffn_b1,
           L0_ffn_w2, L0_ffn_b2, L1_xattn_Wq, L1_xattn_Wk, L1_xattn_Wv, L1_xattn_Wo, L1_ffn_w_gate,
           L1_ffn_w_up, L1_ffn_w_down):
    import numpy as np
    import concourse.bacc as bacc
    from concourse import mybir as mb
    from concourse.bass_utils import run_bass_kernel_spmd

    def by_dim(w):
        return np.reshape(np.swapaxes(np.reshape(w, (*w.shape[:-1], H, DK)), -1, -2), w.shape)

    a = {
        "x": x,
        "ctx_t": np.transpose(ctx_1024, (2, 0, 1)).reshape(D, T),
        "mask": mask_BxS2_if1,
        "L0_Wq": by_dim(np.transpose(L0_xattn_Wq)), "L0_Wk": by_dim(np.transpose(L0_xattn_Wk)),
        "L0_Wv": np.transpose(L0_xattn_Wv), "L0_Wo": np.transpose(L0_xattn_Wo),
        "L1_Wq": by_dim(L1_xattn_Wq), "L1_Wk": by_dim(L1_xattn_Wk), "L1_Wv": L1_xattn_Wv, "L1_Wo": L1_xattn_Wo,
        "bq": np.reshape(by_dim(L0_xattn_bq), (D, 1)), "bk": np.reshape(by_dim(L0_xattn_bk), (D, 1)),
        "bv": np.reshape(L0_xattn_bv, (1, D)), "bo": np.reshape(L0_xattn_bo, (1, D)),
        "norm_w": np.reshape(L0_ffn_norm_weight, (D, 1)),
        "gate_w": np.transpose(L0_ffn_gate_w),
        "w1": np.transpose(L0_ffn_w1, (2, 0, 1)),
        "b1": np.transpose(np.reshape(L0_ffn_b1, (E * M, P))),
        "w2": np.transpose(np.reshape(L0_ffn_w2, (E, D, M, P)), (3, 0, 2, 1)),
        "b2": L0_ffn_b2,
        "w_gate": np.transpose(L1_ffn_w_gate), "w_up": np.transpose(L1_ffn_w_up),
        "w_down": np.transpose(np.reshape(L1_ffn_w_down, (D, FK, P)), (2, 1, 0)),
    }
    nc = bacc.Bacc("TRN2", target_bir_lowering=False, num_devices=1)
    arrays, t = {}, {}
    for name, value in a.items():
        value = np.ascontiguousarray(value)
        arrays[f"in_{name}"] = value
        t[name] = nc.dram_tensor(f"in_{name}", value.shape, mb.dt.from_np(value.dtype), kind="ExternalInput").ap()
    t["out"] = nc.dram_tensor("out", (B, P, D), mb.dt.float32, kind="ExternalOutput").ap()
    main_kernel(nc, t)
    return run_bass_kernel_spmd(nc, [arrays], core_ids=[0]).results[0]["out"]
```

```python
from contextlib import ExitStack

import concourse.bass as bass
from concourse import mybir

ALU = mybir.AluOpType
ACT = mybir.ActivationFunctionType
AX_X = mybir.AxisListType.X
F32 = mybir.dt.float32
BF16 = mybir.dt.bfloat16
I32 = mybir.dt.int32
U32 = mybir.dt.uint32

P = 128
B = 16
T = B * P
D = 128
H = 16
DK = D // H
HQ = 4
NQ = H // HQ
G = 4
NG = B // G
GT = G * P
E = 8
HID = 256
M = HID // P
F = 512
FK = F // P
EPS_LN = 1e-5
EPS_RMS = 1e-6
SCALE = 1.0 / DK ** 0.5
MASKED = -1e30
MAGIC = 1.5 * 2.0 ** 23

PARTS = 3
PRODUCTS = PARTS * PARTS * DK
ROW_MAX = 96
ROW_MASK = ROW_MAX + PARTS
K_PARTS = 5
SLOTS = 4
STAT_STEPS = 7


def wait(eng, sem, value):
    if isinstance(value, int) and value <= 0:
        return
    eng.wait_ge(sem, value)


def exists(b):
    return not isinstance(b, int) or 0 <= b < B


def of_slot(b, r, slots, each):
    return (b - r) * (each // slots) + each


def batch_of(x_all, b):
    return x_all[:, bass.ds(b, 1), :].rearrange("p b d -> p (b d)")


class Chain:

    def __init__(self, eng, sem, base):
        self.eng, self.sem, self.base, self.n = eng, sem, base, 0

    def step(self, ins):
        self.n += 1
        ins.then_inc(self.sem, 1)

    def settle(self):
        wait(self.eng, self.sem, self.base + self.n)


def mean_and_variance(dve, sem, base, st, mean, vareps, tmp, stages=(0, 1, 2)):
    c = Chain(dve, sem, base)
    for stage in stages:
        c.n = 3 * stage
        if stage == 0:
            c.step(dve.tensor_tensor(mean, st[:, :, 1], st[:, :, 4], ALU.add))
            c.step(dve.tensor_tensor(tmp, st[:, :, 1], st[:, :, 4], ALU.subtract))
            c.step(dve.tensor_tensor(vareps, st[:, :, 2], st[:, :, 5], ALU.add))
        elif stage == 1:
            c.settle()
            c.step(dve.tensor_scalar(mean, mean, 0.5, None, ALU.mult))
            c.step(dve.tensor_tensor(tmp, tmp, tmp, ALU.mult))
            c.step(dve.tensor_scalar(vareps, vareps, 1.0 / D, EPS_LN, ALU.mult, ALU.add))
        else:
            c.settle()
            c.step(dve.scalar_tensor_tensor(out=vareps, in0=tmp, scalar=0.25, in1=vareps, op0=ALU.mult, op1=ALU.add))
            assert c.n == STAT_STEPS


def load_rows(sp, c, layer, b, r):
    k_rows, q_rows, rows_in = c["k_rows"], c["q_rows"], c["rows_in"][layer]
    rows = c["k_dram"][layer, bass.ds(b, 1)]
    windows = bass.AP(tensor=rows.tensor, offset=rows.offset,
                      ap=[[DK * H * P, PARTS], [H * P, PARTS * DK], [1, H * P]])
    sp.dma_start(k_rows[0:PRODUCTS, r].rearrange("p h t -> p (h t)"), windows).then_inc(rows_in[r], 16)
    sp.dma_start(q_rows[0:PRODUCTS, r].rearrange("p h t -> p (h t)"),
                 c["q_dram"][layer, bass.ds(b, 1)].rearrange("b r (d h) s -> b (r d) (h s)", h=H)
                 .to_broadcast([PARTS, PARTS * DK, H * P])).then_inc(rows_in[r], 16)
    if layer == 1:
        sp.dma_start(k_rows[ROW_MASK:ROW_MASK + 1, r],
                     c["mask_dram"][bass.ds(b, 1)].unsqueeze(1).to_broadcast([1, H, P])).then_inc(rows_in[r], 16)


def store_parts(sp, dram, b, parts, n_stored, sem):
    for r in range(n_stored):
        sp.dma_start(dram[bass.ds(b, G), r].rearrange("b p s -> p b s"), parts[:, r % PARTS, :]).then_inc(sem, 16)


UNITS = [("k", 0), ("k", 1), ("q", 0), ("k", 2), ("q", 1), ("k", 3), ("q", 2), ("q", 3)]
EARLY = 3
LATE = (4, 3, 6, 5, 7)
AHEAD = 2
WEIGHT_LOADS = 2 * E + 3


def store_unit(sp, c, n, sem):
    kind, g = UNITS[n]
    store_parts(sp, c[kind + "_dram"][0], g * G, c["parts"][:, n], K_PARTS if kind == "k" else PARTS, sem)


class Queries:

    def __init__(self, nc, ctx, c):
        def sb(name, shape, dt):
            return ctx.enter_context(nc.sbuf_tensor("q1_" + name, shape, dt))

        def sem(name):
            return ctx.enter_context(nc.semaphore("q1_" + name))

        self.c = c
        self.full, self.rest = sb("full", [P, GT], F32), sb("rest", [P, GT], F32)
        self.xn, self.xn_t = sb("xn", [P, G, D], F32), sb("xn_t", [P, GT], F32)
        self.st, self.mean, self.tmp = sb("st", [P, G, 6], F32), sb("mean", [P, G], F32), sb("tmp", [P, G], F32)
        self.vareps, self.rstd = sb("vareps", [P, G], F32), sb("rstd", [P, G], F32)
        self.st_ready, self.stats_step, self.xn_ready, self.turned, self.xt_ready = (
            sem("st_ready"), sem("stats_step"), sem("xn_ready"), sem("turned"), sem("xt_ready"))
        self.done, self.copied, self.rest_ready, self.split_step = (
            sem("done"), sem("copied"), sem("rest_ready"), sem("split_step"))
        self.stored = [sem(f"stored{n}") for n in range(3)]

    def parts(self, g):
        return self.c["parts"][:, bass.ds(NG + g, 1)].rearrange("p g r s -> p (g r) s")

    def stats(self, dve, g, batches=range(G)):
        for j in batches:
            dve.bn_stats(self.st[:, j, :], batch_of(self.c["x"], g * G + j)).then_inc(self.st_ready, 1)

    def variance(self, dve, g):
        wait(dve, self.st_ready, (g + 1) * G)
        mean_and_variance(dve, self.stats_step, g * (STAT_STEPS + 1), self.st, self.mean[:], self.vareps[:], self.tmp[:])

    def root(self, pool, g):
        wait(pool, self.stats_step, g * (STAT_STEPS + 1) + STAT_STEPS)
        pool.tensor_tensor(self.rstd[:], self.vareps[:], self.c["half"][:, 0:G], ALU.pow).then_inc(self.stats_step, 1)

    def normalise(self, dve, g, batches=range(G)):
        wait(dve, self.stats_step, (g + 1) * (STAT_STEPS + 1))
        for j in batches:
            dve.tensor_scalar(self.xn[:, j, :], batch_of(self.c["x"], g * G + j), self.mean[:, j:j + 1],
                              self.rstd[:, j:j + 1], ALU.subtract, ALU.mult).then_inc(self.xn_ready, 1)

    def turn(self, pe, g, bank):
        wait(pe, self.xn_ready, (g + 1) * G)
        for j in range(G):
            last = pe.transpose(bank[:, j * P:(j + 1) * P], self.xn[:, j, :], self.c["ident"][:])
        last.then_inc(self.turned, 1)

    def copy_turned(self, act, g, bank):
        wait(act, self.turned, g + 1)
        act.activation(self.xn_t[:], bank, ACT.Copy).then_inc(self.xt_ready, 1)

    def project(self, pe, g, bank):
        wait(pe, self.xt_ready, g + 1)
        pe.matmul(bank, self.c["attn_w"][:, 1, 0, :], self.xn_t[:], start=True, stop=True).then_inc(self.done, 1)

    def copy(self, act, g, bank):
        wait(act, self.done, g + 1)
        act.activation(self.parts(g)[:, 0, :], bank, ACT.Copy).then_inc(self.copied, 1)
        act.activation(self.full[:], bank, ACT.Copy).then_inc(self.copied, 1)

    def leave(self, pool, g):
        wait(pool, self.copied, 2 * (g + 1))
        pool.tensor_tensor(self.rest[:], self.full[:], self.parts(g)[:, 0, :], ALU.subtract).then_inc(self.rest_ready, 1)

    def split(self, dve, g):
        wait(dve, self.rest_ready, g + 1)
        dve.tensor_copy(self.parts(g)[:, 1, :], self.rest[:]).then_inc(self.split_step, 1)
        wait(dve, self.split_step, 2 * g + 1)
        dve.tensor_tensor(self.parts(g)[:, 2, :], self.rest[:], self.parts(g)[:, 1, :], ALU.subtract)\
           .then_inc(self.split_step, 1)

    def store(self, sp, g, signal):
        wait(sp, self.split_step, 2 * (g + 1))
        store_parts(sp, self.c["q_dram"][1], g * G, self.parts(g), PARTS, signal)


class Tokens:
    STEPS = STAT_STEPS + 3

    def __init__(self, nc, ctx, c):
        def sb(name, shape):
            return ctx.enter_context(nc.sbuf_tensor("tok_" + name, shape, F32))

        self.c = c
        self.tk, self.tmp = sb("tk", [P, B, D]), sb("tmp", [P, B])
        self.x_scl, self.x_off = sb("x_scl", [P, B]), sb("x_off", [P, B])
        self.stats_step, self.tk_ready = (
            ctx.enter_context(nc.semaphore("tok_" + n)) for n in ("stats_step", "tk_ready"))

    def variance(self, dve, g, stages=(0, 1, 2)):
        cols = bass.ds(g * G, G)
        mean_and_variance(dve, self.stats_step, g * self.STEPS, self.c["st"][:, cols, :],
                          self.c["mean"][:, cols], self.c["vareps"][:, cols], self.tmp[:, cols], stages)

    def square(self, dve, g, stages=(0, 1)):
        cols, vareps = bass.ds(g * G, G), self.c["vareps"]
        for stage in stages:
            dve.wait_ge(self.stats_step, g * self.STEPS + STAT_STEPS + stage)
            if stage == 0:
                dve.tensor_scalar(self.tmp[:, cols], vareps[:, cols], -EPS_LN, None, ALU.add).then_inc(self.stats_step, 1)
            else:
                dve.scalar_tensor_tensor(out=vareps[:, bass.ds(g * G + B, G)], in0=vareps[:, cols], scalar=EPS_RMS,
                                         in1=self.tmp[:, cols], op0=ALU.mult, op1=ALU.add).then_inc(self.stats_step, 1)

    def root(self, pool, g):
        def both(tile):
            return tile[:].rearrange("p (n b) -> p n b", n=2)[:, :, bass.ds(g * G, G)]

        wait(pool, self.stats_step, g * self.STEPS + STAT_STEPS + 2)
        pool.tensor_tensor(both(self.c["rstd"]), both(self.c["vareps"]), self.c["half"][:, 0:2 * G]
                           .rearrange("p (n b) -> p n b", n=2), ALU.pow).then_inc(self.stats_step, 1)

    def normalise(self, dve, g, batches=range(G)):
        wait(dve, self.stats_step, (g + 1) * self.STEPS)
        for j in batches:
            b = g * G + j
            dve.tensor_scalar(batch_of(self.tk, b), batch_of(self.c["x"], b), self.c["mean"][:, bass.ds(b, 1)],
                              self.c["rstd"][:, bass.ds(b + B, 1)], ALU.subtract, ALU.mult).then_inc(self.tk_ready, 1)

    def scales(self, dve):
        dve.tensor_scalar(self.x_scl[:], self.c["rstd"][:, 0:B], 1.0, None, ALU.add).then_inc(self.tk_ready, 1)
        dve.scalar_tensor_tensor(out=self.x_off[:], in0=self.c["mean"][:], scalar=-1.0,
                                 in1=self.c["rstd"][:, 0:B], op0=ALU.mult, op1=ALU.mult).then_inc(self.tk_ready, 1)

    def piece(self, dve, g, n):
        if n < 3:
            self.variance(dve, g, (n,))
            if n == 2:
                self.square(dve, g, (0,))
        elif n == 3:
            self.square(dve, g, (1,))
        elif n >= 5:
            self.normalise(dve, g, ((0,), (1, 2), (3,))[n - 5])


class Inputs:
    STEPS = 5

    def __init__(self, nc, ctx, c):
        def sb(name, shape):
            return ctx.enter_context(nc.sbuf_tensor("in_" + name, shape, F32))

        self.c = c
        self.xh, self.tmp = sb("xh", [P, B, D]), sb("tmp", [P, B])
        self.max, self.scl, self.inv = sb("max", [P, B]), sb("scl", [P, B]), sb("inv", [P, B])
        self.gate_scl, self.up_scl = sb("gate_scl", [P, B]), sb("up_scl", [P, B])
        self.stats_step, self.xh_ready, self.scale_step = (
            ctx.enter_context(nc.semaphore("in_" + n)) for n in ("stats_step", "xh_ready", "scale_step"))

    def of_group(self, tile, g):
        return tile[:, bass.ds(g * G, G)]

    def variance(self, dve, g, stages=(0, 1, 2)):
        mean_and_variance(dve, self.stats_step, g * (STAT_STEPS + 1), self.c["st"][:, bass.ds(g * G, G), :],
                          *(self.of_group(tile, g) for tile in (self.c["mean"], self.c["vareps"], self.tmp)), stages)

    def root(self, pool, g):
        wait(pool, self.stats_step, g * (STAT_STEPS + 1) + STAT_STEPS)
        pool.tensor_tensor(self.of_group(self.c["rstd"], g), self.of_group(self.c["vareps"], g), self.c["half"][:, 0:G],
                           ALU.pow).then_inc(self.stats_step, 1)

    def normalise(self, dve, g, batches=range(G)):
        wait(dve, self.stats_step, (g + 1) * (STAT_STEPS + 1))
        for j in batches:
            b = g * G + j
            dve.tensor_scalar(batch_of(self.xh, b), batch_of(self.c["x"], b), self.c["mean"][:, bass.ds(b, 1)],
                              self.c["rstd"][:, bass.ds(b, 1)], ALU.subtract, ALU.mult).then_inc(self.xh_ready, 1)

    def scales(self, dve, g, stages=(0, 1, 2)):
        x_max, scl, inv, gate_scl, up_scl = (self.of_group(tile, g) for tile in
                                             (self.max, self.scl, self.inv, self.gate_scl, self.up_scl))
        ch = Chain(dve, self.scale_step, g * self.STEPS)
        for stage in stages:
            ch.n = stage
            if stage == 0:
                wait(dve, self.xh_ready, (g + 1) * G)
                ch.step(dve.tensor_reduce(x_max, self.xh[:, bass.ds(g * G, G), :], AX_X, ALU.max,
                                          apply_absolute_value=True))
            elif stage == 1:
                ch.settle()
                ch.step(dve.tensor_scalar(scl, x_max, 1e-5, 1.0 / 127.0, ALU.max, ALU.mult))
            else:
                ch.settle()
                ch.step(dve.reciprocal(inv, scl))
                ch.step(dve.tensor_scalar(gate_scl, scl, self.c["w_scale"][:, 0:1], None, ALU.mult))
                ch.step(dve.tensor_scalar(up_scl, scl, self.c["w_scale"][:, 1:2], None, ALU.mult))
                assert ch.n == self.STEPS

    def piece(self, dve, g, n):
        if n < 3:
            self.variance(dve, g, (n,))
        elif n in (5, 6):
            self.normalise(dve, g, ((0, 1), (2, 3))[n - 5])
        elif n in (7, 8, 9):
            self.scales(dve, g, (n - 7,))


def main_kernel(nc, t):
    with ExitStack() as ctx:
        def sb(name, shape, dt):
            return ctx.enter_context(nc.sbuf_tensor(name, shape, dt))

        c = {
            "x": sb("x_all", [P, B, D], F32), "st": sb("st_all", [P, B, 6], F32),
            "mean": sb("mean", [P, B], F32), "vareps": sb("vareps", [P, 2 * B], F32),
            "rstd": sb("rstd", [P, 2 * B], F32), "half": sb("half", [P, 2 * B], F32),
            "ident": sb("ident", [P, P], F32), "identb": sb("identb", [P, P], BF16),
            "ones": sb("ones", [P, P], F32),
            "upper": sb("upper", [P, P], BF16),
            "lower": sb("lower", [P, P], BF16),
            "attn_w": sb("attn_w", [P, 2, 4, D], F32),
            "attn_bias": sb("attn_bias", [P, 2], F32),
            "row_bias": sb("row_bias", [P, 2, D], F32),
            "v": sb("v_all", [P, 2, B, D], F32),
            "k_rows": sb("k_rows", [P, SLOTS, H, P], BF16), "q_rows": sb("q_rows", [P, SLOTS, H, P], BF16),
            "ffn_wq": sb("ffn_wq", [P, 3, F], BF16),
            "w_scale": sb("w_scale", [P, 3], F32),
            "zero": sb("zero", [P, 1], I32),
            "ctx_t": sb("ctx_t", [P, T], F32),
            "w1": sb("w1", [P, E, HID], F32), "w2": sb("w2", [P, E, M, D], F32), "ffn_w": sb("ffn_w", [P, 3, F], F32),
            "gate_w": sb("gate_w", [P, E], F32), "norm_w": sb("norm_w", [P, 1], F32),
            "b1": sb("b1", [P, E * M], F32), "b2": sb("b2", [E, D], F32),
            "weights_in": ctx.enter_context(nc.semaphore("weights_in")),
            "late_stored": ctx.enter_context(nc.semaphore("late_stored")),
            "last_stored": ctx.enter_context(nc.semaphore("last_stored")),
            "parts": sb("parts", [P, 2 * NG, PARTS, GT], BF16),
            "parts_stored": ctx.enter_context(nc.semaphore("parts_stored")),
            "rows_in": [[ctx.enter_context(nc.semaphore(f"rows_in{layer}_{r}")) for r in range(SLOTS)]
                        for layer in range(2)],
            "k_dram": nc.dram_tensor("k_dram", (2, B, K_PARTS, P, P), BF16).ap(),
            "q_dram": nc.dram_tensor("q_dram", (2, B, PARTS, P, P), BF16).ap(),
            "mask_dram": nc.dram_tensor("mask_dram", (B, P), BF16).ap(),
        }
        c["q1"] = Queries(nc, ctx, c)
        c["tokens"], c["inputs"] = Tokens(nc, ctx, c), Inputs(nc, ctx, c)
        context(nc, t, c)
        attention(nc, t, c, 0)
        experts(nc, t, c)
        attention(nc, t, c, 1)
        ternary_ffn(nc, t, c)


def context(nc, t, c):
    x_all, ident, identb, upper = c["x"], c["ident"], c["identb"], c["upper"]
    attn_w, k_rows, q_rows, ctx_t, mean, rstd = (c["attn_w"], c["k_rows"], c["q_rows"], c["ctx_t"], c["mean"], c["rstd"])
    with ExitStack() as ph:
        def sb(name, shape, dt):
            return ph.enter_context(nc.sbuf_tensor(name, shape, dt))

        def sem(name):
            return ph.enter_context(nc.semaphore(name))

        N = len(UNITS)
        xn, xn_t = sb("xn", [P, B, D], F32), sb("xn_t", [P, NG, GT], F32)
        full = sb("full", [P, N, GT], F32)
        rest = sb("rest", [P, N, GT], F32)
        parts = c["parts"]
        mask_i, mask_b = sb("mask_i", [B, P], I32), sb("mask_b", [B, P], BF16)
        one_rows = sb("one_rows", [H, SLOTS * P], BF16)
        tmp = sb("tmp", [P, B], F32)
        ps_p = ph.enter_context(nc.psum_tensor("ps_p", [P, 2, GT], F32))
        ps_x = ph.enter_context(nc.psum_tensor("ps_x", [P, 2, GT], F32))
        ps_v = ph.enter_context(nc.psum_tensor("ps_v", [P, 2, GT], F32))
        w_in = {m: sem(f"w{m}_in") for m in (0, 1, 2)}
        x_in, late_in, mask_in, bias_in, row_in = sem("x_in"), sem("late_in"), sem("mask_in"), sem("bias_in"), sem("row_in")
        ctx_in = [sem(f"ctx_in{g}") for g in range(NG)]
        made, consts, ones_ready, rows_clear, rows_set = (
            sem("made"), sem("consts"), sem("ones_ready"), sem("rows_clear"), sem("rows_set"))
        stats_ready, stats_step, mask_ready = sem("stats_ready"), sem("stats_step"), sem("mask_ready")
        xn_ready, t_done, xt_ready = sem("xn_ready"), sem("t_done"), sem("xt_ready")
        p_done, v_done, copied, rest_ready, split_step, v_ready = (
            sem("p_done"), sem("v_done"), sem("copied"), sem("rest_ready"), sem("split_step"), sem("v_ready"))
        first_stored, stored = sem("first_stored"), c["parts_stored"]
        block = ph.enter_context(nc.Block())

        @block.sync
        def _(sp):
            def load_ctx(g):
                sp.dma_start(ctx_t[:, g * GT:(g + 1) * GT], t["ctx_t"][:, g * GT:(g + 1) * GT]).then_inc(ctx_in[g], 16)

            def load_w(layer, m, signal):
                sp.dma_start(attn_w[:, layer, m, :], t[f"L{layer}_" + ("Wq", "Wk", "Wv", "Wo")[m]]).then_inc(signal, 16)

            load_w(0, 1, w_in[1])
            load_ctx(0)
            sp.dma_start(x_all[:], t["x"].rearrange("b s d -> s b d")).then_inc(x_in, 16)
            sp.dma_start(c["attn_bias"][:, 0:1], t["bq"]).then_inc(bias_in, 16)
            sp.dma_start(c["attn_bias"][:, 1:2], t["bk"]).then_inc(bias_in, 16)
            load_w(0, 2, w_in[2])
            load_ctx(1)
            for n, row in enumerate(("bv", "bo")):
                sp.dma_start(c["row_bias"][:, n, :], t[row].to_broadcast([P, D])).then_inc(row_in, 16)
            load_w(0, 0, w_in[0])
            load_ctx(2)
            load_ctx(3)
            sp.dma_start(mask_i[:], t["mask"]).then_inc(mask_in, 16)
            for layer, m in ((0, 3), (1, 0), (1, 1), (1, 2), (1, 3)):
                load_w(layer, m, late_in)
            sp.wait_ge(ones_ready, 1)
            sp.wait_ge(rows_clear, 3)
            for r in range(PARTS):
                sp.dma_start(k_rows[ROW_MAX + r:ROW_MAX + r + 1], one_rows[:]).then_inc(rows_set, 16)
            sp.dma_start(q_rows[ROW_MASK:ROW_MASK + 1], one_rows[:]).then_inc(rows_set, 16)
            for n in range(EARLY):
                sp.wait_ge(split_step, 2 * (n + 1))
                store_unit(sp, c, n, first_stored if UNITS[n][1] == 0 else stored)
                if UNITS[n] == ("q", 0):
                    sp.wait_ge(mask_ready, 1)
                    sp.dma_start(c["mask_dram"], mask_b[:]).then_inc(late_in, 16)
                    sp.wait_ge(first_stored, 16 * (K_PARTS + PARTS))
                    for b in range(AHEAD):
                        load_rows(sp, c, 0, b, b)
            sp.wait_ge(rows_set, 16 * (PARTS + 1))
            sp.wait_ge(late_in, 16 * (5 + 1))

        @block.gpsimd
        def _(pool):
            pool.memset(ident[:], 0.0).then_inc(made, 1)
            pool.memset(identb[:], 0.0).then_inc(made, 1)
            pool.memset(upper[:], 0.0).then_inc(made, 1)
            pool.memset(c["lower"][:], 0.0).then_inc(made, 1)
            pool.memset(c["half"][:], -0.5).then_inc(consts, 1)
            pool.memset(c["ones"][:], 1.0).then_inc(consts, 1)
            pool.memset(c["zero"][:], 0).then_inc(consts, 1)
            pool.wait_ge(made, 4)
            for tile in (ident, identb):
                pool.affine_select(out=tile[:], in_=tile[:], compare_op=ALU.not_equal, fill=1.0, base=0,
                                   pattern=[[-1, P]], channel_multiplier=1).then_inc(consts, 1)
            pool.affine_select(out=upper[:], in_=upper[:], compare_op=ALU.is_ge, fill=MASKED, base=0,
                               pattern=[[-1, P]], channel_multiplier=1).then_inc(consts, 1)
            pool.affine_select(out=c["lower"][:], in_=c["lower"][:], compare_op=ALU.is_ge, fill=MASKED, base=0,
                               pattern=[[1, P]], channel_multiplier=-1).then_inc(consts, 1)
            pool.memset(one_rows[:], 1.0).then_inc(ones_ready, 1)
            pool.memset(q_rows[:, 0:2].rearrange("p s h t -> p (s h t)").bitcast(U32), 0).then_inc(rows_clear, 1)
            pool.wait_ge(consts, 7)
            for n in range(N):
                for g in {1: (0, 1), 2: (2, 3)}.get(n, ()):
                    pool.wait_ge(stats_step, STAT_STEPS)
                    cols = slice(g * G, (g + 1) * G)
                    pool.tensor_tensor(rstd[:, cols], c["vareps"][:, cols], c["half"][:, cols], ALU.pow)\
                        .then_inc(stats_step, 1)
                pool.wait_ge(copied, 2 * (n + 1))
                pool.tensor_tensor(rest[:, n], full[:, n], parts[:, n, 0], ALU.subtract).then_inc(rest_ready, 1)

        @block.vector
        def _(dve):
            dve.memset(k_rows[:].rearrange("p s h t -> p (s h t)").bitcast(U32), 0).then_inc(rows_clear, 1)
            dve.memset(q_rows[:, 2:SLOTS].rearrange("p s h t -> p (s h t)").bitcast(U32), 0).then_inc(rows_clear, 1)
            dve.wait_ge(x_in, 16)
            for b in range(B):
                dve.bn_stats(c["st"][:, b, :], x_all[:, b, :]).then_inc(stats_ready, 1)
            dve.wait_ge(stats_ready, B)
            mean_and_variance(dve, stats_step, 0, c["st"], mean[:], c["vareps"][:, 0:B], tmp[:])

            def values(g):
                dve.wait_ge(v_done, g + 1)
                dve.wait_ge(row_in, 32)
                dve.tensor_tensor(c["v"][:, 0, g * G:(g + 1) * G, :], ps_v[:, g % 2, :].rearrange("p (b d) -> p b d", b=G),
                                  c["row_bias"][:, 0, :].unsqueeze(1).to_broadcast([P, G, D]), ALU.add)\
                   .then_inc(v_ready, 1)

            def normalise(g):
                dve.wait_ge(stats_step, STAT_STEPS + g + 1)
                for b in range(g * G, (g + 1) * G):
                    dve.tensor_scalar(xn[:, b, :], x_all[:, b, :], mean[:, b:b + 1], rstd[:, b:b + 1],
                                      ALU.subtract, ALU.mult).then_inc(xn_ready, 1)

            def split(n):
                dve.wait_ge(rest_ready, n + 1)
                dve.tensor_copy(parts[:, n, 1], rest[:, n]).then_inc(split_step, 1)
                dve.wait_ge(split_step, 2 * n + 1)
                dve.tensor_tensor(parts[:, n, 2], rest[:, n], parts[:, n, 1], ALU.subtract).then_inc(split_step, 1)

            values(0)
            split(0)
            normalise(0)
            dve.wait_ge(mask_in, 16)
            dve.tensor_scalar(mask_b[:], mask_i[:], 0, MASKED, ALU.is_equal, ALU.mult).then_inc(mask_ready, 1)
            normalise(1)
            values(1)
            split(1)
            normalise(2)
            split(2)
            values(2)
            normalise(3)
            split(3)
            split(4)
            values(3)
            split(5)
            split(6)
            split(7)

        @block.tensor
        def _(pe):
            def turn(g):
                pe.wait_ge(xn_ready, (g + 1) * G)
                wait(pe, xt_ready, g - 1)
                for j in range(G):
                    last = pe.transpose(ps_x[:, g % 2, j * P:(j + 1) * P], xn[:, g * G + j, :], ident[:])
                last.then_inc(t_done, 1)

            def values(g):
                wait(pe, v_ready, g - 1)
                for j in range(G):
                    last = pe.matmul(ps_v[:, g % 2, j * D:(j + 1) * D], ctx_t[:, (g * G + j) * P:(g * G + j + 1) * P],
                                     attn_w[:, 0, 2, :], start=True, stop=True)
                last.then_inc(v_done, 1)

            for n, (kind, g) in enumerate(UNITS):
                wait(pe, copied, 2 * (n - 1))
                if kind == "k":
                    if g == 0:
                        pe.wait_ge(w_in[1], 16)
                    pe.wait_ge(ctx_in[g], 16)
                    pe.matmul(ps_p[:, n % 2, :], attn_w[:, 0, 1, :], ctx_t[:, g * GT:(g + 1) * GT],
                              start=True, stop=True).then_inc(p_done, 1)
                    if g == 0:
                        pe.wait_ge(w_in[2], 16)
                    values(g)
                else:
                    if g == 0:
                        pe.wait_ge(consts, 7)
                        turn(0)
                        pe.wait_ge(w_in[0], 16)
                    if g + 1 < NG:
                        turn(g + 1)
                    pe.wait_ge(xt_ready, g + 1)
                    pe.matmul(ps_p[:, n % 2, :], attn_w[:, 0, 0, :], xn_t[:, g, :],
                              start=True, stop=True).then_inc(p_done, 1)

        @block.scalar
        def _(act):
            act.wait_ge(bias_in, 32)

            def copy_turned(g):
                act.wait_ge(t_done, g + 1)
                act.activation(xn_t[:, g, :], ps_x[:, g % 2, :], ACT.Copy).then_inc(xt_ready, 1)

            for n, (kind, g) in enumerate(UNITS):
                if kind == "q":
                    if g == 0:
                        copy_turned(0)
                    if g + 1 < NG:
                        copy_turned(g + 1)
                act.wait_ge(p_done, n + 1)
                bias = c["attn_bias"][:, 1:2] if kind == "k" else c["attn_bias"][:, 0:1]
                act.activation(parts[:, n, 0], ps_p[:, n % 2, :], ACT.Identity, bias=bias).then_inc(copied, 1)
                act.activation(full[:, n], ps_p[:, n % 2, :], ACT.Identity, bias=bias).then_inc(copied, 1)


def attention(nc, t, c, layer):
    x_all, ident, identb, attn_w = c["x"], c["ident"], c["identb"], c["attn_w"]
    k_rows, q_rows, rows_in = c["k_rows"], c["q_rows"], c["rows_in"][layer]
    with ExitStack() as ph:
        def sb(name, shape, dt):
            return ph.enter_context(nc.sbuf_tensor(f"{name}{layer}", shape, dt))

        def psum(name, shape, dt):
            return ph.enter_context(nc.psum_tensor(f"{name}{layer}", shape, dt))

        def sem(name):
            return ph.enter_context(nc.semaphore(f"{name}{layer}"))

        W = HQ * P
        VW = 32
        neg = sb("neg", [P, 2, H], F32)
        neg_rest = sb("neg_rest", [P, 2, H], F32)
        neg_parts = sb("neg_parts", [P, 2, P], BF16)
        neg_t = sb("neg_t", [PARTS * H, 2, P], BF16)
        probs = sb("probs", [P, NQ, W], F32)
        v_aug = sb("v_aug", [P, 2, H, VW], F32)
        o_t = sb("o_t", [P, 2, W], F32)
        inv = sb("inv", [P, 2, H], F32)
        o = sb("o", [P, 2, D], F32)
        oo_t = sb("oo_t", [P, 2, P], F32)
        ps_s = psum("ps_s", [P, 2, W], F32)
        ps_e = psum("ps_e", [P, 2, W], F32)
        ps_v = psum("ps_pv", [P, W], F32)
        ps_o = psum("ps_o", [P, W], F32)
        ps_n = psum("ps_n", [P, 2 * W], BF16)
        ps_y = psum("ps_y", [P, W], F32)

        bias_added, gate_in = sem("bias_added"), sem("gate_in")
        scored, max_done, neg_step, neg_ready = sem("scored"), sem("max_done"), sem("neg_step"), sem("neg_ready")
        negt_done, negt_ready = sem("negt_done"), sem("negt_ready")
        neg_laid = [sem(f"neg_laid{r}_") for r in range(SLOTS)]
        shifted, exp_done, pv_done, vaug_ready = (
            sem("shifted"), sem("exp_done"), sem("pv_done"), sem("vaug_ready"))
        ot_ready, ot_back, o_step = sem("ot_ready"), sem("ot_back"), sem("o_step")
        oot_done, oot_ready, y_done, x_ready = sem("oot_done"), sem("oot_ready"), sem("y_done"), sem("x_ready")
        st_ready, cleared, row_clear = sem("st_ready"), sem("cleared"), sem("row_clear")
        n_loads = 2 if layer == 0 else 3
        block = ph.enter_context(nc.Block())

        queries, last = c["q1"], NG - 1
        also = layer == 1
        inputs = c["tokens"] if layer == 0 else c["inputs"]

        def run(eng, step, after, beside=None):
            for b in range(-3, 2 + SLOTS):
                if b > -3:
                    step(b, b % SLOTS)
                if b in after:
                    after[b]()
            with eng.Fori(1, (B - 4) // SLOTS) as i:
                for j in range(SLOTS):
                    if beside:
                        beside(j, i - 1)
                    step(i * SLOTS + (2 + j), (2 + j) % SLOTS)
            for b in range(B - 2, B + 2):
                if beside:
                    beside(b - (B - 2), NG - 2)
                step(b, b % SLOTS)

        @block.sync
        def _(sp):
            def lay_maxima(b, r):
                wait(sp, negt_ready, b + 1)
                sp.dma_start(q_rows[ROW_MAX:ROW_MASK, r], neg_t[:, r % 2, :]).then_inc(neg_laid[r], 16)

            def load(b, r):
                sp.wait_ge(shifted, (b - SLOTS + 1) * NQ)
                load_rows(sp, c, layer, b, r)
                lay_maxima(b - 2, (r - 2) % SLOTS)

            if layer == 1:
                queries.store(sp, last - 1, queries.stored[2])
            if layer == 0:
                for b in range(AHEAD, SLOTS):
                    load_rows(sp, c, 0, b, b)
                store_unit(sp, c, LATE[0], c["parts_stored"])
            for b in range(2):
                lay_maxima(b, b)
                if layer == 0:
                    store_unit(sp, c, LATE[1 + b], c["late_stored"])
            if layer == 0:
                sp.wait_ge(c["parts_stored"], 16 * (K_PARTS + PARTS))
            else:
                sp.wait_ge(queries.stored[1], 16 * PARTS)
            for b in range(SLOTS, 2 * SLOTS):
                load(b, b % SLOTS)
                if layer == 0 and b < SLOTS + 2:
                    store_unit(sp, c, LATE[3 + b - SLOTS], c["last_stored"])
                if layer == 1 and b == SLOTS + 2:
                    queries.store(sp, last, queries.stored[2])
            if layer == 0:
                sp.wait_ge(c["late_stored"], 16 * (K_PARTS + PARTS))
            else:
                sp.wait_ge(queries.stored[2], 16 * PARTS * 2)
            with sp.Fori(2, B // SLOTS) as i:
                for r in range(SLOTS):
                    load(i * SLOTS + r, r)
                    if layer == 0:
                        e = bass.ds(i * SLOTS + (r - 2 * SLOTS), 1)
                        sp.dma_start(c["w1"][:, e, :], t["w1"][:, e, :]).then_inc(c["weights_in"], 16)
                        sp.dma_start(c["w2"][:, e], t["w2"][:, e]).then_inc(c["weights_in"], 16)
                if layer == 0:
                    sp.wait_ge(c["last_stored"], 16 * (K_PARTS + PARTS))
            for b in range(B - 2, B):
                lay_maxima(b, b % SLOTS)
            if layer == 0:
                for key in ("gate_w", "norm_w", "b1", "b2"):
                    sp.dma_start(c[key][:], t[key]).then_inc(gate_in, 16)
                for n, key in enumerate(("w_gate", "w_up")):
                    sp.dma_start(c["ffn_w"][:, n, :], t[key]).then_inc(c["weights_in"], 16)
                sp.dma_start(c["ffn_w"][:, 2, :].rearrange("p (k o) -> p k o", k=FK), t["w_down"])\
                  .then_inc(c["weights_in"], 16)
                sp.wait_ge(gate_in, 16 * 4)

        @block.tensor
        def _(pe):
            def scores(b, q, r):
                n = b * NQ + q
                if q == 0:
                    wait(pe, rows_in[r], of_slot(b, r, SLOTS, 16 * n_loads))
                    wait(pe, row_clear, b - SLOTS + 1)
                wait(pe, max_done, n - 1)
                if layer == 1:
                    pe.matmul(ps_s[:, q % 2, :], identb[:], c["upper"][:].unsqueeze(1).to_broadcast([P, HQ, P]),
                              start=True, stop=False, skip_group_check=True)
                for j in range(HQ):
                    h = q * HQ + j
                    last = pe.matmul(ps_s[:, q % 2, j * P:(j + 1) * P], q_rows[:, r, h, :], k_rows[:, r, h, :],
                                     start=(layer == 0), stop=True, skip_group_check=True)
                last.then_inc(scored, 1)

            def shifted_scores(b, q, r):
                n = b * NQ + q
                if q == 0:
                    wait(pe, neg_laid[r], of_slot(b, r, SLOTS, 16))
                wait(pe, exp_done, n - 1)
                if layer == 1:
                    pe.matmul(ps_e[:, q % 2, :], identb[:], c["lower"][:].unsqueeze(1).to_broadcast([P, HQ, P]),
                              start=True, stop=False, skip_group_check=True)
                for j in range(HQ):
                    h = q * HQ + j
                    last = pe.matmul(ps_e[:, q % 2, j * P:(j + 1) * P], k_rows[:, r, h, :], q_rows[:, r, h, :],
                                     start=(layer == 0), stop=True, skip_group_check=True)
                last.then_inc(shifted, 1)

            def values(b, q, s):
                n = b * NQ + q
                if q == 0:
                    wait(pe, vaug_ready, b + 1)
                    wait(pe, ot_ready, b)
                wait(pe, exp_done, n + 1)
                for j in range(HQ):
                    last = pe.matmul(ps_v[VW * j:VW * (j + 1), q * P:(q + 1) * P], v_aug[:, s, q * HQ + j, :],
                                     probs[:, q, j * P:(j + 1) * P], start=True, stop=True)
                last.then_inc(pv_done, 1)

            def turn_maxima(b, s):
                wait(pe, neg_ready, b + 1)
                wait(pe, negt_ready, b)
                pe.transpose(ps_n[:, 0:P], neg_parts[:, s, :], identb[:]).then_inc(negt_done, 1)

            def turn_back(b, s):
                wait(pe, ot_ready, b + 1)
                wait(pe, o_step, 2 * b)
                for q in range(NQ):
                    last = pe.transpose(ps_o[:, q * P:(q + 1) * P], o_t[:, s, q * P:(q + 1) * P], ident[:])
                last.then_inc(ot_back, 1)

            def turn_output(b, s):
                if also and isinstance(b, int) and b == 0:
                    pe.wait_ge(queries.copied, 2 * NG)
                wait(pe, o_step, 2 * b + 2)
                wait(pe, x_ready, b)
                pe.transpose(ps_y[:, 0:P], o[:, s, :], ident[:]).then_inc(oot_done, 1)

            def project(b, s):
                wait(pe, oot_ready, b + 1)
                pe.matmul(ps_y[:, P:2 * P], oo_t[:, s, :], attn_w[:, layer, 3, :], start=True, stop=True)\
                  .then_inc(y_done, 1)

            def step(b, r):
                s = r % 2
                for q in range(NQ):
                    if exists(b + 2):
                        scores(b + 2, q, (r + 2) % SLOTS)
                    if q == 0 and exists(b - 1):
                        values(b - 1, NQ - 1, 1 - s)
                    if exists(b):
                        shifted_scores(b, q, r)
                    if q == 1 and exists(b - 2):
                        turn_output(b - 2, s)
                    if q > 0 and exists(b):
                        values(b, q - 1, s)
                    if q == 1 and exists(b + 1):
                        turn_maxima(b + 1, 1 - s)
                    if q == 2 and exists(b - 2):
                        project(b - 2, s)
                    if q == 2 and exists(b - 1):
                        turn_back(b - 1, 1 - s)

            run(pe, step, {0: lambda: queries.turn(pe, last, ps_y[:]),
                           1: lambda: queries.project(pe, last, ps_y[:])} if also else {})

        @block.vector
        def _(dve):
            dve.wait_ge(cleared, 1)

            def maxima(b, q, s):
                n = b * NQ + q
                wait(dve, scored, n + 1)
                dve.tensor_reduce(neg[:, s, q * HQ:(q + 1) * HQ], ps_s[:, q % 2, :].rearrange("p (h k) -> p h k", h=HQ),
                                  AX_X, ALU.max, negate=True).then_inc(max_done, 1)

            def split(b, s):
                ch = Chain(dve, neg_step, b * 3)
                wait(dve, max_done, (b + 1) * NQ)
                ch.step(dve.tensor_copy(neg_parts[:, s, 0:H], neg[:, s, :]))
                ch.settle()
                ch.step(dve.tensor_tensor(neg_rest[:, s, :], neg[:, s, :], neg_parts[:, s, 0:H], ALU.subtract))
                ch.settle()
                ch.step(dve.tensor_copy(neg_parts[:, s, H:2 * H], neg_rest[:, s, :]))
                ch.settle()
                dve.tensor_tensor(neg_parts[:, s, 2 * H:3 * H], neg_rest[:, s, :], neg_parts[:, s, H:2 * H],
                                  ALU.subtract).then_inc(neg_ready, 1)

            def normalise_output(b, s):
                wait(dve, ot_back, b + 1)
                heads = ps_o[:].rearrange("p (h c) -> p h c", h=H)
                dve.reciprocal(inv[:, s, :], heads[:, :, DK]).then_inc(o_step, 1)
                wait(dve, o_step, 2 * b + 1)
                dve.tensor_tensor(o[:, s, :].rearrange("p (h d) -> p h d", h=H), heads[:, :, 0:DK],
                                  inv[:, s, :].unsqueeze(2).to_broadcast([P, H, DK]), ALU.mult).then_inc(o_step, 1)

            def residual(b):
                wait(dve, y_done, b + 1)
                dve.tensor_tensor(batch_of(x_all, b), ps_y[:, P:2 * P], batch_of(x_all, b), ALU.add).then_inc(x_ready, 1)

            def stats(b):
                dve.bn_stats(batch_of(c["st"], b), batch_of(x_all, b)).then_inc(st_ready, 1)

            piece = []

            def step(b, r):
                s = r % 2
                for q in range(NQ):
                    if q == 3 and exists(b - 2):
                        residual(b - 2)
                        wait(dve, x_ready, b - 1)
                    if q == 3 and piece and layer == 0:
                        piece[0](1)
                    if exists(b + 2):
                        maxima(b + 2, q, s)
                    if q == 3 and exists(b - 2):
                        stats(b - 2)
                    if q == 3 and exists(b - 1):
                        normalise_output(b - 1, 1 - s)
                    if q == 2 and piece and layer == 0:
                        piece[0](0)
                    if q < 3 and piece and layer == 1:
                        piece[0](q)
                piece.clear()
                if exists(b + 2):
                    split(b + 2, s)

            def measure_queries():
                piece[:] = [lambda q: queries.stats(dve, last, ((0, 1), (2, 3))[q]) if q < 2
                            else queries.variance(dve, last)]

            def normalise_queries():
                piece[:] = [lambda q: queries.normalise(dve, last, ((0, 1), (2, 3))[q]) if q < 2 else None]

            def beside(j, g):
                if j == 0:
                    wait(dve, st_ready, (g + 1) * G)
                piece[:] = [lambda q: inputs.piece(dve, g, (2 if layer == 0 else 3) * j + q)]

            run(dve, step, {-2: measure_queries, -1: normalise_queries, 2: lambda: queries.split(dve, last)} if also
                else {1: lambda: dve.wait_ge(bias_added, 1)}, beside)

        @block.scalar
        def _(act):
            def exponentials(b, q):
                n = b * NQ + q
                wait(act, shifted, n + 1)
                wait(act, pv_done, n - NQ + 1)
                act.activation(probs[:, q, :], ps_e[:, q % 2, :], ACT.Exp, scale=SCALE).then_inc(exp_done, 1)

            def copy_sums(b, s):
                wait(act, pv_done, (b + 1) * NQ)
                act.activation(o_t[:, s, :], ps_v[:], ACT.Copy).then_inc(ot_ready, 1)

            def copy_maxima(b, r):
                s = r % 2
                wait(act, negt_done, b + 1)
                wait(act, neg_laid[(r - 2) % SLOTS], of_slot(b - 2, (r - 2) % SLOTS, SLOTS, 16))
                act.activation(neg_t[:, s, :], ps_n[0:PARTS * H, 0:P], ACT.Copy).then_inc(negt_ready, 1)

            def copy_output(b, s):
                wait(act, oot_done, b + 1)
                act.activation(oo_t[:, s, :], ps_y[:, 0:P], ACT.Copy).then_inc(oot_ready, 1)

            def step(b, r):
                s = r % 2
                for q in range(NQ):
                    if q == 0 and exists(b - 1):
                        copy_sums(b - 1, 1 - s)
                    if exists(b):
                        exponentials(b, q)
                    if q == 1 and exists(b - 2):
                        copy_output(b - 2, s)
                    if q == 1 and exists(b + 1):
                        copy_maxima(b + 1, (r + 1) % SLOTS)

            run(act, step, {0: lambda: queries.copy_turned(act, last, ps_y[:]),
                            1: lambda: queries.copy(act, last, ps_y[:])} if also else {})

        @block.gpsimd
        def _(pool):
            pool.memset(neg_parts[:], 0.0).then_inc(cleared, 1)
            pool.memset(v_aug[:], 0.0).then_inc(cleared, 1)
            pool.wait_ge(cleared, 2)
            pool.memset(v_aug[:, :, :, DK:DK + 1], 1.0).then_inc(cleared, 1)
            pool.wait_ge(cleared, 3)

            def fill(b, s):
                wait(pool, pv_done, (b - 1) * NQ)
                wait(pool, row_clear, b - 2)
                pool.tensor_copy(v_aug[:, s, :, 0:DK],
                                 c["v"][:, layer, bass.ds(b, 1), :].rearrange("p b (h d) -> p (b h) d", h=H))\
                    .then_inc(vaug_ready, 1)

            def clear_maxima(b, r):
                wait(pool, vaug_ready, b + 3 if exists(b + 2) else B)
                zeros = c["zero"][ROW_MAX:ROW_MASK, 0:1].to_broadcast([PARTS, H * P // 2])
                pool.tensor_tensor(q_rows[ROW_MAX:ROW_MASK, r].rearrange("p h t -> p (h t)").bitcast(I32), zeros, zeros,
                                   ALU.add).then_inc(row_clear, 1)

            def step(b, r):
                if exists(b + 1):
                    fill(b + 1, 1 - r % 2)
                if exists(b - 1) and exists(b + 1):
                    clear_maxima(b - 1, (r - 1) % SLOTS)

            def add_bias():
                pool.wait_ge(row_clear, 1)
                pool.tensor_tensor(x_all[:], x_all[:], c["row_bias"][:, 1, :].unsqueeze(1).to_broadcast([P, B, D]),
                                   ALU.add).then_inc(bias_added, 1)
                pool.wait_ge(bias_added, 1)

            def leave_queries():
                pool.wait_ge(row_clear, 1)
                queries.leave(pool, last)

            def beside(j, g):
                if j == (2 if layer == 0 else 1):
                    wait(pool, row_clear, B - 2 if isinstance(g, int) else (g + 1) * G + 1 + j)
                    inputs.root(pool, g)
                    wait(pool, inputs.stats_step, (g + 1) * (Tokens.STEPS if layer == 0 else STAT_STEPS + 1))

            run(pool, step, {-1: lambda: queries.root(pool, last), 1: leave_queries} if also else {1: add_bias}, beside)


def experts(nc, t, c):
    x_all, ident = c["x"], c["ident"]
    attn_w, ctx_t, w1, w2, ffn_w = c["attn_w"], c["ctx_t"], c["w1"], c["w2"], c["ffn_w"]
    gate_w, norm_w, b1, b2 = c["gate_w"], c["norm_w"], c["b1"], c["b2"]
    with ExitStack() as ph:
        def sb(name, shape, dt):
            return ph.enter_context(nc.sbuf_tensor(name, shape, dt))

        def sem(name):
            return ph.enter_context(nc.semaphore(name))

        wtmp = sb("wtmp", [P, 3, F], F32)
        wsum, winv = sb("wsum", [P, 3], F32), sb("winv", [P, 3], F32)
        tok_t = sb("tok_t", [P, T], F32)
        rank_i, rank = sb("rank_i", [P, E], I32), sb("rank", [P, E], F32)
        tokens = c["tokens"]
        tk, tk_ready = tokens.tk, tokens.tk_ready
        k_full, k_rest, k_parts = sb("k1_full", [P, NG, GT], F32), sb("k1_rest", [P, NG, GT], F32), c["parts"][:, 0:NG]
        logits, second = sb("logits", [P, B, E], F32), sb("second", [P, B, E], F32)
        best, eq, score = sb("best", [P, 2, B], F32), sb("eq", [P, 2, B, E], F32), sb("score", [P, 2, B, E], F32)
        mark, sel = sb("mark", [P, 2, B], F32), sb("sel", [P, 2, B, E], F32)
        diff, ex, den, wt = sb("diff", [P, B], F32), sb("ex", [P, B], F32), sb("den", [P, B], F32), sb("wt", [P, 2, B], F32)
        lg_t = sb("lg_t", [E, NG, GT], F32)
        comb = sb("comb", [P, B, E], F32)
        hid = sb("hid", [P, 2 * M, GT], F32)
        c_g, c_t = sb("c_g", [P, G, E], F32), sb("c_t", [E, GT], F32)
        ps_h = ph.enter_context(nc.psum_tensor("ps_h", [P, 2, GT], F32))
        ps_y = ph.enter_context(nc.psum_tensor("ps_ym", [P, 2, GT], F32))
        ps_c = ph.enter_context(nc.psum_tensor("ps_c", [P, GT], F32))
        ps_b = ph.enter_context(nc.psum_tensor("ps_b", [P, GT], F32))
        ps_g = ph.enter_context(nc.psum_tensor("ps_g", [P, GT], F32))
        ps_q = ph.enter_context(nc.psum_tensor("ps_q", [P, GT], F32))
        x_added, rank_ready, lg_done, lg_ready = sem("x_added"), sem("rank_ready"), sem("lg_done"), sem("lg_ready")
        k_done, k_copied, k_rest_ready, k_split, k_stored, v_done, v_ready = (
            sem("k1_done"), sem("k1_copied"), sem("k1_rest"), sem("k1_split"), sem("k1_stored"), sem("v1_done"), sem("v1_ready"))
        t_done, tok_ready, g_done, top_step, diff_ready, ex_ready = (
            sem("t_done_m"), sem("tok_ready"), sem("g_done"), sem("top_step"), sem("diff_ready"), sem("ex_ready"))
        wsum_ready, sums_done, quant_step = sem("wsum_ready"), sem("sums_done"), sem("quant_step")
        h_done, h_ready, y_done, y_read = sem("h_done"), sem("h_ready"), sem("y_done_m"), sem("y_read")
        cg_ready, ct_done, ct_ready, b_done, b_read = (
            sem("cg_ready"), sem("ct_done"), sem("ct_ready"), sem("b_done"), sem("b_read"))
        queries = c["q1"]
        block = ph.enter_context(nc.Block())

        lent = (ps_q, ps_c)

        @block.sync
        def _(sp):
            for g in range(NG):
                sp.wait_ge(k_split, 2 * (g + 1))
                store_parts(sp, c["k_dram"][1], g * G, k_parts[:, g], K_PARTS, k_stored)

            queries.store(sp, 0, queries.stored[0])
            sp.wait_ge(k_stored, 16 * K_PARTS * NG)
            sp.wait_ge(queries.stored[0], 16 * PARTS)
            for b in range(SLOTS):
                load_rows(sp, c, 1, b, b)
            queries.store(sp, 1, queries.stored[1])

        @block.gpsimd
        def _(pool):
            pool.iota(rank_i[:], pattern=[[-1, E]], base=E, channel_multiplier=0).then_inc(rank_ready, 1)
            pool.wait_ge(rank_ready, 1)
            pool.tensor_copy(rank[:], rank_i[:]).then_inc(rank_ready, 1)
            tokens.root(pool, NG - 1)
            for g in range(NG):
                pool.wait_ge(k_copied, 2 * (g + 1))
                pool.tensor_tensor(k_rest[:, g], k_full[:, g], k_parts[:, g, 0], ALU.subtract).then_inc(k_rest_ready, 1)

            with pool.Fori(0, NG - 1) as g:
                queries.root(pool, g)
                queries.leave(pool, g)

        @block.vector
        def _(dve):
            tokens.variance(dve, NG - 1)
            tokens.square(dve, NG - 1)
            tokens.normalise(dve, NG - 1)
            tokens.scales(dve)
            dve.wait_ge(c["weights_in"], 16 * WEIGHT_LOADS)
            for n in range(3):
                dve.tensor_reduce(wsum[:, n:n + 1], ffn_w[:, n, :], AX_X, ALU.add,
                                  apply_absolute_value=True).then_inc(wsum_ready, 1)

            dve.wait_ge(tk_ready, B + 2)
            for b in range(B):
                dve.tensor_scalar(x_all[:, b, :], x_all[:, b, :], tokens.x_scl[:, b:b + 1], tokens.x_off[:, b:b + 1],
                                  ALU.mult, ALU.add).then_inc(x_added, 1)

            ch = Chain(dve, top_step, 0)
            dve.wait_ge(g_done, 1)
            dve.wait_ge(rank_ready, 2)
            ch.step(dve.tensor_copy(logits[:].rearrange("p b e -> p (b e)"), ps_g[:, 0:B * E]))
            ch.settle()
            rank_b = rank[:].unsqueeze(1).to_broadcast([P, B, E])
            for n, lg in enumerate((logits, second)):
                ch.step(dve.tensor_reduce(best[:, n, :], lg[:], AX_X, ALU.max))
                ch.settle()
                ch.step(dve.tensor_tensor(eq[:, n], lg[:], best[:, n, :].unsqueeze(2).to_broadcast([P, B, E]), ALU.is_equal))
                ch.settle()
                ch.step(dve.tensor_tensor(score[:, n], eq[:, n], rank_b, ALU.mult))
                ch.settle()
                ch.step(dve.tensor_reduce(mark[:, n, :], score[:, n], AX_X, ALU.max))
                ch.settle()
                ch.step(dve.tensor_tensor(sel[:, n], rank_b, mark[:, n, :].unsqueeze(2).to_broadcast([P, B, E]), ALU.is_equal))
                ch.settle()
                if n == 0:
                    ch.step(dve.scalar_tensor_tensor(out=second[:], in0=sel[:, 0], scalar=-3e38, in1=logits[:],
                                                     op0=ALU.mult, op1=ALU.add))
                    ch.settle()
            dve.tensor_tensor(diff[:], best[:, 1, :], best[:, 0, :], ALU.subtract).then_inc(diff_ready, 1)
            dve.wait_ge(ex_ready, 1)
            ch.step(dve.tensor_scalar(den[:], ex[:], 1.0, None, ALU.add))
            ch.settle()
            ch.step(dve.reciprocal(wt[:, 0, :], den[:]))
            ch.settle()
            ch.step(dve.tensor_tensor(wt[:, 1, :], ex[:], wt[:, 0, :], ALU.mult))
            ch.settle()
            for n in range(2):
                ch.step(dve.tensor_tensor(sel[:, n], sel[:, n], wt[:, n, :].unsqueeze(2).to_broadcast([P, B, E]), ALU.mult))
            ch.settle()
            ch.step(dve.tensor_tensor(comb[:], sel[:, 0], sel[:, 1], ALU.add))
            ch.settle()
            dve.wait_ge(x_added, B)

            def split_keys(g):
                dve.wait_ge(k_rest_ready, g + 1)
                dve.tensor_copy(k_parts[:, g, 1], k_rest[:, g]).then_inc(k_split, 1)
                dve.wait_ge(k_split, 2 * g + 1)
                dve.tensor_tensor(k_parts[:, g, 2], k_rest[:, g], k_parts[:, g, 1], ALU.subtract).then_inc(k_split, 1)

            def group(g, first=False):
                wait(dve, y_read, g * E * G)
                wait(dve, ct_done, g)
                dve.tensor_copy(c_g[:], comb[:, bass.ds(g * G, G), :]).then_inc(cg_ready, 1)
                if not first:
                    queries.stats(dve, g - 1)
                dve.wait_ge(cg_ready, g + 1)
                for e in range(E):
                    n = g * E + e
                    dve.wait_ge(y_done, n + 1)
                    for j in range(G):
                        wait(dve, y_read, (n - 1) * G + j + 1)
                        dve.scalar_tensor_tensor(out=batch_of(x_all, g * G + j), in0=ps_y[:, e % 2, j * D:(j + 1) * D],
                                                 scalar=c_g[:, j, e:e + 1], in1=batch_of(x_all, g * G + j),
                                                 op0=ALU.mult, op1=ALU.add).then_inc(y_read, 1)
                    if e == 3:
                        dve.wait_ge(b_done, g + 1)
                        dve.wait_ge(y_read, (n + 1) * G)
                        x_g = x_all[:, bass.ds(g * G, G), :]
                        dve.tensor_tensor(x_g, ps_b[:].rearrange("p (j d) -> p j d", j=G), x_g, ALU.add).then_inc(b_read, 1)
                        dve.wait_ge(b_read, g + 1)
                    if first and e == 0:
                        dve.wait_ge(sums_done, 1)
                        qs.step(dve.tensor_scalar(c["w_scale"][:], ps_b[:, 0:3], 1.0 / (D * F), 1e-5, ALU.mult, ALU.max))
                    if first and e >= E - NG:
                        split_keys(e - (E - NG))
                    if not first:
                        if e == 0:
                            queries.variance(dve, g - 1)
                        if e == 2:
                            queries.normalise(dve, g - 1)
                        if e == E - 2:
                            queries.split(dve, g - 1)

            qs = Chain(dve, quant_step, 0)
            group(0, first=True)
            qs.settle()
            qs.step(dve.reciprocal(winv[:], c["w_scale"][:]))
            qs.settle()
            for n in range(3):
                qs.step(dve.tensor_scalar(wtmp[:, n, :], ffn_w[:, n, :], winv[:, n:n + 1], 1.0, ALU.mult, ALU.min))
            qs.settle()
            qs.step(dve.tensor_scalar(wtmp[:], wtmp[:], -1.0, MAGIC, ALU.max, ALU.add))
            qs.settle()
            qs.step(dve.tensor_scalar(c["ffn_wq"][:], wtmp[:], -MAGIC, None, ALU.add))
            with dve.Fori(1, NG) as g:
                group(g)

        @block.tensor
        def _(pe):

            def context_group(g):
                pe.matmul(ps_q[:], attn_w[:, 1, 1, :], ctx_t[:, g * GT:(g + 1) * GT], start=True, stop=True)\
                  .then_inc(k_done, 1)
                for j in range(G):
                    last = pe.matmul(ps_c[:, j * D:(j + 1) * D], ctx_t[:, (g * G + j) * P:(g * G + j + 1) * P],
                                     attn_w[:, 1, 2, :], start=True, stop=True)
                last.then_inc(v_done, 1)

            def turn_tokens(g):
                pe.wait_ge(tk_ready, (g + 1) * G)
                wait(pe, tok_ready, g - 1)
                for j in range(G):
                    last = pe.transpose(lent[g % 2][:, j * P:(j + 1) * P], tk[:, g * G + j, :], ident[:])
                last.then_inc(t_done, 1)

            def gate(g):
                pe.wait_ge(tok_ready, g + 1)
                wait(pe, lg_ready, g - 1)
                pe.matmul(ps_y[0:E, g % 2, :], gate_w[:], tok_t[:, g * GT:(g + 1) * GT], start=True, stop=True)\
                  .then_inc(lg_done, 1)

            def turn_logits(g):
                pe.wait_ge(lg_ready, g + 1)
                for j in range(G):
                    b = g * G + j
                    last = pe.transpose(ps_g[:, b * E:(b + 1) * E], lg_t[:, g, j * P:(j + 1) * P], ident[0:E, 0:E])
                return last

            def hidden(g, e):
                for m in range(M):
                    n = g * (E * M) + e * M + m
                    wait(pe, h_ready, n - 1)
                    pe.matmul(ps_h[:, m, :], w1[:, e, m * P:(m + 1) * P], tok_t[:, bass.ds(g * GT, GT)],
                              start=True, stop=True).then_inc(h_done, 1)

            def out(g, e):
                n = g * E + e
                pe.wait_ge(h_ready, (n + 1) * M)
                wait(pe, y_read, (n - 1) * G)
                for j in range(G):
                    for m in range(M):
                        last = pe.matmul(ps_y[:, e % 2, j * D:(j + 1) * D],
                                         hid[:, (e % 2) * M + m, j * P:(j + 1) * P], w2[:, e, m, :],
                                         start=(m == 0), stop=(m == M - 1))
                last.then_inc(y_done, 1)

            def turn_weights(g):
                pe.wait_ge(cg_ready, g + 1)
                wait(pe, ct_ready, g)
                for j in range(G):
                    last = pe.transpose(ps_c[0:E, j * P:(j + 1) * P], c_g[:, j, :], ident[:])
                last.then_inc(ct_done, 1)

            def bias(g):
                pe.wait_ge(ct_ready, g + 1)
                wait(pe, b_read, g)
                for j in range(G):
                    last = pe.matmul(ps_b[:, j * D:(j + 1) * D], c_t[:, j * P:(j + 1) * P], b2[:],
                                     start=True, stop=True)
                last.then_inc(b_done, 1)

            turn_tokens(0)
            turn_tokens(1)
            pe.wait_ge(tok_ready, 1)
            pe.wait_ge(c["weights_in"], 16 * WEIGHT_LOADS)
            hidden(0, 0)
            gate(0)
            gate(1)
            turn_tokens(2)
            turn_tokens(3)
            gate(2)
            gate(3)
            for g in range(NG):
                last = turn_logits(g)
            last.then_inc(g_done, 1)

            def group(g, first=False):
                if not first:
                    hidden(g, 0)
                for e in range(E):
                    if e + 1 < E:
                        hidden(g, e + 1)
                    if first and e == 0:
                        context_group(0)
                        pe.wait_ge(wsum_ready, 3)
                        pe.matmul(ps_b[:, 0:3], c["ones"][:], wsum[:], start=True, stop=True).then_inc(sums_done, 1)
                    if e == 2:
                        if first:
                            pe.wait_ge(v_ready, 1)
                        turn_weights(g)
                    if e == 3:
                        if first:
                            pe.wait_ge(quant_step, 1)
                        bias(g)
                    out(g, e)
                    if first and 3 <= e < 3 + NG - 1:
                        if e == 3:
                            pe.wait_ge(ct_ready, 1)
                        pe.wait_ge(k_copied, 2 * (e - 2))
                        pe.wait_ge(v_ready, e - 2)
                        context_group(e - 2)
                    if not first:
                        if e == 3:
                            queries.turn(pe, g - 1, ps_c[:])
                        if e == 4:
                            queries.project(pe, g - 1, ps_q[:])

            group(0, first=True)
            pe.wait_ge(k_copied, 2 * NG)
            pe.wait_ge(v_ready, NG)
            with pe.Fori(1, NG) as g:
                group(g)

        @block.scalar
        def _(act):

            def copy_context(g):
                act.wait_ge(k_done, g + 1)
                act.activation(k_parts[:, g, 0], ps_q[:], ACT.Copy).then_inc(k_copied, 1)
                act.activation(k_full[:, g], ps_q[:], ACT.Copy).then_inc(k_copied, 1)
                act.wait_ge(v_done, g + 1)
                act.activation(c["v"][:, 1, g * G:(g + 1) * G, :].rearrange("p b d -> p (b d)"), ps_c[:], ACT.Copy)\
                   .then_inc(v_ready, 1)

            def copy_tokens(g):
                act.wait_ge(t_done, g + 1)
                act.activation(tok_t[:, g * GT:(g + 1) * GT], lent[g % 2][:], ACT.Copy, scale=norm_w[:, 0:1])\
                   .then_inc(tok_ready, 1)

            def copy_logits(g):
                act.wait_ge(lg_done, g + 1)
                act.activation(lg_t[:, g], ps_y[0:E, g % 2, :], ACT.Copy).then_inc(lg_ready, 1)

            def activate(g, e):
                for m in range(M):
                    n = g * (E * M) + e * M + m
                    act.wait_ge(h_done, n + 1)
                    wait(act, y_done, g * E + e - 1)
                    act.activation(hid[:, (e % 2) * M + m, :], ps_h[:, m, :], ACT.Gelu,
                                   bias=b1[:, e * M + m:e * M + m + 1]).then_inc(h_ready, 1)

            copy_tokens(0)
            copy_tokens(1)
            activate(0, 0)
            copy_logits(0)
            copy_logits(1)
            copy_tokens(2)
            copy_tokens(3)
            copy_logits(2)
            copy_logits(3)
            activate(0, 1)
            copy_context(0)
            act.wait_ge(diff_ready, 1)
            act.activation(ex[:], diff[:], ACT.Exp).then_inc(ex_ready, 1)

            def group(g, first=False):
                for e in range(E):
                    if not (first and e < 2):
                        activate(g, e)
                    if e == 2:
                        act.wait_ge(ct_done, g + 1)
                        wait(act, b_done, g)
                        act.activation(c_t[:], ps_c[0:E, :], ACT.Copy).then_inc(ct_ready, 1)
                    if first and 4 <= e < 4 + NG - 1:
                        copy_context(e - 3)
                    if not first:
                        if e == 4:
                            queries.copy_turned(act, g - 1, ps_c[:])
                        if e == 5:
                            queries.copy(act, g - 1, ps_q[:])

            group(0, first=True)
            with act.Fori(1, NG) as g:
                group(g)


def ternary_ffn(nc, t, c):
    x_all, ident, inputs = c["x"], c["ident"], c["inputs"]
    with ExitStack() as ph:
        def sb(name, shape, dt):
            return ph.enter_context(nc.sbuf_tensor(name, shape, dt))

        def sem(name):
            return ph.enter_context(nc.semaphore(name))

        xr = sb("xr", [P, B, D], F32)
        magic = sb("magic", [P, 2], F32)
        xq_t = sb("xq_t", [P, B, P], BF16)
        gate, gu, gr = sb("gate", [P, 2, F], F32), sb("gu", [P, 2, F], F32), sb("gr", [P, 2, F], F32)
        g_max, g_scl = sb("g_max", [P, 4], F32), sb("g_scl", [P, 4, 4], F32)
        gq_t = sb("gq_t", [P, 2, F], BF16)
        ps_t = ph.enter_context(nc.psum_tensor("ps_tf", [P, 2, F], F32))
        ps_g = ph.enter_context(nc.psum_tensor("ps_gf", [P, 2, F], F32))
        ps_u = ph.enter_context(nc.psum_tensor("ps_uf", [P, 2, F], F32))
        ps_d = ph.enter_context(nc.psum_tensor("ps_df", [P, 2, F], F32))
        magic_ready = sem("magic_ready")
        fma_ready, clamp_ready, xt_done, xt_ready = (
            sem("fma_ready"), sem("clamp_ready"), sem("xt_done_f"), sem("xt_ready_f"))
        gu_done, gate_ready, gu_ready, gmax_ready, gscl_step, gr_ready, gc_ready = (
            sem("gu_done"), sem("gate_ready"), sem("gu_ready"), sem("gmax_ready"), sem("gscl_step"), sem("gr_ready"), sem("gc_ready"))
        gt_done, gt_ready, d_done, out_ready = sem("gt_done"), sem("gt_ready"), sem("d_done"), sem("out_ready")
        stored = sem("stored_f")
        block = ph.enter_context(nc.Block())
        def run(eng, step, head):
            for h in range(NG):
                head(h)
                step(h, h % 4)
            head(NG)
            with eng.Fori(1, B // 4) as i:
                for j in range(4):
                    step(i * 4 + j, j)
            for h in range(B, B + 4):
                step(h, h % 4)

        @block.gpsimd
        def _(pool):
            pool.memset(magic[:, 0:1], MAGIC).then_inc(magic_ready, 1)
            pool.memset(magic[:, 1:2], -MAGIC).then_inc(magic_ready, 1)
            inputs.root(pool, NG - 1)

        @block.vector
        def _(dve):
            inputs.variance(dve, NG - 1)

            def clamp_x(g):
                a, b = g * G, (g + 1) * G
                dve.wait_ge(fma_ready, b)
                dve.tensor_scalar(xr[:, a:b, :], xr[:, a:b, :], MAGIC + 127.0, MAGIC - 128.0, ALU.min, ALU.max)\
                   .then_inc(clamp_ready, 1)

            def head(g):
                if g < NG:
                    clamp_x(g)
                if g == 0:
                    inputs.normalise(dve, NG - 1)
                if g == 1:
                    inputs.scales(dve, NG - 1)
                    dve.wait_ge(inputs.scale_step, NG * inputs.STEPS)

            def product(b, s):
                wait(dve, gate_ready, b + 1)
                wait(dve, gr_ready, b - 1)
                dve.scalar_tensor_tensor(out=gu[:, s, :], in0=ps_u[:, s, :], scalar=inputs.up_scl[:, bass.ds(b, 1)],
                                         in1=gate[:, s, :], op0=ALU.mult, op1=ALU.mult).then_inc(gu_ready, 1)

            def maximum(b, r):
                wait(dve, gu_ready, b + 1)
                dve.tensor_reduce(g_max[:, r:r + 1], gu[:, r % 2, :], AX_X, ALU.max, apply_absolute_value=True)\
                   .then_inc(gmax_ready, 1)

            def scales(b, r):
                wait(dve, gmax_ready, b + 1)
                dve.tensor_scalar(g_scl[:, r, 0:1], g_max[:, r:r + 1], 1e-5, 1.0 / 127.0, ALU.max, ALU.mult)\
                   .then_inc(gscl_step, 1)
                wait(dve, gscl_step, b * 3 + 1)
                dve.reciprocal(g_scl[:, r, 1:2], g_scl[:, r, 0:1]).then_inc(gscl_step, 1)
                dve.tensor_scalar(g_scl[:, r, 2:3], c["w_scale"][:, 2:3], g_scl[:, r, 0:1], None, ALU.mult)\
                   .then_inc(gscl_step, 1)

            def clamp_gu(b, s):
                wait(dve, gt_ready, b + 1)
                dve.tensor_scalar(gq_t[:, s, :], gq_t[:, s, :], 127.0, -128.0, ALU.min, ALU.max).then_inc(gc_ready, 1)

            def tail(b, r):
                wait(dve, d_done, b + 1)
                dve.scalar_tensor_tensor(out=batch_of(x_all, b), in0=ps_d[:, r % 2, 0:D], scalar=g_scl[:, r, 2:3],
                                         in1=batch_of(x_all, b), op0=ALU.mult, op1=ALU.add).then_inc(out_ready, 1)

            def step(h, r):
                if exists(h - 1):
                    product(h - 1, (r - 1) % 2)
                if exists(h - 3):
                    clamp_gu(h - 3, (r - 3) % 2)
                if exists(h - 1):
                    maximum(h - 1, (r - 1) % 4)
                if exists(h - 4):
                    tail(h - 4, r)
                if exists(h - 1):
                    scales(h - 1, (r - 1) % 4)

            run(dve, step, head)

        @block.scalar
        def _(act):
            act.wait_ge(magic_ready, 2)

            def round_x(g):
                act.wait_ge(inputs.scale_step, (g + 1) * inputs.STEPS)
                for n in range(g * G, (g + 1) * G):
                    act.activation(xr[:, n, :], inputs.xh[:, n, :], ACT.Identity, bias=magic[:, 0:1],
                                   scale=inputs.inv[:, n:n + 1])\
                       .then_inc(fma_ready, 1)

            def copy_x(g):
                act.wait_ge(xt_done, g + 1)
                act.activation(xq_t[:, g * G:(g + 1) * G, :].rearrange("p b s -> p (b s)"), ps_d[:, g % 2, :],
                               ACT.Identity, bias=magic[:, 1:2]).then_inc(xt_ready, 1)

            round_x(0)

            def head(g):
                if g + 1 < NG:
                    round_x(g + 1)
                if g < NG:
                    copy_x(g)

            def silu(b, s):
                wait(act, gu_done, b + 1)
                wait(act, gu_ready, b - 1)
                act.activation(gate[:, s, :], ps_g[:, s, :], ACT.Silu, scale=inputs.gate_scl[:, bass.ds(b, 1)])\
                   .then_inc(gate_ready, 1)

            def round_gu(b, r):
                wait(act, gscl_step, b * 3 + 3)
                wait(act, gt_done, b - 1)
                act.activation(gr[:, r % 2, :], gu[:, r % 2, :], ACT.Identity, bias=magic[:, 0:1], scale=g_scl[:, r, 1:2])\
                   .then_inc(gr_ready, 1)

            def copy_gu(b, s):
                wait(act, gt_done, b + 1)
                act.activation(gq_t[:, s, :], ps_t[:, s, :], ACT.Identity, bias=magic[:, 1:2]).then_inc(gt_ready, 1)

            def step(h, r):
                if exists(h - 3):
                    copy_gu(h - 3, (r - 3) % 2)
                if exists(h - 2):
                    round_gu(h - 2, (r - 2) % 4)
                if exists(h):
                    silu(h, r % 2)

            run(act, step, head)

        @block.tensor
        def _(pe):
            def head(g):
                if g == NG:
                    pe.wait_ge(xt_ready, NG)
                    return
                pe.wait_ge(clamp_ready, g + 1)
                wait(pe, xt_ready, g - 1)
                for j in range(G):
                    last = pe.transpose(ps_d[:, g % 2, j * P:(j + 1) * P], xr[:, g * G + j, :], ident[:])
                last.then_inc(xt_done, 1)
                if g == 0:
                    pe.wait_ge(xt_ready, 1)

            def gate_and_up(b, s):
                wait(pe, gu_ready, b - 1)
                x_b = xq_t[:, bass.ds(b, 1), :].rearrange("p b s -> p (b s)")
                pe.matmul(ps_g[:, s, :], x_b, c["ffn_wq"][:, 0, :], start=True, stop=True)
                pe.matmul(ps_u[:, s, :], x_b, c["ffn_wq"][:, 1, :], start=True, stop=True).then_inc(gu_done, 1)

            def turn(b, s):
                wait(pe, gr_ready, b + 1)
                wait(pe, gt_ready, b - 1)
                for k in range(FK):
                    last = pe.transpose(ps_t[:, s, k * P:(k + 1) * P], gr[:, s, k * P:(k + 1) * P], ident[:])
                last.then_inc(gt_done, 1)

            def down(b, s):
                wait(pe, gc_ready, b + 1)
                for k in range(FK):
                    last = pe.matmul(ps_d[:, s, 0:D], gq_t[:, s, k * P:(k + 1) * P], c["ffn_wq"][:, 2, k * D:(k + 1) * D],
                                     start=(k == 0), stop=(k == FK - 1))
                last.then_inc(d_done, 1)

            def step(h, r):
                if exists(h):
                    gate_and_up(h, r % 2)
                if exists(h - 4):
                    down(h - 4, r % 2)
                if exists(h - 2):
                    turn(h - 2, r % 2)

            run(pe, step, head)

        @block.sync
        def _(sp):
            with sp.Fori(0, B) as b:
                sp.wait_ge(out_ready, b + 1)
                sp.dma_start(t["out"][bass.ds(b, 1)].rearrange("b s d -> (b s) d"), batch_of(x_all, b))\
                  .then_inc(stored, 16)
            sp.wait_ge(stored, 16 * B)


def kernel(x, ctx_1024, mask_BxS2_if1, L0_xattn_Wq, L0_xattn_bq, L0_xattn_Wk, L0_xattn_bk, L0_xattn_Wv,
           L0_xattn_bv, L0_xattn_Wo, L0_xattn_bo, L0_ffn_norm_weight, L0_ffn_gate_w, L0_ffn_w1, L0_ffn_b1,
           L0_ffn_w2, L0_ffn_b2, L1_xattn_Wq, L1_xattn_Wk, L1_xattn_Wv, L1_xattn_Wo, L1_ffn_w_gate,
           L1_ffn_w_up, L1_ffn_w_down):
    import numpy as np
    import concourse.bacc as bacc
    from concourse import mybir as mb
    from concourse.bass_utils import run_bass_kernel_spmd

    def by_dim(w):
        return np.reshape(np.swapaxes(np.reshape(w, (*w.shape[:-1], H, DK)), -1, -2), w.shape)

    a = {
        "x": x,
        "ctx_t": np.transpose(ctx_1024, (2, 0, 1)).reshape(D, T),
        "mask": mask_BxS2_if1,
        "L0_Wq": by_dim(np.transpose(L0_xattn_Wq)), "L0_Wk": by_dim(np.transpose(L0_xattn_Wk)),
        "L0_Wv": np.transpose(L0_xattn_Wv), "L0_Wo": np.transpose(L0_xattn_Wo),
        "L1_Wq": by_dim(L1_xattn_Wq), "L1_Wk": by_dim(L1_xattn_Wk), "L1_Wv": L1_xattn_Wv, "L1_Wo": L1_xattn_Wo,
        "bq": np.reshape(by_dim(L0_xattn_bq), (D, 1)), "bk": np.reshape(by_dim(L0_xattn_bk), (D, 1)),
        "bv": np.reshape(L0_xattn_bv, (1, D)), "bo": np.reshape(L0_xattn_bo, (1, D)),
        "norm_w": np.reshape(L0_ffn_norm_weight, (D, 1)),
        "gate_w": np.transpose(L0_ffn_gate_w),
        "w1": np.transpose(L0_ffn_w1, (2, 0, 1)),
        "b1": np.transpose(np.reshape(L0_ffn_b1, (E * M, P))),
        "w2": np.transpose(np.reshape(L0_ffn_w2, (E, D, M, P)), (3, 0, 2, 1)),
        "b2": L0_ffn_b2,
        "w_gate": np.transpose(L1_ffn_w_gate), "w_up": np.transpose(L1_ffn_w_up),
        "w_down": np.transpose(np.reshape(L1_ffn_w_down, (D, FK, P)), (2, 1, 0)),
    }
    nc = bacc.Bacc("TRN2", target_bir_lowering=False, num_devices=1)
    arrays, t = {}, {}
    for name, value in a.items():
        value = np.ascontiguousarray(value)
        arrays[f"in_{name}"] = value
        t[name] = nc.dram_tensor(f"in_{name}", value.shape, mb.dt.from_np(value.dtype), kind="ExternalInput").ap()
    t["out"] = nc.dram_tensor("out", (B, P, D), mb.dt.float32, kind="ExternalOutput").ap()
    main_kernel(nc, t)
    return run_bass_kernel_spmd(nc, [arrays], core_ids=[0]).results[0]["out"]
```
